# Optimizing a Trainium2 kernel written in Bass

```python
import numpy as np
import jax
import jax.numpy as jnp

def _softmax(x, axis=-1):
    return jax.nn.softmax(x, axis=axis)

def _gelu(x):
    return jax.nn.gelu(x, approximate=True)

def _silu(x):
    return jax.nn.silu(x)

def _sigmoid(x):
    return jax.nn.sigmoid(x)

def _layernorm(x, axis=-1, eps=1e-05):
    m = jnp.mean(x, axis=axis, keepdims=True)
    v = jnp.var(x, axis=axis, keepdims=True)
    return (x - m) / jnp.sqrt(v + eps)

def _scatter_add(tgt, idx, src, axis=0):
    return tgt.at[idx].add(src)

def _segment_sum(src, seg, n):
    return jax.ops.segment_sum(src, seg, n)
kernel_name = 'mk_decoder_postln_d1_seqx_r8_0a999d'

def setup_inputs(seed: int=0):
    np.random.seed(seed)
    _w = jnp.asarray

    def _rec_inputs():
        import jax
        import jax.numpy as jnp
        _rk = jax.random.key(seed)
        x = 7.22e-05 + 1 * jax.random.normal(jax.random.fold_in(_rk, 1), (16, 128, 256), jnp.float32)
        _lenS = 128 - jax.random.randint(jax.random.fold_in(_rk, 7), (16,), 0, max(1, 128 // 4) + 1, jnp.int32)
        _lenS2 = 128 - jax.random.randint(jax.random.fold_in(_rk, 8), (16,), 0, max(1, 128 // 4) + 1, jnp.int32)
        _ctx_2048P = jax.random.normal(jax.random.fold_in(_rk, 11), (16, 16, 256), jnp.float32)
        _ctx_2048c = jax.random.dirichlet(jax.random.fold_in(_rk, 511), 0.3 * jnp.ones((16,), jnp.float32), (16, 128))
        _ctx_2048t = jnp.einsum('bsk,bkd->bsd', _ctx_2048c, _ctx_2048P)
        _ctx_2048t = _ctx_2048t * jax.lax.rsqrt(jnp.mean(jnp.square(_ctx_2048t)) + 1e-12) * 0.953939
        ctx_2048 = 4.13588e-05 + 0.999923 * (_ctx_2048t + 0.3 * jax.random.normal(jax.random.fold_in(_rk, 611), (16, 128, 256), jnp.float32))
        return (x, ctx_2048)
    x, ctx_2048 = _rec_inputs()

    def _L0_attn_setup():
        import jax, jax.numpy as jnp
        import numpy as np
        B, S, D = (2, 256, 256)
        H, DH, GROUPS = (16, 128, 4)
        KV = H // GROUPS
        G = GROUPS
        key = jax.random.key(seed)
        ks = jax.random.split(key, 5)
        sd = 1.0 / np.sqrt(D)
        return {'x': jax.random.normal(ks[0], (B, S, D), dtype=jnp.float32), 'Wq': jax.random.normal(ks[1], (D, H * DH), dtype=jnp.float32) * sd, 'bq': jnp.zeros((H * DH,), dtype=jnp.float32), 'Wk': jax.random.normal(ks[2], (D, KV * DH), dtype=jnp.float32) * sd, 'bk': jnp.zeros((KV * DH,), dtype=jnp.float32), 'Wv': jax.random.normal(ks[3], (D, KV * DH), dtype=jnp.float32) * sd, 'bv': jnp.zeros((KV * DH,), dtype=jnp.float32), 'Wo': jax.random.normal(ks[4], (H * DH, D), dtype=jnp.float32) * (1.0 / np.sqrt(H * DH)), 'bo': jnp.zeros((D,), dtype=jnp.float32)}
    _L0_attn_all = _L0_attn_setup()
    _L0_attn_in = {k: v for k, v in _L0_attn_all.items() if k in ('Wq', 'bq', 'Wk', 'bk', 'Wv', 'bv', 'Wo', 'bo')}
    del _L0_attn_all

    def _L0_xattn_setup():
        import jax, jax.numpy as jnp
        import numpy as np
        B, S, DIM, HD = (4, 128, 256, 128)
        H = DIM // HD
        GN_EPS = 0.001

        def _decay_masks(n_heads, seq_len):
            gam = 1.0 - 2.0 ** (-5.0 - jnp.arange(n_heads, dtype=jnp.float32))
            idx = jnp.arange(seq_len, dtype=jnp.float32)
            expo = idx[None, :] - idx[:, None]
            D = jnp.where(expo[None, :, :] <= 0, gam[:, None, None] ** expo[None, :, :], 0.0)
            return D / jnp.sqrt(D.sum(axis=-1))[:, None, :]
        key = jax.random.key(seed)
        ks = jax.random.split(key, 8)
        x = jax.random.normal(ks[0], (B, S, DIM), dtype=jnp.float32)
        k = jax.random.normal(ks[1], (B, S, DIM), dtype=jnp.float32)
        v = jax.random.normal(ks[2], (B, S, DIM), dtype=jnp.float32)
        Wh = jax.random.normal(ks[3], (H, HD, HD), dtype=jnp.float32) / np.sqrt(HD)
        wg_w = jax.random.normal(ks[4], (DIM, DIM), dtype=jnp.float32) / np.sqrt(DIM)
        wo_w = jax.random.normal(ks[5], (DIM, DIM), dtype=jnp.float32) / np.sqrt(DIM)
        gn_gamma = jnp.ones((DIM,), dtype=jnp.float32)
        gn_beta = jnp.zeros((DIM,), dtype=jnp.float32)
        return {'x': x, 'k': k, 'v': v, 'Wh': Wh, 'wg_w': wg_w, 'wo_w': wo_w, 'gn_gamma': gn_gamma, 'gn_beta': gn_beta}
    _L0_xattn_all = _L0_xattn_setup()
    _L0_xattn_in = {k: v for k, v in _L0_xattn_all.items() if k in ('Wh', 'wg_w', 'wo_w', 'gn_gamma', 'gn_beta')}
    del _L0_xattn_all

    def _L0_ffn_setup():
        import jax, jax.numpy as jnp
        import numpy as np
        B, S, H, I, E, F, K, R, TOPK = (1, 128, 256, 176, 64, 8, 8, 8, 6)
        ISH = 2 * I

        def _fused_linear(x, W, qa, qb, scale, w):
            out = x @ W.T
            a = jnp.einsum('th,krh->tkr', x, qa)
            b = jnp.einsum('tkr,khr->tkh', a, qb)
            mix = jnp.einsum('tkh,tk->th', b, w)
            return out + scale[None, :] * mix

        def _moe_forward(hidden_states, gate_weight, inv_mapping, mask_up_W, gate_W, gate_qa, gate_qb, gate_scale, up_W, up_qa, up_qb, up_scale, down_W, down_qa, down_qb, down_scale, sh_gate_W, sh_up_W, sh_down_W):
            b, s, h = hidden_states.shape
            x = hidden_states.reshape(-1, h)
            T = x.shape[0]
            scores = jax.nn.softmax(x @ gate_weight.T, axis=-1)
            topk_w, topk_idx = jax.lax.top_k(scores, TOPK)
            w_dense = jnp.zeros((T, E), x.dtype).at[jnp.arange(T)[:, None], topk_idx].add(topk_w)
            flat = w_dense[:, inv_mapping]
            scalar = flat.sum(-1)
            soft = jax.nn.softmax(jnp.where(flat == 0, -1000000000.0, flat), axis=-1)

            def expert(muW, gW, gqa, gqb, gs, uW, uqa, uqb, us, dW, dqa, dqb, ds, w):
                xe = x + w @ muW.T
                gate = jax.nn.silu(_fused_linear(xe, gW, gqa, gqb, gs, w))
                up = _fused_linear(xe, uW, uqa, uqb, us, w)
                return _fused_linear(gate * up, dW, dqa, dqb, ds, w)
            outs = jax.vmap(expert, in_axes=(0,) * 13 + (1,))(mask_up_W, gate_W, gate_qa, gate_qb, gate_scale, up_W, up_qa, up_qb, up_scale, down_W, down_qa, down_qb, down_scale, soft)
            y = jnp.einsum('fth,tf->th', outs, scalar).reshape(b, s, h)
            sh = jax.nn.silu(hidden_states @ sh_gate_W.T) * (hidden_states @ sh_up_W.T) @ sh_down_W.T
            return y + sh
        key = jax.random.key(seed)
        ks = jax.random.split(key, 20)
        g = lambda k, shape, s=0.02: jax.random.normal(k, shape, jnp.float32) * s
        return {'hidden_states': jax.random.normal(ks[0], (B, S, H), jnp.float32), 'gate_weight': g(ks[1], (E, H)), 'inv_mapping': jnp.arange(E, dtype=jnp.int32).reshape(F, K), 'mask_up_W': g(ks[2], (F, H, K)), 'gate_W': g(ks[3], (F, I, H)), 'gate_qa': g(ks[4], (F, K, R, H)), 'gate_qb': g(ks[5], (F, K, I, R)), 'gate_scale': jnp.full((F, I), 0.1, jnp.float32), 'up_W': g(ks[6], (F, I, H)), 'up_qa': g(ks[7], (F, K, R, H)), 'up_qb': g(ks[8], (F, K, I, R)), 'up_scale': jnp.full((F, I), 0.1, jnp.float32), 'down_W': g(ks[9], (F, H, I)), 'down_qa': g(ks[10], (F, K, R, I)), 'down_qb': g(ks[11], (F, K, H, R)), 'down_scale': jnp.full((F, H), 0.1, jnp.float32), 'sh_gate_W': g(ks[12], (ISH, H)), 'sh_up_W': g(ks[13], (ISH, H)), 'sh_down_W': g(ks[14], (H, ISH))}
    _L0_ffn_all = _L0_ffn_setup()
    _L0_ffn_in = {k: v for k, v in _L0_ffn_all.items() if k in ('gate_weight', 'inv_mapping', 'mask_up_W', 'gate_W', 'gate_qa', 'gate_qb', 'gate_scale', 'up_W', 'up_qa', 'up_qb', 'up_scale', 'down_W', 'down_qa', 'down_qb', 'down_scale', 'sh_gate_W', 'sh_up_W', 'sh_down_W')}
    del _L0_ffn_all
    return {'x': x, 'ctx_2048': ctx_2048, 'L0_attn_Wq': _L0_attn_in['Wq'], 'L0_attn_bq': _L0_attn_in['bq'], 'L0_attn_Wk': _L0_attn_in['Wk'], 'L0_attn_bk': _L0_attn_in['bk'], 'L0_attn_Wv': _L0_attn_in['Wv'], 'L0_attn_bv': _L0_attn_in['bv'], 'L0_attn_Wo': _L0_attn_in['Wo'], 'L0_attn_bo': _L0_attn_in['bo'], 'L0_xattn_Wh': _L0_xattn_in['Wh'], 'L0_xattn_wg_w': _L0_xattn_in['wg_w'], 'L0_xattn_wo_w': _L0_xattn_in['wo_w'], 'L0_xattn_gn_gamma': _L0_xattn_in['gn_gamma'], 'L0_xattn_gn_beta': _L0_xattn_in['gn_beta'], 'L0_ffn_gate_weight': _L0_ffn_in['gate_weight'], 'L0_ffn_inv_mapping': _L0_ffn_in['inv_mapping'], 'L0_ffn_mask_up_W': _L0_ffn_in['mask_up_W'], 'L0_ffn_gate_W': _L0_ffn_in['gate_W'], 'L0_ffn_gate_qa': _L0_ffn_in['gate_qa'], 'L0_ffn_gate_qb': _L0_ffn_in['gate_qb'], 'L0_ffn_gate_scale': _L0_ffn_in['gate_scale'], 'L0_ffn_up_W': _L0_ffn_in['up_W'], 'L0_ffn_up_qa': _L0_ffn_in['up_qa'], 'L0_ffn_up_qb': _L0_ffn_in['up_qb'], 'L0_ffn_up_scale': _L0_ffn_in['up_scale'], 'L0_ffn_down_W': _L0_ffn_in['down_W'], 'L0_ffn_down_qa': _L0_ffn_in['down_qa'], 'L0_ffn_down_qb': _L0_ffn_in['down_qb'], 'L0_ffn_down_scale': _L0_ffn_in['down_scale'], 'L0_ffn_sh_gate_W': _L0_ffn_in['sh_gate_W'], 'L0_ffn_sh_up_W': _L0_ffn_in['sh_up_W'], 'L0_ffn_sh_down_W': _L0_ffn_in['sh_down_W']}

def reference(x, ctx_2048, L0_attn_Wq, L0_attn_bq, L0_attn_Wk, L0_attn_bk, L0_attn_Wv, L0_attn_bv, L0_attn_Wo, L0_attn_bo, L0_xattn_Wh, L0_xattn_wg_w, L0_xattn_wo_w, L0_xattn_gn_gamma, L0_xattn_gn_beta, L0_ffn_gate_weight, L0_ffn_inv_mapping, L0_ffn_mask_up_W, L0_ffn_gate_W, L0_ffn_gate_qa, L0_ffn_gate_qb, L0_ffn_gate_scale, L0_ffn_up_W, L0_ffn_up_qa, L0_ffn_up_qb, L0_ffn_up_scale, L0_ffn_down_W, L0_ffn_down_qa, L0_ffn_down_qb, L0_ffn_down_scale, L0_ffn_sh_gate_W, L0_ffn_sh_up_W, L0_ffn_sh_down_W):
    import jax
    import jax.numpy as jnp

    def _L0_attn_ref(x, Wq, bq, Wk, bk, Wv, bv, Wo, bo):
        import jax, jax.numpy as jnp
        import numpy as np
        B, S, D = (2, 256, 256)
        H, DH, GROUPS = (16, 128, 4)
        KV = H // GROUPS
        G = GROUPS
        b, s, _ = x.shape
        Q = (x @ Wq + bq).reshape(b, s, KV, G, DH)
        K = (x @ Wk + bk).reshape(b, s, KV, DH)
        V = (x @ Wv + bv).reshape(b, s, KV, DH)
        scale = 1.0 / np.sqrt(DH).astype(np.float32)
        scores = jnp.einsum('bqkgd,bpkd->bkgqp', Q, K) * scale
        attn = jax.nn.softmax(scores, axis=-1)
        out = jnp.einsum('bkgqp,bpkd->bqkgd', attn, V)
        out = out.reshape(b, s, H * DH)
        return out @ Wo + bo

    def _L0_xattn_ref(x, k, v, Wh, wg_w, wo_w, gn_gamma, gn_beta):
        import jax, jax.numpy as jnp
        import numpy as np
        B, S, DIM, HD = (4, 128, 256, 128)
        H = DIM // HD
        GN_EPS = 0.001

        def _decay_masks(n_heads, seq_len):
            gam = 1.0 - 2.0 ** (-5.0 - jnp.arange(n_heads, dtype=jnp.float32))
            idx = jnp.arange(seq_len, dtype=jnp.float32)
            expo = idx[None, :] - idx[:, None]
            D = jnp.where(expo[None, :, :] <= 0, gam[:, None, None] ** expo[None, :, :], 0.0)
            return D / jnp.sqrt(D.sum(axis=-1))[:, None, :]
        b, s, dim = x.shape
        h, hd, _ = Wh.shape
        xh = x.reshape(b, s, h, hd)
        kh = k.reshape(b, s, h, hd)
        vh = v.reshape(b, s, h, hd)
        Q = jnp.einsum('bshd,hde->bshe', xh, Wh)
        K = jnp.einsum('bshd,hde->bshe', kh, Wh)
        V = jnp.einsum('bshd,hde->bshe', vh, Wh)
        scores = jnp.einsum('bshe,bthe->bhst', Q, K) / jnp.sqrt(jnp.float32(hd))
        Dn = _decay_masks(h, s)
        masked = scores * Dn[None, :, :, :]
        A = jnp.maximum(jnp.abs(masked.sum(axis=0)), 1.0)
        O = jnp.einsum('hst,bthe->bshe', A, V).reshape(b, s, dim)
        mu = O.mean(axis=-1, keepdims=True)
        var = O.var(axis=-1, keepdims=True)
        Y = (O - mu) / jnp.sqrt(var + GN_EPS) * gn_gamma + gn_beta
        W = jax.nn.relu(x @ wg_w)
        return W * Y @ wo_w

    def _L0_ffn_ref(hidden_states, gate_weight, inv_mapping, mask_up_W, gate_W, gate_qa, gate_qb, gate_scale, up_W, up_qa, up_qb, up_scale, down_W, down_qa, down_qb, down_scale, sh_gate_W, sh_up_W, sh_down_W):
        import jax, jax.numpy as jnp
        import numpy as np
        B, S, H, I, E, F, K, R, TOPK = (1, 128, 256, 176, 64, 8, 8, 8, 6)
        ISH = 2 * I

        def _fused_linear(x, W, qa, qb, scale, w):
            out = x @ W.T
            a = jnp.einsum('th,krh->tkr', x, qa)
            b = jnp.einsum('tkr,khr->tkh', a, qb)
            mix = jnp.einsum('tkh,tk->th', b, w)
            return out + scale[None, :] * mix

        def _moe_forward(hidden_states, gate_weight, inv_mapping, mask_up_W, gate_W, gate_qa, gate_qb, gate_scale, up_W, up_qa, up_qb, up_scale, down_W, down_qa, down_qb, down_scale, sh_gate_W, sh_up_W, sh_down_W):
            b, s, h = hidden_states.shape
            x = hidden_states.reshape(-1, h)
            T = x.shape[0]
            scores = jax.nn.softmax(x @ gate_weight.T, axis=-1)
            topk_w, topk_idx = jax.lax.top_k(scores, TOPK)
            w_dense = jnp.zeros((T, E), x.dtype).at[jnp.arange(T)[:, None], topk_idx].add(topk_w)
            flat = w_dense[:, inv_mapping]
            scalar = flat.sum(-1)
            soft = jax.nn.softmax(jnp.where(flat == 0, -1000000000.0, flat), axis=-1)

            def expert(muW, gW, gqa, gqb, gs, uW, uqa, uqb, us, dW, dqa, dqb, ds, w):
                xe = x + w @ muW.T
                gate = jax.nn.silu(_fused_linear(xe, gW, gqa, gqb, gs, w))
                up = _fused_linear(xe, uW, uqa, uqb, us, w)
                return _fused_linear(gate * up, dW, dqa, dqb, ds, w)
            outs = jax.vmap(expert, in_axes=(0,) * 13 + (1,))(mask_up_W, gate_W, gate_qa, gate_qb, gate_scale, up_W, up_qa, up_qb, up_scale, down_W, down_qa, down_qb, down_scale, soft)
            y = jnp.einsum('fth,tf->th', outs, scalar).reshape(b, s, h)
            sh = jax.nn.silu(hidden_states @ sh_gate_W.T) * (hidden_states @ sh_up_W.T) @ sh_down_W.T
            return y + sh
        return _moe_forward(hidden_states, gate_weight, inv_mapping, mask_up_W, gate_W, gate_qa, gate_qb, gate_scale, up_W, up_qa, up_qb, up_scale, down_W, down_qa, down_qb, down_scale, sh_gate_W, sh_up_W, sh_down_W)
    x = _layernorm(x + _L0_attn_ref(x, L0_attn_Wq, L0_attn_bq, L0_attn_Wk, L0_attn_bk, L0_attn_Wv, L0_attn_bv, L0_attn_Wo, L0_attn_bo), axis=-1)
    x = _layernorm(x + _L0_xattn_ref(x, ctx_2048, ctx_2048, L0_xattn_Wh, L0_xattn_wg_w, L0_xattn_wo_w, L0_xattn_gn_gamma, L0_xattn_gn_beta), axis=-1)
    x = _layernorm(x + _L0_ffn_ref(x, L0_ffn_gate_weight, L0_ffn_inv_mapping, L0_ffn_mask_up_W, L0_ffn_gate_W, L0_ffn_gate_qa, L0_ffn_gate_qb, L0_ffn_gate_scale, L0_ffn_up_W, L0_ffn_up_qa, L0_ffn_up_qb, L0_ffn_up_scale, L0_ffn_down_W, L0_ffn_down_qa, L0_ffn_down_qb, L0_ffn_down_scale, L0_ffn_sh_gate_W, L0_ffn_sh_up_W, L0_ffn_sh_down_W), axis=-1)
    return x

_drawn_inputs = setup_inputs


def setup_inputs(seed=0):
    import zlib

    import numpy as np

    out = dict(_drawn_inputs(seed))
    spreads = {'L0_attn_bq': (0.0, 0.56),
     'L0_attn_bk': (0.0, 0.8),
     'L0_attn_bv': (0.0, 0.1),
     'L0_attn_bo': (0.0, 0.1),
     'L0_xattn_gn_gamma': (1.0, 0.2),
     'L0_xattn_gn_beta': (0.0, 0.1),
     'L0_ffn_gate_scale': (0.10000000149011612, 0.6),
     'L0_ffn_up_scale': (0.10000000149011612, 0.6),
     'L0_ffn_down_scale': (0.10000000149011612, 0.6)}
    factors = {'L0_ffn_gate_weight': 8.0,
     'L0_ffn_mask_up_W': 8.0,
     'L0_ffn_gate_W': 8.0,
     'L0_ffn_gate_qa': 8.0,
     'L0_ffn_gate_qb': 8.0,
     'L0_ffn_up_W': 8.0,
     'L0_ffn_up_qa': 8.0,
     'L0_ffn_up_qb': 8.0,
     'L0_ffn_down_W': 8.0,
     'L0_ffn_down_qa': 8.0,
     'L0_ffn_down_qb': 8.0,
     'L0_ffn_sh_gate_W': 2.869,
     'L0_ffn_sh_up_W': 2.845,
     'L0_ffn_sh_down_W': 2.831}
    for name, (base, spread) in spreads.items():
        noise = np.random.default_rng([zlib.crc32(name.encode()), seed]).standard_normal(out[name].shape)
        drawn = base * np.exp(spread * noise) if base else spread * noise
        out[name] = jnp.asarray(drawn.astype(out[name].dtype))
    for name, factor in factors.items():
        out[name] = (out[name] * factor).astype(out[name].dtype)
    return out
```

```python
from contextlib import ExitStack

import concourse.bass as bass
from concourse import mybir
from concourse.alu_op_type import AluOpType as ALU

F32 = mybir.dt.float32
F32R = mybir.dt.float32r
ACT = mybir.ActivationFunctionType
AX = mybir.AxisListType

P = 128
B, S, D = 16, 128, 256
DK = D // P
H, KV, DH = 16, 4, 128
G = H // KV
PAIR = 2
TURNS = B // PAIR
TOK = PAIR * S
XH, HD = 2, 128
E, F, TOPK, I, R = 64, 8, 6, 176, 8
IH = I // 2
LN_EPS, GN_EPS = 1e-5, 1e-3


class Split:

    def __init__(self, hi, lo):
        self.hi, self.lo = hi, lo

    def __getitem__(self, at):
        return Split(self.hi[at], self.lo[at])

    def rearrange(self, *a, **k):
        return Split(self.hi.rearrange(*a, **k), self.lo.rearrange(*a, **k))


def product(pe, out, left, right, first=True, last=True, **more):
    pe.matmul(out, left.hi, right.hi, start=first, stop=False, **more)
    pe.matmul(out, left.hi, right.lo, start=False, stop=False, **more)
    return pe.matmul(out, left.lo, right.hi, start=False, stop=last, **more)


class Memory:

    def __init__(self, nc, stage):
        self.nc, self.stage, self.ctx = nc, stage, ExitStack()

    def sb(self, name, cols, dt=F32, parts=P):
        return self.ctx.enter_context(self.nc.sbuf_tensor(f"{self.stage}_{name}", [parts, cols], dt))

    def split(self, name, cols, parts=P):
        return Split(self.sb(name + "_hi", cols, F32R, parts), self.sb(name + "_lo", cols, F32R, parts))

    def bank(self, name):
        return self.ctx.enter_context(self.nc.psum_tensor(f"{self.stage}_{name}", [P, 512], F32))

    def sem(self, name):
        return self.ctx.enter_context(self.nc.semaphore(f"{self.stage}_{name}"))


def self_attention(nc, a, r1, stats1, ident):
    m = Memory(nc, "att")
    with m.ctx:
        CH = 1024
        stage = [m.sb(f"stage{n}", CH) for n in range(4)]
        Wq = m.split("Wq", KV * CH)
        Wk, Wv = m.split("Wk", CH), m.split("Wv", CH)
        Wo = m.split("Wo", KV * CH)
        bq, bk, bv = m.sb("bq", H), m.sb("bk", KV), m.sb("bv", KV)
        bo = m.sb("bo", PAIR * D)
        xT32 = m.sb("xT32", DK * TOK)
        xT = m.split("xT", DK * TOK)
        x_tok = m.sb("x_tok", PAIR * D)
        QT = [m.split(f"QT{n}", G * TOK) for n in range(2)]
        KT = m.split("KT", KV * TOK)
        V = m.split("V", PAIR * KV * DH)
        probs = [m.sb(f"probs{b}", G * S) for b in range(PAIR)]
        PT = [m.split(f"PT{b}", G * S) for b in range(PAIR)]
        OT = m.split("OT", G * TOK)
        top = [m.sb(f"top{b}", G) for b in range(PAIR)]
        bias = [m.sb(f"bias{b}", G) for b in range(PAIR)]
        mass = [m.sb(f"mass{b}", G) for b in range(PAIR)]
        share = [m.sb(f"share{b}", G) for b in range(PAIR)]
        stats, r_now = m.sb("stats", PAIR * 6), m.sb("r_now", PAIR * D)

        proj = [m.bank(f"proj{n}") for n in range(2)]
        score = [m.bank(f"score{b}") for b in range(PAIR)]
        mix = [m.bank(f"mix{b}") for b in range(PAIR)]
        acc = m.bank("acc")

        small_in = m.sem("small_in")
        w_in = [m.sem(f"w_in{n}") for n in range(4)]
        w_hi, w_lo = m.sem("w_hi"), m.sem("w_lo")
        pool_hi, pool_lo = m.sem("pool_hi"), m.sem("pool_lo")
        xT_in, xT_hi, xT_lo = m.sem("xT_in"), m.sem("xT_hi"), m.sem("xT_lo")
        x_in, xb_ready = m.sem("x_in"), m.sem("xb_ready")
        proj_ready, proj_hi, proj_lo = m.sem("proj_ready"), m.sem("proj_hi"), m.sem("proj_lo")
        score_ready, max_ready, bias_ready = m.sem("score_ready"), m.sem("max_ready"), m.sem("bias_ready")
        exp_ready, share_ready, prob_ready = m.sem("exp_ready"), m.sem("share_ready"), m.sem("prob_ready")
        pt_ready, pt_hi, pt_lo = m.sem("pt_ready"), m.sem("pt_hi"), m.sem("pt_lo")
        o_ready, o_hi, o_lo = m.sem("o_ready"), m.sem("o_hi"), m.sem("o_lo")
        acc_ready, r_ready, stats_ready, kept_ready = (
            m.sem("acc_ready"), m.sem("r_ready"), m.sem("stats_ready"), m.sem("kept_ready"))

        SCALE = float(DH) ** -0.5
        chunks = [(a["Wk"], Wk, "act"), (a["Wq"][:, 0:CH], Wq[:, 0:CH], "act"), (a["Wv"], Wv, "act")]
        for j in range(KV):
            c = slice(j * CH, (j + 1) * CH)
            if j:
                chunks.append((a["Wq"][:, c], Wq[:, c], "pool"))
            chunks.append((a["Wo"][:, c], Wo[:, c], "pool"))
        pool_chunks = [n for n, c in enumerate(chunks) if c[2] == "pool"]
        wq_at = {1: 2, 2: 4, 3: 6}
        wo_at = {0: 1, 1: 3, 2: 5, 3: 7}
        FIRST, PER = 6, 12

        def unit(g, n):
            return FIRST + PER * g + n

        def units_of(kind):
            if kind == "K":
                return [("K", 0), ("K", 1)]
            if kind == "V":
                return [("V", 0), ("V", 1)]
            return [("Q", kind, 0), ("Q", kind, 1)]

        def step_units(j, last):
            if j < KV - 1:
                return units_of(j + 1)
            return [] if last else units_of("K") + units_of(0)

        block = m.ctx.enter_context(nc.Block())

        @block.sync
        def _(sp):
            sp.dma_start(xT32[:, :].rearrange("p (k t) -> p k t", k=DK), a["xT"][:, :, 0:TOK]).then_inc(xT_in, 16)
            for n, (src, _dst, _who) in enumerate(chunks):
                if n == 1:
                    for dst, src_s in ((bq[:, :], a["bq"]), (bk[:, :], a["bk"]), (bv[:, :], a["bv"])):
                        sp.dma_start(dst, src_s).then_inc(small_in, 16)
                    sp.dma_start(bo[:, :].rearrange("p (b d) -> p b d", b=PAIR),
                                 a["bo"].rearrange("(o b d) -> o b d", o=1, b=1).to_broadcast([P, PAIR, D])
                                 ).then_inc(small_in, 16)
                    sp.dma_start(ident[:, :], a["ident"]).then_inc(small_in, 16)
                if n >= 4:
                    if chunks[n - 4][2] == "act":
                        sp.wait_ge(w_lo, n - 3)
                    else:
                        sp.wait_ge(pool_lo, pool_chunks.index(n - 4) + 1)
                sp.dma_start(stage[n % 4][:, :], src).then_inc(w_in[n % 4], 16)
            with sp.Fori(0, TURNS - 1) as g:
                sp.wait_ge(xT_lo, g + 1)
                sp.dma_start(xT32[:, :].rearrange("p (k t) -> p k t", k=DK),
                             a["xT"][:, :, bass.ds(g * TOK + TOK, TOK)]).then_inc(xT_in, 16)

        @block.gpsimd
        def _(pool):
            def load_x(g):
                pool.dma_start(x_tok[:, :], a["x_tok"][:, bass.ds(g * PAIR * D, PAIR * D)]).then_inc(x_in, 16)

            def split_x(g):
                pool.wait_ge(xT_hi, g + 1)
                pool.tensor_tensor(xT.lo[:, :], xT32[:, :], xT.hi[:, :].bitcast(F32), ALU.subtract).then_inc(xT_lo, 1)

            split_x(0)
            for n, at in enumerate(pool_chunks):
                dst = chunks[at][1]
                pool.wait_ge(w_in[at % 4], 16 * (at // 4 + 1))
                pool.tensor_copy(dst.hi, stage[at % 4][:, :]).then_inc(pool_hi, 1)
                pool.wait_ge(pool_hi, n + 1)
                pool.tensor_tensor(dst.lo, stage[at % 4][:, :], dst.hi.bitcast(F32), ALU.subtract).then_inc(pool_lo, 1)

            def turn(g, last):
                load_x(g)
                for j in range(KV):
                    if j == KV - 1 and not last:
                        split_x(g + 1)
                    for b in range(PAIR):
                        n = PAIR * j + b + 1
                        pool.wait_ge(share_ready, g * KV * PAIR + n)
                        p3 = probs[b][:, :].rearrange("p (h k) -> p h k", h=G)
                        pool.tensor_tensor(p3, p3, share[b][:, :].rearrange("p (h o) -> p h o", o=1).to_broadcast([P, G, S]),
                                           ALU.mult).then_inc(prob_ready, 1)
                    if j == 1:
                        pool.wait_ge(small_in, 80)
                        pool.wait_ge(x_in, g * 16 + 16)
                        pool.tensor_tensor(x_tok[:, :], x_tok[:, :], bo[:, :], ALU.add).then_inc(xb_ready, 1)
                pool.wait_ge(r_ready, g + 1)

            with pool.Fori(0, TURNS - 1) as g:
                turn(g, False)
            turn(TURNS - 1, True)

        @block.tensor
        def _(pe):
            def project(what, n):
                out = proj[(n + 1) % 2]
                if what[0] == "V":
                    b = what[1]
                    for k in range(DK):
                        mm = product(pe, out[:, :], xT[:, k * TOK + b * S:k * TOK + (b + 1) * S],
                                     Wv[:, k * 512:(k + 1) * 512], first=k == 0, last=k == DK - 1)
                else:
                    W = Wk[:, :] if what[0] == "K" else Wq[:, what[1] * CH:(what[1] + 1) * CH]
                    for h in range(2):
                        head = 2 * what[-1] + h
                        for k in range(DK):
                            mm = product(pe, out[:, h * TOK:(h + 1) * TOK],
                                         W[:, k * 512 + head * DH:k * 512 + (head + 1) * DH],
                                         xT[:, k * TOK:(k + 1) * TOK], first=k == 0, last=k == DK - 1)
                mm.then_inc(proj_ready, 1)

            pe.wait_ge(xT_lo, 1)
            pe.wait_ge(w_lo, 2)
            for n, what in enumerate(units_of("K") + units_of(0) + units_of("V"), 1):
                if what == ("V", 0):
                    pe.wait_ge(w_lo, 3)
                if n > 2:
                    pe.wait_ge(proj_lo, n - 2)
                project(what, n)
            pe.wait_ge(small_in, 80)

            def turn(g, last, weights):
                n = 0

                def projects(what):
                    nonlocal n
                    n += 1
                    pe.wait_ge(proj_lo, unit(g, n) - 2)
                    project(what, n)

                def out_project(j):
                    if weights:
                        pe.wait_ge(pool_lo, wo_at[j])
                    pe.wait_ge(o_lo, g * KV * PAIR + PAIR * (j + 1))
                    if j == 0:
                        if not weights:
                            pe.wait_ge(r_ready, g)
                    for b in range(PAIR):
                        for h in range(G):
                            mm = product(pe, acc[:, b * D:(b + 1) * D],
                                         OT[:, (h * PAIR + b) * S:(h * PAIR + b + 1) * S],
                                         Wo[:, j * CH + h * D:j * CH + (h + 1) * D],
                                         first=j == 0 and b == 0 and h == 0, last=j == KV - 1 and h == G - 1,
                                         skip_group_check=True)
                    if j == KV - 1:
                        mm.then_inc(acc_ready, 1)

                for j in range(KV):
                    pe.wait_ge(proj_lo, unit(g, 0) - 2 if j == 0 else unit(g, 2 * j))
                    for b in range(PAIR):
                        for h in range(G):
                            mm = product(pe, score[b][:, h * S:(h + 1) * S],
                                         QT[j % 2][:, h * TOK + b * S:h * TOK + (b + 1) * S],
                                         KT[:, j * TOK + b * S:j * TOK + (b + 1) * S])
                        mm.then_inc(score_ready, 1)
                    if j < KV - 1 and weights:
                        pe.wait_ge(pool_lo, wq_at[j + 1])
                    if j == KV - 1 and not last:
                        pe.wait_ge(xT_lo, g + 2)
                    for what in step_units(j, last):
                        projects(what)
                    for b in range(PAIR):
                        pe.wait_ge(prob_ready, g * KV * PAIR + PAIR * j + b + 1)
                        if j:
                            pe.wait_ge(o_lo, g * KV * PAIR + PAIR * (j - 1) + b + 1)
                        elif not weights:
                            pe.wait_ge(o_lo, g * KV * PAIR - PAIR + b + 1)
                        for h in range(G):
                            mm = pe.transpose(mix[b][:, h * S:(h + 1) * S], probs[b][:, h * S:(h + 1) * S], ident[:, :])
                        mm.then_inc(pt_ready, 1)
                    if j:
                        out_project(j - 1)
                    if j == 0:
                        pe.wait_ge(proj_lo, unit(g, 0))
                    for b in range(PAIR):
                        pe.wait_ge(pt_lo, g * KV * PAIR + PAIR * j + b + 1)
                        product(pe, mix[b][:, :], V[:, (b * KV + j) * DH:(b * KV + j + 1) * DH],
                                PT[b][:, :]).then_inc(o_ready, 1)
                    if j == KV - 1:
                        if not last:
                            for what in units_of("V"):
                                projects(what)
                        out_project(j)

            turn(0, False, True)
            with pe.Fori(1, TURNS - 1) as g:
                turn(g, False, False)
            turn(TURNS - 1, True, False)

        def copy_out(what):
            if what[0] == "V":
                b = what[1]
                return [(slice(0, 512), V[:, b * 512:(b + 1) * 512], None)]
            out = []
            for h in range(2):
                head = 2 * what[-1] + h
                where = slice(h * TOK, (h + 1) * TOK)
                if what[0] == "K":
                    out.append((where, KT[:, head * TOK:(head + 1) * TOK], bk[:, head:head + 1]))
                else:
                    q = what[1] * G + head
                    out.append((where, QT[what[1] % 2][:, head * TOK:(head + 1) * TOK], bq[:, q:q + 1]))
            return out

        @block.scalar
        def _(act):
            def high_x(g):
                act.wait_ge(xT_in, g * 16 + 16)
                act.activation(xT.hi[:, :], xT32[:, :], ACT.Copy).then_inc(xT_hi, 1)

            high_x(0)
            for n in range(3):
                act.wait_ge(w_in[n], 16)
                act.activation(chunks[n][1].hi if n == 1 else chunks[n][1].hi[:, :], stage[n][:, :], ACT.Copy).then_inc(w_hi, 1)
            act.wait_ge(small_in, 80)

            def high(what, g, n):
                act.wait_ge(proj_ready, unit(g, n))
                for where, dst, b in copy_out(what):
                    src = proj[(n + 1) % 2][:, where]
                    if b is None:
                        ins = act.activation(dst.hi, src, ACT.Copy)
                    else:
                        ins = act.activation(dst.hi, src, ACT.Identity, bias=b)
                ins.then_inc(proj_hi, 1)

            for n, what in enumerate(units_of("K") + units_of(0) + units_of("V"), 1):
                high(what, -1, n + PER - FIRST)

            def turn(g, last):
                n = 0
                for j in range(KV):
                    units = step_units(j, last)
                    for b in range(PAIR):
                        at = g * KV * PAIR + PAIR * j + b + 1
                        act.wait_ge(bias_ready, at)
                        for h in range(G):
                            c = slice(h * S, (h + 1) * S)
                            ins = act.activation(probs[b][:, c], score[b][:, c], ACT.Exp, bias=bias[b][:, h:h + 1],
                                                 scale=SCALE, accum_out=mass[b][:, h:h + 1])
                        ins.then_inc(exp_ready, 1)
                        for what in units[b::2] if len(units) == 2 else units[2 * b:2 * b + 2]:
                            n += 1
                            high(what, g, n)
                    if j == KV - 2 and not last:
                        high_x(g + 1)
                    for b in range(PAIR):
                        act.wait_ge(pt_ready, g * KV * PAIR + PAIR * j + b + 1)
                        act.activation(PT[b].hi[:, :], mix[b][:, :], ACT.Copy).then_inc(pt_hi, 1)
                    for b in range(PAIR):
                        act.wait_ge(o_ready, g * KV * PAIR + PAIR * j + b + 1)
                        act.activation(OT.hi[:, :].rearrange("p (h b q) -> p h b q", h=G, b=PAIR)[:, :, b, :],
                                       mix[b][:, :].rearrange("p (h q) -> p h q", h=G), ACT.Identity,
                                       bias=bv[:, j:j + 1]).then_inc(o_hi, 1)
                if not last:
                    for what in units_of("V"):
                        n += 1
                        high(what, g, n)

            with act.Fori(0, TURNS - 1) as g:
                turn(g, False)
            turn(TURNS - 1, True)

        @block.vector
        def _(dve):
            for n in range(3):
                dst = chunks[n][1]
                dve.wait_ge(w_hi, n + 1)
                dve.tensor_tensor(dst.lo[:, :], stage[n][:, :], dst.hi[:, :].bitcast(F32), ALU.subtract).then_inc(w_lo, 1)
            dve.wait_ge(small_in, 80)

            def low(what, g, n):
                dve.wait_ge(proj_hi, unit(g, n))
                for where, dst, b in copy_out(what):
                    src = proj[(n + 1) % 2][:, where]
                    if b is None:
                        ins = dve.tensor_tensor(dst.lo, src, dst.hi.bitcast(F32), ALU.subtract)
                    else:
                        ins = dve.scalar_tensor_tensor(dst.lo, src, b, dst.hi.bitcast(F32), ALU.add, ALU.subtract)
                ins.then_inc(proj_lo, 1)

            for n, what in enumerate(units_of("K") + units_of(0) + units_of("V"), 1):
                low(what, -1, n + PER - FIRST)

            def turn(g, last):
                n = 0
                for j in range(KV):
                    units = step_units(j, last)
                    for b in range(PAIR):
                        at = g * KV * PAIR + PAIR * j + b + 1
                        dve.wait_ge(score_ready, at)
                        dve.tensor_reduce(top[b][:, :], score[b][:, :].rearrange("p (h k) -> p h k", h=G), AX.X,
                                          ALU.max).then_inc(max_ready, 1)
                        dve.wait_ge(max_ready, at)
                        dve.tensor_scalar(bias[b][:, :], top[b][:, :], -SCALE, None, ALU.mult).then_inc(bias_ready, 1)
                    for b in range(PAIR):
                        at = g * KV * PAIR + PAIR * j + b + 1
                        dve.wait_ge(exp_ready, at)
                        dve.reciprocal(share[b][:, :], mass[b][:, :]).then_inc(share_ready, 1)
                        for what in units[b::2] if len(units) == 2 else units[2 * b:2 * b + 2]:
                            n += 1
                            low(what, g, n)
                    for b in range(PAIR):
                        dve.wait_ge(pt_hi, g * KV * PAIR + PAIR * j + b + 1)
                        dve.tensor_tensor(PT[b].lo[:, :], mix[b][:, :], PT[b].hi[:, :].bitcast(F32), ALU.subtract
                                          ).then_inc(pt_lo, 1)
                    for b in range(PAIR):
                        dve.wait_ge(o_hi, g * KV * PAIR + PAIR * j + b + 1)
                        o4 = lambda t: t[:, :].rearrange("p (h b q) -> p h b q", h=G, b=PAIR)[:, :, b, :]
                        dve.scalar_tensor_tensor(o4(OT.lo), mix[b][:, :].rearrange("p (h q) -> p h q", h=G), bv[:, j:j + 1],
                                                 o4(OT.hi).bitcast(F32), ALU.add, ALU.subtract).then_inc(o_lo, 1)
                if not last:
                    for what in units_of("V"):
                        n += 1
                        low(what, g, n)
                dve.wait_ge(acc_ready, g + 1)
                dve.wait_ge(xb_ready, g + 1)
                dve.tensor_tensor(r_now[:, :], acc[:, :], x_tok[:, :], ALU.add).then_inc(r_ready, 1)
                dve.wait_ge(r_ready, g + 1)
                for b in range(PAIR):
                    ins = dve.bn_stats(stats[:, 6 * b:6 * b + 6], r_now[:, b * D:(b + 1) * D])
                ins.then_inc(stats_ready, 1)
                dve.tensor_scalar(r1[:, bass.ds(g * PAIR * D, PAIR * D)], r_now[:, :], 1.0, None, ALU.mult
                                  ).then_inc(kept_ready, 1)
                dve.wait_ge(stats_ready, g + 1)
                dve.tensor_scalar(stats1[:, bass.ds(g * PAIR * 6, PAIR * 6)], stats[:, :], 1.0, None, ALU.mult
                                  ).then_inc(kept_ready, 1)
                dve.wait_ge(kept_ready, 2 * g + 2)

            with dve.Fori(0, TURNS - 1) as g:
                turn(g, False)
            turn(TURNS - 1, True)


def cross_attention(nc, a, r, stats, ident, xT):
    m = Memory(nc, "cross")
    CB = 4
    CT = CB * S
    CHUNKS = B // CB
    HH = XH * HD
    with m.ctx:
        small = m.sb("small", 2 * HH + 2 * DK * D)
        Ws = m.split("W", 2 * HH + 2 * DK * D)
        Wh, WhT = Ws[:, 0:HH], Ws[:, HH:2 * HH]
        wg, wo = Ws[:, 2 * HH:2 * HH + DK * D], Ws[:, 2 * HH + DK * D:]
        gram = m.split("gram", HH)
        gamma, beta = m.sb("gamma", D), m.sb("beta", D)
        decay = m.sb("decay", XH * S)
        ctx32 = m.sb("ctx32", XH * CT)
        ctxT = [m.split(f"ctxT{n}", XH * CT) for n in range(2)]
        KG = m.split("KG", XH * B * S)
        V = m.split("V", XH * B * HD)
        masked, positive = m.sb("masked", XH * S), m.sb("positive", XH * S)
        AT = m.split("AT", XH * S)
        Y = m.sb("Y", CB * D)
        WYT = [m.split(f"WYT{n}", 2 * D) for n in range(2)]
        WY = [small[:, n * 2 * D:(n + 1) * 2 * D] for n in range(2)]
        rstd = m.sb("rstd", B)
        std = m.sb("std", B)
        var = m.sb("var", B)
        ostats, omv = m.sb("ostats", CB * 12), m.sb("omv", CB * 2)
        ovar, ostd, orstd = m.sb("ovar", CB), m.sb("ostd", CB), m.sb("orstd", CB)
        mv = m.sb("mv", B * 2)
        bank = [m.bank(f"bank{n}") for n in range(8)]

        small_in, w_hi, w_lo = m.sem("small_in"), m.sem("w_hi"), m.sem("w_lo")
        const_in = m.sem("const_in")
        gram_ready, gram_hi, gram_lo = m.sem("gram_ready"), m.sem("gram_hi"), m.sem("gram_lo")
        ctx_in = m.sem("ctx_in")
        ctx_hi, ctx_lo = m.sem("ctx_hi"), m.sem("ctx_lo")
        kv_ready, kv_hi, kv_lo = m.sem("kv_ready"), m.sem("kv_hi"), m.sem("kv_lo")
        var_ready, std_ready, rstd_ready = m.sem("var_ready"), m.sem("std_ready"), m.sem("rstd_ready")
        x_ready, turned, turned_hi, turned_lo = m.sem("x_ready"), m.sem("turned"), m.sem("turned_hi"), m.sem("turned_lo")
        sum_ready, masked_ready, at32_ready, at_hi, at_lo = (
            m.sem("sum_ready"), m.sem("masked_ready"), m.sem("at32_ready"), m.sem("at_hi"), m.sem("at_lo"))
        o_ready, ostats_ready, omv_ready, ovar_ready, ostd_ready, orstd_ready, y_ready = (
            m.sem("o_ready"), m.sem("ostats_ready"), m.sem("omv_ready"), m.sem("ovar_ready"), m.sem("ostd_ready"),
            m.sem("orstd_ready"), m.sem("y_ready"))
        positive_ready = m.sem("positive_ready")
        scaled_ready, shifted_ready = m.sem("scaled_ready"), m.sem("shifted_ready")
        gate_ready, wy_ready, wyt_ready, wyt_hi, wyt_lo = (
            m.sem("gate_ready"), m.sem("wy_ready"), m.sem("wyt_ready"), m.sem("wyt_hi"), m.sem("wyt_lo"))
        out_ready, r_ready, stats_ready, mv_ready = (
            m.sem("out_ready"), m.sem("r_ready"), m.sem("stats_ready"), m.sem("mv_ready"))

        mean = lambda t: mv[:, 2 * t:2 * t + 1]
        tile = lambda t: r[:, t * D:(t + 1) * D]
        xT3 = lambda part: part[:, :].rearrange("p (k t) -> p k t", k=DK)

        block = m.ctx.enter_context(nc.Block())

        @block.sync
        def _(sp):
            sp.dma_start(small[:, :], a["cross_w"]).then_inc(small_in, 16)
            for c in range(CHUNKS):
                if c:
                    sp.wait_ge(ctx_lo, c)
                sp.dma_start(ctx32[:, :].rearrange("p (h t) -> p h t", h=XH),
                             a["ctxT"][:, :, c * CT:(c + 1) * CT]).then_inc(ctx_in, 16)
                if c == 1:
                    sp.dma_start(decay[:, :], a["decay"]).then_inc(const_in, 16)
                    for dst, src in ((gamma, a["gamma"]), (beta, a["beta"])):
                        sp.dma_start(dst[:, :], src.rearrange("(o d) -> o d", o=1).to_broadcast([P, D])
                                     ).then_inc(const_in, 16)

        @block.gpsimd
        def _(pool):
            def normalise(t, at):
                pool.tensor_scalar(tile(t), tile(t), mean(t), rstd[:, t:t + 1], ALU.subtract, ALU.mult
                                   ).then_inc(x_ready, 1)

            for c in range(CHUNKS):
                pool.wait_ge(ctx_in, 16 * (c + 1))
                if c >= 2:
                    pool.wait_ge(kv_ready, 4 * (c - 1))
                pool.tensor_copy(ctxT[c % 2].hi[:, :], ctx32[:, :]).then_inc(ctx_hi, 1)
                pool.wait_ge(ctx_hi, c + 1)
                pool.tensor_tensor(ctxT[c % 2].lo[:, :], ctx32[:, :], ctxT[c % 2].hi[:, :].bitcast(F32),
                                   ALU.subtract).then_inc(ctx_lo, 1)
                if c == 0:
                    pool.wait_ge(rstd_ready, 1)
                for t in range(c * CB, (c + 1) * CB):
                    normalise(t, 0)
            pool.wait_ge(const_in, 48)
            for c in range(CHUNKS):
                Y3 = Y[:, :].rearrange("p (b d) -> p b d", b=CB)
                pool.wait_ge(y_ready, c + 1)
                pool.tensor_tensor(Y3, Y3, gamma[:, :].rearrange("p (o d) -> p o d", o=1).to_broadcast([P, CB, D]),
                                   ALU.mult).then_inc(scaled_ready, 1)
                pool.wait_ge(scaled_ready, c + 1)
                pool.tensor_tensor(Y3, Y3, beta[:, :].rearrange("p (o d) -> p o d", o=1).to_broadcast([P, CB, D]),
                                   ALU.add).then_inc(shifted_ready, 1)
            pool.wait_ge(rstd_ready, 2)
            for t in range(B):
                normalise(t, 1)

        @block.tensor
        def _(pe):
            def turn_tiles(u, at, banks, first_free):
                pe.wait_ge(x_ready, at * B + 2 * u + 2)
                if u >= 2:
                    pe.wait_ge(turned_lo, at * (B // 2) + u - 1)
                for k in range(DK):
                    for i in range(2):
                        t = 2 * u + i
                        mm = pe.transpose(bank[banks[u % 2]][:, (k * 2 + i) * P:(k * 2 + i + 1) * P],
                                          r[:, t * D + k * P:t * D + (k + 1) * P], ident[:, :])
                mm.then_inc(turned, 1)

            pe.wait_ge(w_lo, 1)
            for h in range(XH):
                mm = product(pe, bank[4][:, h * HD:(h + 1) * HD], WhT[:, h * HD:(h + 1) * HD], WhT[:, h * HD:(h + 1) * HD])
            mm.then_inc(gram_ready, 1)
            pe.wait_ge(gram_lo, 1)
            for c in range(CHUNKS):
                pe.wait_ge(ctx_lo, c + 1)
                for h in range(XH):
                    n = 4 * c + 2 * h
                    if n >= 4:
                        pe.wait_ge(kv_lo, n - 3)
                    product(pe, bank[n % 4][:, :], gram[:, h * HD:(h + 1) * HD], ctxT[c % 2][:, h * CT:(h + 1) * CT]
                            ).then_inc(kv_ready, 1)
                    if n >= 4:
                        pe.wait_ge(kv_lo, n - 2)
                    for b in range(CB):
                        mm = product(pe, bank[(n + 1) % 4][:, b * HD:(b + 1) * HD],
                                     ctxT[c % 2][:, h * CT + b * S:h * CT + (b + 1) * S], Wh[:, h * HD:(h + 1) * HD])
                    mm.then_inc(kv_ready, 1)

            def sum_scores(u):
                pe.wait_ge(turned_lo, u + 1)
                if u == 0:
                    pe.wait_ge(kv_lo, 4 * CHUNKS)
                for b in (2 * u, 2 * u + 1):
                    for h in range(XH):
                        at = slice(h * B * S + b * S, h * B * S + (b + 1) * S)
                        mm = product(pe, bank[6 + h][:, 0:S], KG[:, at], xT[:, at], first=b == 0, last=b == B - 1)
                if u == B // 2 - 1:
                    mm.then_inc(sum_ready, 1)

            for u in range(B // 2):
                turn_tiles(u, 0, (4, 5), None)
                if u:
                    sum_scores(u - 1)
            sum_scores(B // 2 - 1)

            def mix_values(c):
                if c:
                    pe.wait_ge(y_ready, c)
                for h in range(XH):
                    mm = product(pe, bank[h][:, :], AT[:, h * S:(h + 1) * S],
                                 V[:, (h * B + c * CB) * HD:(h * B + (c + 1) * CB) * HD])
                mm.then_inc(o_ready, 1)

            def gates(c):
                for i in range(2):
                    if c:
                        pe.wait_ge(wy_ready, 2 * (c - 1) + i + 1)
                    for j in range(2):
                        b = c * CB + 2 * i + j
                        for k in range(DK):
                            mm = product(pe, bank[2 + i][:, j * D:(j + 1) * D], xT[:, (k * B + b) * S:(k * B + b + 1) * S],
                                         wg[:, k * D:(k + 1) * D], first=k == 0, last=k == DK - 1)
                    mm.then_inc(gate_ready, 1)

            gates(0)
            pe.wait_ge(at_lo, 1)
            mix_values(0)
            for c in range(CHUNKS):
                if c < CHUNKS - 1:
                    mix_values(c + 1)
                for i in range(2):
                    pe.wait_ge(wy_ready, 2 * c + i + 1)
                    for j in range(4):
                        mm = pe.transpose(bank[4 + i][:, j * P:(j + 1) * P], WY[i][:, j * P:(j + 1) * P], ident[:, :])
                    mm.then_inc(wyt_ready, 1)
                if c < CHUNKS - 1:
                    gates(c + 1)
                for i in range(2):
                    pe.wait_ge(wyt_lo, 2 * c + i + 1)
                    if c:
                        pe.wait_ge(r_ready, 2 * (c - 1) + i + 1)
                    else:
                        pe.wait_ge(masked_ready, 1)
                    for j in range(2):
                        for k in range(DK):
                            mm = product(pe, bank[6 + i][:, j * D:(j + 1) * D], WYT[i][:, (2 * j + k) * P:(2 * j + k + 1) * P],
                                         wo[:, k * D:(k + 1) * D], first=k == 0, last=k == DK - 1)
                    mm.then_inc(out_ready, 1)
            for u in range(B // 2):
                turn_tiles(u, 1, (0, 1), None)

        def split_turned(eng, u, at, banks):
            n = at * (B // 2) + u + 1
            src = bank[banks[u % 2]][:, :].rearrange("p (k t) -> p k t", k=DK)
            to = lambda part: xT3(part)[:, :, 2 * u * P:(2 * u + 2) * P]
            if eng == "act":
                nc.scalar.wait_ge(turned, n)
                nc.scalar.activation(to(xT.hi), src, ACT.Copy).then_inc(turned_hi, 1)
            else:
                nc.vector.wait_ge(turned_hi, n)
                nc.vector.tensor_tensor(to(xT.lo), src, to(xT.hi).bitcast(F32), ALU.subtract).then_inc(turned_lo, 1)

        def kv_to(n):
            c, h = n // 4, n // 2 % 2
            if n % 2 == 0:
                return KG[:, h * B * S + c * CT:h * B * S + (c + 1) * CT]
            return V[:, (h * B + c * CB) * HD:(h * B + (c + 1) * CB) * HD]

        @block.scalar
        def _(act):
            act.wait_ge(var_ready, 1)
            act.activation(std[:, :], var[:, :], ACT.Sqrt).then_inc(std_ready, 1)
            act.wait_ge(small_in, 16)
            act.activation(Ws.hi[:, :], small[:, :], ACT.Copy).then_inc(w_hi, 1)
            act.wait_ge(gram_ready, 1)
            act.activation(gram.hi[:, :], bank[4][:, 0:HH], ACT.Copy).then_inc(gram_hi, 1)
            for n in range(4 * CHUNKS):
                act.wait_ge(kv_ready, n + 1)
                act.activation(kv_to(n).hi, bank[n % 4][:, :], ACT.Copy).then_inc(kv_hi, 1)
            for u in range(B // 2):
                split_turned("act", u, 0, (4, 5))
            act.wait_ge(at32_ready, 1)
            act.activation(AT.hi[:, :], masked[:, :], ACT.Copy).then_inc(at_hi, 1)
            for c in range(CHUNKS):
                act.wait_ge(ovar_ready, c + 1)
                act.activation(ostd[:, :], ovar[:, :], ACT.Sqrt).then_inc(ostd_ready, 1)
                for i in range(2):
                    act.wait_ge(wyt_ready, 2 * c + i + 1)
                    act.activation(WYT[i].hi[:, :], bank[4 + i][:, :], ACT.Copy).then_inc(wyt_hi, 1)
            act.wait_ge(var_ready, 2)
            act.activation(std[:, :], var[:, :], ACT.Sqrt).then_inc(std_ready, 1)
            for u in range(B // 2):
                split_turned("act", u, 1, (0, 1))

        @block.vector
        def _(dve):
            def norm_factors(at):
                for t in range(B):
                    ins = dve.bn_aggr(mv[:, 2 * t:2 * t + 2], stats[:, 6 * t:6 * t + 6])
                ins.then_inc(mv_ready, 1)
                dve.wait_ge(mv_ready, at + 1)
                dve.tensor_scalar(var[:, :], mv[:, :].rearrange("p (t s) -> p t s", s=2)[:, :, 1], LN_EPS, None,
                                  ALU.add).then_inc(var_ready, 1)
                dve.wait_ge(std_ready, at + 1)
                dve.reciprocal(rstd[:, :], std[:, :]).then_inc(rstd_ready, 1)

            norm_factors(0)
            dve.wait_ge(w_hi, 1)
            dve.tensor_tensor(Ws.lo[:, :], small[:, :], Ws.hi[:, :].bitcast(F32), ALU.subtract).then_inc(w_lo, 1)
            dve.wait_ge(gram_hi, 1)
            dve.tensor_tensor(gram.lo[:, :], bank[4][:, 0:HH], gram.hi[:, :].bitcast(F32), ALU.subtract).then_inc(gram_lo, 1)
            for n in range(4 * CHUNKS):
                dve.wait_ge(kv_hi, n + 1)
                dve.tensor_tensor(kv_to(n).lo, bank[n % 4][:, :], kv_to(n).hi.bitcast(F32), ALU.subtract).then_inc(kv_lo, 1)
            for u in range(B // 2):
                split_turned("dve", u, 0, (4, 5))
            dve.wait_ge(sum_ready, 1)
            dve.wait_ge(const_in, 48)
            for h in range(XH):
                c = slice(h * S, (h + 1) * S)
                ins = dve.scalar_tensor_tensor(masked[:, c], bank[6 + h][:, 0:S], float(HD) ** -0.5, decay[:, c],
                                               ALU.mult, ALU.mult)
            ins.then_inc(masked_ready, 1)
            dve.wait_ge(masked_ready, 1)
            dve.scalar_tensor_tensor(positive[:, :], masked[:, :], -1.0, masked[:, :], ALU.mult, ALU.max
                                     ).then_inc(positive_ready, 1)
            dve.wait_ge(positive_ready, 1)
            dve.tensor_scalar(masked[:, :], positive[:, :], 1.0, None, ALU.max).then_inc(at32_ready, 1)
            dve.wait_ge(at_hi, 1)
            dve.tensor_tensor(AT.lo[:, :], masked[:, :], AT.hi[:, :].bitcast(F32), ALU.subtract).then_inc(at_lo, 1)

            def normalise_mix(c):
                dve.wait_ge(o_ready, c + 1)
                if c:
                    dve.wait_ge(wy_ready, 2 * c)
                for b in range(CB):
                    for h in range(XH):
                        ins = dve.bn_stats(ostats[:, b * 12 + h * 6:b * 12 + h * 6 + 6], bank[h][:, b * HD:(b + 1) * HD])
                ins.then_inc(ostats_ready, 1)
                dve.wait_ge(ostats_ready, c + 1)
                for b in range(CB):
                    ins = dve.bn_aggr(omv[:, 2 * b:2 * b + 2], ostats[:, 12 * b:12 * b + 12])
                ins.then_inc(omv_ready, 1)
                dve.wait_ge(omv_ready, c + 1)
                dve.tensor_scalar(ovar[:, :], omv[:, :].rearrange("p (t s) -> p t s", s=2)[:, :, 1], GN_EPS, None,
                                  ALU.add).then_inc(ovar_ready, 1)
                dve.wait_ge(ostd_ready, c + 1)
                dve.reciprocal(orstd[:, :], ostd[:, :]).then_inc(orstd_ready, 1)
                dve.wait_ge(orstd_ready, c + 1)
                for b in range(CB):
                    for h in range(XH):
                        ins = dve.tensor_scalar(Y[:, b * D + h * HD:b * D + (h + 1) * HD], bank[h][:, b * HD:(b + 1) * HD],
                                                omv[:, 2 * b:2 * b + 1], orstd[:, b:b + 1], ALU.subtract, ALU.mult)
                ins.then_inc(y_ready, 1)

            def gate_mix(c):
                dve.wait_ge(shifted_ready, c + 1)
                for i in range(2):
                    dve.wait_ge(gate_ready, 2 * c + i + 1)
                    if c:
                        dve.wait_ge(wyt_ready, 2 * (c - 1) + i + 1)
                    dve.scalar_tensor_tensor(WY[i][:, :], bank[2 + i][:, :], 0.0, Y[:, i * 2 * D:(i + 1) * 2 * D],
                                             ALU.max, ALU.mult).then_inc(wy_ready, 1)

            for c in range(CHUNKS):
                normalise_mix(c)
                gate_mix(c)
                for i in range(2):
                    dve.wait_ge(wyt_hi, 2 * c + i + 1)
                    dve.tensor_tensor(WYT[i].lo[:, :], bank[4 + i][:, :], WYT[i].hi[:, :].bitcast(F32), ALU.subtract
                                      ).then_inc(wyt_lo, 1)
                for i in range(2):
                    t = c * CB + 2 * i
                    two = r[:, t * D:(t + 2) * D]
                    dve.wait_ge(out_ready, 2 * c + i + 1)
                    dve.tensor_tensor(two, bank[6 + i][:, :], two, ALU.add).then_inc(r_ready, 1)
                    dve.wait_ge(r_ready, 2 * c + i + 1)
                    for j in range(2):
                        ins = dve.bn_stats(stats[:, 6 * (t + j):6 * (t + j) + 6], tile(t + j))
                    ins.then_inc(stats_ready, 1)
            dve.wait_ge(stats_ready, 2 * CHUNKS)
            norm_factors(1)
            for u in range(B // 2):
                split_turned("dve", u, 1, (0, 1))


FK = E
CT = 512
CHUNKS = B * S // CT
TT = CT // P
SI = 3


def route_and_share(nc, a, r, ident, xT, xT32, softT, share_of, soft_dram):
    m = Memory(nc, "route")
    with m.ctx:
        NW = DK * E + 2 * DK * SI * P + SI * D
        w32 = m.sb("w32", NW)
        W = m.split("W", NW)
        Wr = W[:, 0:DK * E]
        at = DK * E
        Wg, Wu = W[:, at:at + DK * SI * P], W[:, at + DK * SI * P:at + 2 * DK * SI * P]
        Wd = W[:, at + 2 * DK * SI * P:]
        inv_raw = m.sb("inv_raw", FK, mybir.dt.int32, E)
        inv = m.sb("inv", FK, F32, E)
        rows = m.sb("rows", 1, F32, E)
        onehot = m.sb("onehot", FK, F32, E)
        EX = E + 2
        top1, mass, part = m.sb("top1", TT), m.sb("mass", TT), m.sb("part", TT)
        e1, soft1 = m.sb("e1", TT * E), m.sb("soft1", TT * EX)
        top8, rest = m.sb("top8", TT * 8), m.sb("rest", TT * EX)
        kept = m.sb("kept", TT * E)
        keptT = m.sb("keptT", CT, F32, E)
        unused, e2 = m.sb("unused", TT * FK), m.sb("e2", TT * FK)
        top2, mass2, part2 = m.sb("top2", TT * F), m.sb("mass2", TT * F), m.sb("part2", TT * F)
        softT32 = m.sb("softT32", CT, F32, FK)
        silu = [m.sb(f"silu{n}", CT) for n in range(2)]
        inner = [m.sb(f"inner{n}", CT) for n in range(2)]
        innerT = [[m.split(f"inner{n}_{k}", CT) for k in range(SI)] for n in range(2)]

        gate_bank = [m.bank(f"gate{n}") for n in range(2)]
        up_bank = [m.bank(f"up{n}") for n in range(2)]
        y_bank = [m.bank(f"y{n}") for n in range(2)]
        token_bank, turned_bank = m.bank("token"), m.bank("turned")

        w_in, small_in, w_hi, w_lo = m.sem("w_in"), m.sem("small_in"), m.sem("w_hi"), m.sem("w_lo")
        inv_ready, onehot_ready, sentinels = m.sem("inv_ready"), m.sem("onehot_ready"), m.sem("sentinels")
        logit_ready, top1_ready, less1_ready, exp1_ready = (
            m.sem("logit_ready"), m.sem("top1_ready"), m.sem("less1_ready"), m.sem("exp1_ready"))
        mass1_ready, part1_ready, soft1_ready, top8_ready, rest_ready, kept_ready = (
            m.sem("mass1_ready"), m.sem("part1_ready"), m.sem("soft1_ready"), m.sem("top8_ready"),
            m.sem("rest_ready"), m.sem("kept_ready"))
        kept_turned, keptT_ready, flat_ready = m.sem("kept_turned"), m.sem("keptT_ready"), m.sem("flat_ready")
        unused_ready, masked_ready, top2_ready, less2_ready, exp2_ready, mass2_ready, part2_ready, soft2_ready = (
            m.sem("unused_ready"), m.sem("masked_ready"), m.sem("top2_ready"), m.sem("less2_ready"),
            m.sem("exp2_ready"), m.sem("mass2_ready"), m.sem("part2_ready"), m.sem("soft2_ready"))
        soft_turned, softT_hi, softT32_ready, softT_lo, stored = (
            m.sem("soft_turned"), m.sem("softT_hi"), m.sem("softT32_ready"), m.sem("softT_lo"), m.sem("stored"))
        up_ready, silu_ready, inner_ready, inner_hi, inner_lo = (
            m.sem("up_ready"), m.sem("silu_ready"), m.sem("inner_ready"), m.sem("inner_hi"), m.sem("inner_lo"))
        y_ready, r_ready, x32_ready = m.sem("y_ready"), m.sem("r_ready"), m.sem("x32_ready")

        t3 = lambda t, w=E: t[:, :].rearrange("p (t e) -> p t e", t=TT, e=w) if t.shape[1] == TT * w else None
        wide = lambda t, n, w: t[:, :].rearrange("p (t o) -> p t o", o=1).to_broadcast([P, n, w])
        tok3 = token_bank[:, 0:TT * E].rearrange("p (t e) -> p t e", t=TT)
        tok8 = token_bank[:, 0:TT * FK].rearrange("p (t k) -> p t k", k=F)
        e2_8 = e2[:, :].rearrange("p (t k) -> p t k", k=F)
        s3 = soft1[:, :].rearrange("p (t e) -> p t e", t=TT)
        rest3 = rest[:, :].rearrange("p (t e) -> p t e", t=TT)

        block = m.ctx.enter_context(nc.Block())

        @block.sync
        def _(sp):
            sp.dma_start(w32[:, :], a["route_w"]).then_inc(w_in, 16)
            sp.dma_start(inv_raw[:, :], a["inv"].rearrange("(o e) -> o e", o=1).to_broadcast([E, FK])).then_inc(small_in, 16)
            sp.dma_start(rows[:, :], a["rows"]).then_inc(small_in, 16)
            for c in range(CHUNKS):
                sp.wait_ge(softT32_ready, c + 1)
                sp.dma_start(soft_dram[:, c * CT:(c + 1) * CT], softT32[:, :]).then_inc(stored, 16)
            sp.wait_ge(stored, 16 * CHUNKS)

        @block.gpsimd
        def _(pool):
            for n in range(2 * CHUNKS):
                c = slice(n * CT, (n + 1) * CT)
                pool.tensor_tensor(xT32[:, c], xT.hi[:, c].bitcast(F32), xT.lo[:, c].bitcast(F32), ALU.add
                                   ).then_inc(x32_ready, 1)
                if n % 2 == 1:
                    for k in range(SI):
                        u = n // 2 * SI + k
                        pool.wait_ge(inner_hi, u + 1)
                        pool.tensor_tensor(innerT[n // 2 % 2][k].lo[:, :], inner[u % 2][:, :],
                                           innerT[n // 2 % 2][k].hi[:, :].bitcast(F32), ALU.subtract).then_inc(inner_lo, 1)

        @block.tensor
        def _(pe):
            def shared_in(c, k):
                u = c * SI + k
                if u >= 2:
                    pe.wait_ge(inner_ready, u - 1)
                for W_, bank in ((Wg, gate_bank), (Wu, up_bank)):
                    for d in range(DK):
                        mm = product(pe, bank[u % 2][:, :], W_[:, (d * SI + k) * P:(d * SI + k + 1) * P],
                                     xT[:, d * B * S + c * CT:d * B * S + (c + 1) * CT], first=d == 0, last=d == DK - 1)
                mm.then_inc(up_ready, 1)

            def shared_out(c):
                pe.wait_ge(inner_lo, SI * (c + 1))
                for i in range(2):
                    if c:
                        pe.wait_ge(r_ready, 2 * (c - 1) + i + 1)
                    for j in range(2):
                        t = 2 * i + j
                        for k in range(SI):
                            mm = product(pe, y_bank[i][:, j * D:(j + 1) * D], innerT[c % 2][k][:, t * P:(t + 1) * P],
                                         Wd[:, k * D:(k + 1) * D], first=k == 0, last=k == SI - 1)
                    mm.then_inc(y_ready, 1)

            pe.wait_ge(w_lo, 1)
            for c in range(CHUNKS):
                if c:
                    pe.wait_ge(masked_ready, c)
                for t in range(TT):
                    for d in range(DK):
                        at = d * B * S + c * CT + t * P
                        mm = product(pe, token_bank[:, t * E:(t + 1) * E], xT[:, at:at + P], Wr[:, d * E:(d + 1) * E],
                                     first=d == 0, last=d == DK - 1)
                mm.then_inc(logit_ready, 1)
                shared_in(c, 0)
                shared_in(c, 1)
                pe.wait_ge(kept_ready, c + 1)
                if c:
                    pe.wait_ge(softT_lo, c)
                for t in range(TT):
                    mm = pe.transpose(turned_bank[0:E, t * P:(t + 1) * P], kept[:, t * E:(t + 1) * E], ident[:, :])
                mm.then_inc(kept_turned, 1)
                shared_in(c, 2)
                pe.wait_ge(keptT_ready, c + 1)
                pe.wait_ge(onehot_ready, 1)
                for t in range(TT):
                    mm = pe.matmul(token_bank[:, t * FK:(t + 1) * FK], keptT[:, t * P:(t + 1) * P], onehot[:, :],
                                   start=True, stop=True)
                mm.then_inc(flat_ready, 1)
                if c:
                    shared_out(c - 1)
                pe.wait_ge(soft2_ready, c + 1)
                for t in range(TT):
                    mm = pe.transpose(turned_bank[0:FK, t * P:(t + 1) * P], e2[:, t * FK:(t + 1) * FK], ident[:, :])
                mm.then_inc(soft_turned, 1)
            shared_out(CHUNKS - 1)

        @block.scalar
        def _(act):
            act.wait_ge(w_in, 16)
            act.activation(W.hi[:, :], w32[:, :], ACT.Copy).then_inc(w_hi, 1)

            def shared(c, k):
                u = c * SI + k
                act.wait_ge(up_ready, u + 1)
                if u >= 2:
                    act.wait_ge(inner_ready, u - 1)
                act.activation(silu[u % 2][:, :], gate_bank[u % 2][:, :], ACT.Silu).then_inc(silu_ready, 1)
                act.wait_ge(inner_ready, u + 1)
                if c >= 2:
                    act.wait_ge(y_ready, 2 * (c - 1))
                act.activation(innerT[c % 2][k].hi[:, :], inner[u % 2][:, :], ACT.Copy).then_inc(inner_hi, 1)

            for c in range(CHUNKS):
                act.wait_ge(less1_ready, c + 1)
                act.activation(e1[:, :], e1[:, :], ACT.Exp).then_inc(exp1_ready, 1)
                for k in range(SI):
                    shared(c, k)
                act.wait_ge(less2_ready, c + 1)
                act.activation(e2[:, :], e2[:, :], ACT.Exp).then_inc(exp2_ready, 1)
                act.wait_ge(soft_turned, c + 1)
                act.activation(softT.hi[0:FK, c * CT:(c + 1) * CT], turned_bank[0:FK, :], ACT.Copy).then_inc(softT_hi, 1)

        @block.vector
        def _(dve):
            dve.wait_ge(w_hi, 1)
            dve.tensor_tensor(W.lo[:, :], w32[:, :], W.hi[:, :].bitcast(F32), ALU.subtract).then_inc(w_lo, 1)
            dve.wait_ge(small_in, 32)
            dve.tensor_copy(inv[:, :], inv_raw[:, :]).then_inc(inv_ready, 1)
            dve.wait_ge(inv_ready, 1)
            dve.tensor_scalar(onehot[:, :], inv[:, :], rows[:, 0:1], None, ALU.is_equal).then_inc(onehot_ready, 1)
            dve.memset(s3[:, :, E:E + 1], 3.0).then_inc(sentinels, 1)
            dve.memset(s3[:, :, E + 1:E + 2], 2.0).then_inc(sentinels, 1)
            dve.wait_ge(sentinels, 2)

            def shared(c, k):
                u = c * SI + k
                dve.wait_ge(silu_ready, u + 1)
                if u >= 2:
                    dve.wait_ge(inner_lo, u - 1)
                dve.tensor_tensor(inner[u % 2][:, :], up_bank[u % 2][:, :], silu[u % 2][:, :], ALU.mult).then_inc(inner_ready, 1)

            def shared_out(c):
                for i in range(2):
                    t = c * TT + 2 * i
                    dve.wait_ge(y_ready, 2 * c + i + 1)
                    two = r[:, t * D:(t + 2) * D]
                    dve.tensor_tensor(two, y_bank[i][:, :], two, ALU.add).then_inc(r_ready, 1)

            for c in range(CHUNKS):
                n = c + 1
                dve.wait_ge(logit_ready, n)
                dve.tensor_reduce(top1[:, :], tok3, AX.X, ALU.max).then_inc(top1_ready, 1)
                dve.wait_ge(top1_ready, n)
                dve.tensor_tensor(e1[:, :].rearrange("p (t e) -> p t e", t=TT), tok3, wide(top1, TT, E), ALU.subtract
                                  ).then_inc(less1_ready, 1)
                dve.wait_ge(exp1_ready, n)
                e13 = e1[:, :].rearrange("p (t e) -> p t e", t=TT)
                dve.tensor_reduce(mass[:, :], e13, AX.X, ALU.add).then_inc(mass1_ready, 1)
                dve.wait_ge(mass1_ready, n)
                dve.reciprocal(part[:, :], mass[:, :]).then_inc(part1_ready, 1)
                dve.wait_ge(part1_ready, n)
                dve.tensor_tensor(s3[:, :, 0:E], e13, wide(part, TT, E), ALU.mult).then_inc(soft1_ready, 1)
                dve.wait_ge(soft1_ready, n)
                for t in range(TT):
                    ins = dve.max(top8[:, t * 8:(t + 1) * 8], soft1[:, t * EX:(t + 1) * EX])
                ins.then_inc(top8_ready, 1)
                dve.wait_ge(top8_ready, n)
                for t in range(TT):
                    ins = dve.match_replace(rest[:, t * EX:(t + 1) * EX], top8[:, t * 8:(t + 1) * 8],
                                            soft1[:, t * EX:(t + 1) * EX], 0.0)
                ins.then_inc(rest_ready, 1)
                dve.wait_ge(rest_ready, n)
                dve.tensor_tensor(kept[:, :].rearrange("p (t e) -> p t e", t=TT), s3[:, :, 0:E], rest3[:, :, 0:E],
                                  ALU.subtract).then_inc(kept_ready, 1)
                shared(c, 0)
                shared(c, 1)
                dve.wait_ge(kept_turned, n)
                dve.tensor_copy(keptT[:, :], turned_bank[0:E, :]).then_inc(keptT_ready, 1)
                shared(c, 2)
                dve.wait_ge(flat_ready, n)
                dve.tensor_reduce(share_of[:, c * TT * F:(c + 1) * TT * F], tok8, AX.X, ALU.add)
                dve.tensor_scalar(unused[:, :], token_bank[:, 0:TT * FK], 0.0, -1e9, ALU.is_equal, ALU.mult
                                  ).then_inc(unused_ready, 1)
                dve.wait_ge(unused_ready, n)
                if c:
                    dve.wait_ge(soft_turned, c)
                dve.tensor_tensor(e2[:, :], token_bank[:, 0:TT * FK], unused[:, :], ALU.add).then_inc(masked_ready, 1)
                dve.wait_ge(masked_ready, n)
                dve.tensor_reduce(top2[:, :], e2_8, AX.X, ALU.max).then_inc(top2_ready, 1)
                dve.wait_ge(top2_ready, n)
                dve.tensor_tensor(e2_8, e2_8, wide(top2, TT * F, F), ALU.subtract).then_inc(less2_ready, 1)
                dve.wait_ge(exp2_ready, n)
                dve.tensor_reduce(mass2[:, :], e2_8, AX.X, ALU.add).then_inc(mass2_ready, 1)
                dve.wait_ge(mass2_ready, n)
                dve.reciprocal(part2[:, :], mass2[:, :]).then_inc(part2_ready, 1)
                dve.wait_ge(part2_ready, n)
                dve.tensor_tensor(e2_8, e2_8, wide(part2, TT * F, F), ALU.mult).then_inc(soft2_ready, 1)
                if c:
                    shared_out(c - 1)
                dve.wait_ge(softT_hi, n)
                if c:
                    dve.wait_ge(stored, 16 * c)
                dve.tensor_copy(softT32[:, :], turned_bank[0:FK, :]).then_inc(softT32_ready, 1)
                dve.tensor_tensor(softT.lo[0:FK, c * CT:(c + 1) * CT], turned_bank[0:FK, :],
                                  softT.hi[0:FK, c * CT:(c + 1) * CT].bitcast(F32), ALU.subtract).then_inc(softT_lo, 1)
            shared_out(CHUNKS - 1)


GU_AT = 0
QA_AT = GU_AT + DK * 2 * I
QB_AT = QA_AT + DK * P
D1_AT = QB_AT + 2 * I
D2_AT = D1_AT + D
DQ_AT = D2_AT + D
MU_AT = DQ_AT + 2 * P
WCOLS = MU_AT + D
I2 = I - P


def experts(nc, a, r, ident, xT32, softT, share_of, soft_dram):
    m = Memory(nc, "moe")
    UNITS = 2 * CHUNKS
    with m.ctx:
        stage = m.sb("stage", WCOLS)
        scale = m.sb("scale", 2 * I + D)
        W = [m.split(f"W{n}", WCOLS) for n in range(2)]
        xe32 = m.sb("xe32", DK * CT)
        xe = [m.split(f"xe{n}", DK * CT) for n in range(2)]
        spread = [m.sb(f"spread{c}", CT) for c in range(CHUNKS)]
        low32 = m.sb("low32", CT)
        low = [m.split(f"low{n}", CT) for n in range(2)]
        silu = [m.sb(f"silu{n}", I) for n in range(2)]
        inner = m.sb("inner", TT * I)
        innerT = m.split("innerT", 2 * CT)
        dlow32 = m.sb("dlow32", CT)
        shares = m.sb("shares", 2 * B)

        feat = [m.bank(f"feat{n}") for n in range(2)]
        gu = [m.bank(f"gu{n}") for n in range(2)]
        turned = [m.bank(f"turned{n}") for n in range(2)]
        y_bank = [m.bank(f"y{n}") for n in range(2)]

        w_in, scale_in, w_scaled, w_hi, w_lo = (
            m.sem("w_in"), m.sem("scale_in"), m.sem("w_scaled"), m.sem("w_hi"), m.sem("w_lo"))
        spread_in = [m.sem(f"spread_in{c}") for c in range(CHUNKS)]
        xe_ready, xe32_ready, xe_hi, xe_lo = m.sem("xe_ready"), m.sem("xe32_ready"), m.sem("xe_hi"), m.sem("xe_lo")
        low_ready, low32_ready, low_hi, low_lo = m.sem("low_ready"), m.sem("low32_ready"), m.sem("low_hi"), m.sem("low_lo")
        gu_ready, silu_ready, inner_ready = m.sem("gu_ready"), m.sem("silu_ready"), m.sem("inner_ready")
        turned_ready, turned_hi, turned_lo = m.sem("turned_ready"), m.sem("turned_hi"), m.sem("turned_lo")
        dlow_ready, dlow32_ready, dlow_hi, dlow_lo = (
            m.sem("dlow_ready"), m.sem("dlow32_ready"), m.sem("dlow_hi"), m.sem("dlow_lo"))
        y_ready, r_ready, shares_ready, padded = m.sem("y_ready"), m.sem("r_ready"), m.sem("shares_ready"), m.sem("padded")

        TURNS_E = F // 2
        block = m.ctx.enter_context(nc.Block())

        def count(g, u):
            return g * UNITS + u

        @block.sync
        def _(sp):
            def load_weights(e):
                sp.dma_start(stage[:, :], a["expert_w"][bass.ds(e, 1), :, :].rearrange("o p n -> p (o n)")).then_inc(w_in, 16)
                sp.dma_start(scale[:, :], a["expert_scale"][bass.ds(e, 1), :].to_broadcast([P, 2 * I + D])).then_inc(scale_in, 16)

            load_weights(0)
            with sp.Fori(1, F) as e:
                sp.wait_ge(w_lo, e)
                load_weights(e)

        @block.gpsimd
        def _(pool):
            def load_spread(e, c):
                for half in range(2):
                    pool.dma_start(spread[c][half * 64:(half + 1) * 64, :],
                                   soft_dram[bass.ds(e * F, F), c * CT:(c + 1) * CT].rearrange("(k o) t -> k o t", o=1)
                                   .to_broadcast([F, R, CT])).then_inc(spread_in[c], 16)

            def split_weights(n, e):
                w = W[n]
                pool.wait_ge(w_in, e * 16 + 16)
                pool.wait_ge(scale_in, e * 16 + 16)
                qb = slice(QB_AT, QB_AT + 2 * I)
                pool.tensor_tensor(stage[:, qb], stage[:, qb], scale[:, 0:2 * I], ALU.mult).then_inc(w_scaled, 1)
                dn = slice(D2_AT, D2_AT + D)
                pool.wait_ge(w_scaled, e * 2 + 1)
                pool.tensor_tensor(stage[64:P, dn], stage[64:P, dn], scale[64:P, 2 * I:], ALU.mult).then_inc(w_scaled, 1)
                pool.wait_ge(w_hi, e + 1)
                pool.tensor_tensor(w.lo[:, :], stage[:, :], w.hi[:, :].bitcast(F32), ALU.subtract).then_inc(w_lo, 1)

            def xe_low(g, u):
                pool.wait_ge(xe_hi, count(g, u + 1))
                pool.tensor_tensor(xe[u % 2].lo[:, :], xe32[:, :], xe[u % 2].hi[:, :].bitcast(F32), ALU.subtract
                                   ).then_inc(xe_lo, 1)

            for c in range(CHUNKS):
                load_spread(0, c)
            split_weights(0, 0)
            xe_low(0, 0)
            xe_low(0, 1)
            split_weights(1, 1)

            def load_next(g, u):
                pool.wait_ge(dlow32_ready, count(g, u + 1))
                load_spread(g * 2 + u // CHUNKS + 1, u % CHUNKS)

            def turn(g, first, last):
                for u in range(UNITS):
                    if not (last and u >= UNITS - 2):
                        xe_low(g, u + 2)
                    if u == 0 and not first:
                        pool.wait_ge(y_ready, 2 * count(g, 0))
                        split_weights(1, g * 2 + 1)
                    if u == CHUNKS and not last:
                        pool.wait_ge(y_ready, 2 * count(g, CHUNKS))
                        split_weights(0, g * 2 + 2)
                    if u and not (last and u > CHUNKS):
                        load_next(g, u - 1)
                if not last:
                    load_next(g, UNITS - 1)

            turn(0, True, False)
            with pool.Fori(1, TURNS_E - 1) as g:
                turn(g, False, False)
            turn(TURNS_E - 1, False, True)

        @block.tensor
        def _(pe):
            def inputs(g, u, slot):
                c = u % CHUNKS
                for k in range(DK):
                    mm = product(pe, feat[k][:, :], W[slot][0:FK, MU_AT + k * P:MU_AT + (k + 1) * P],
                                 softT[0:FK, c * CT:(c + 1) * CT])
                    mm.then_inc(xe_ready, 1)

            def low_rank(g, u, slot):
                pe.wait_ge(xe_lo, count(g, u + 1))
                for k in range(DK):
                    mm = product(pe, feat[1][:, :], W[slot][:, QA_AT + k * P:QA_AT + (k + 1) * P],
                                 xe[u % 2][:, k * CT:(k + 1) * CT], first=k == 0, last=k == DK - 1)
                mm.then_inc(low_ready, 1)

            def gate_up(g, u, t, slot):
                n = TT * u + t
                for k in range(DK):
                    product(pe, gu[t % 2][:, 0:2 * I], xe[u % 2][:, k * CT + t * P:k * CT + (t + 1) * P],
                            W[slot][:, GU_AT + k * 2 * I:GU_AT + (k + 1) * 2 * I], first=k == 0, last=False)
                if t == 0:
                    pe.wait_ge(low_lo, count(g, u + 1))
                product(pe, gu[t % 2][:, 0:2 * I], low[u % 2][:, t * P:(t + 1) * P], W[slot][:, QB_AT:QB_AT + 2 * I],
                        first=False).then_inc(gu_ready, 1)

            def down_low(g, u, slot):
                pe.wait_ge(turned_lo, 2 * count(g, u + 1))
                product(pe, feat[0][:, :], W[slot][:, DQ_AT:DQ_AT + P], innerT[:, 0:CT], last=False)
                product(pe, feat[0][:, :], W[slot][0:I2, DQ_AT + P:DQ_AT + 2 * P], innerT[0:I2, CT:2 * CT],
                        first=False).then_inc(dlow_ready, 1)

            def down(g, u, slot):
                pe.wait_ge(dlow_lo, count(g, u + 1))
                for i in range(2):
                    for j in range(2):
                        t = 2 * i + j
                        for k, at in ((0, D1_AT), (1, D2_AT)):
                            mm = product(pe, y_bank[i][:, j * D:(j + 1) * D], innerT[:, k * CT + t * P:k * CT + (t + 1) * P],
                                         W[slot][:, at:at + D], first=k == 0, last=k == 1)
                    mm.then_inc(y_ready, 1)

            def turn(g, first, last):
                for u in range(UNITS):
                    slot = u // CHUNKS
                    before = not (first and u == 0)
                    for t in range(TT):
                        if not (first and u == 0 and t < 2):
                            pe.wait_ge(inner_ready, g * UNITS * TT + TT * u + t - 1)
                        gate_up(g, u, t, slot)
                        if t == 1:
                            if before:
                                pe.wait_ge(xe32_ready, 2 * count(g, u + 2) - 1 if not (last and u == UNITS - 1)
                                           else 2 * count(g, u + 1) - 1)
                                down_low(g, u - 1, (u - 1) // CHUNKS if u else 1)
                            if not (last and u == UNITS - 1):
                                pe.wait_ge(xe32_ready, 2 * count(g, u + 2))
                                low_rank(g, u + 1, (u + 1) // CHUNKS % 2)
                    if before:
                        if not (first and u == 1):
                            pe.wait_ge(r_ready, 2 * count(g, u) - 2)
                        down(g, u - 1, (u - 1) // CHUNKS if u else 1)
                    if not (last and u >= UNITS - 2):
                        if u == 2 or u == CHUNKS + 2:
                            pe.wait_ge(w_lo, g * 2 + (2 if u == 2 else 3))
                        if before:
                            pe.wait_ge(dlow32_ready, count(g, u))
                        pe.wait_ge(low32_ready, count(g, u + 2))
                        inputs(g, u + 2, (u + 2) // CHUNKS % 2)
                    pe.wait_ge(inner_ready, g * UNITS * TT + TT * u + TT)
                    for t in range(TT):
                        mm = pe.transpose(turned[0][:, t * P:(t + 1) * P], inner[:, t * I:t * I + P], ident[:, :])
                    mm.then_inc(turned_ready, 1)
                    for t in range(TT):
                        mm = pe.transpose(turned[1][0:I2, t * P:(t + 1) * P], inner[:, t * I + P:(t + 1) * I], ident[:, :])
                    mm.then_inc(turned_ready, 1)

            pe.wait_ge(padded, 2)
            pe.wait_ge(w_lo, 1)
            inputs(0, 0, 0)
            pe.wait_ge(xe32_ready, 2)
            inputs(0, 1, 0)
            pe.wait_ge(xe32_ready, 4)
            low_rank(0, 0, 0)
            pe.wait_ge(low32_ready, 1)
            turn(0, True, False)
            with pe.Fori(1, TURNS_E - 1) as g:
                turn(g, False, False)
            turn(TURNS_E - 1, False, True)
            u = UNITS
            down_low(TURNS_E - 1, u - 1, 1)
            pe.wait_ge(r_ready, 2 * F * CHUNKS - 2)
            down(TURNS_E - 1, u - 1, 1)

        @block.scalar
        def _(act):
            def xe_high(g, u):
                act.wait_ge(xe32_ready, 2 * count(g, u + 1))
                act.activation(xe[u % 2].hi[:, :], xe32[:, :], ACT.Copy).then_inc(xe_hi, 1)

            def low_high(g, u):
                act.wait_ge(low32_ready, count(g, u + 1))
                act.activation(low[u % 2].hi[:, :], low32[:, :], ACT.Copy).then_inc(low_hi, 1)

            def dlow_high(g, u):
                act.wait_ge(dlow32_ready, count(g, u + 1))
                act.activation(innerT.hi[64:P, CT:2 * CT], dlow32[64:P, :], ACT.Copy).then_inc(dlow_hi, 1)

            def weights_high(n, e):
                act.wait_ge(w_scaled, e * 2 + 2)
                act.activation(W[n].hi[:, :], stage[:, :], ACT.Copy).then_inc(w_hi, 1)

            weights_high(0, 0)
            xe_high(0, 0)
            xe_high(0, 1)
            weights_high(1, 1)
            low_high(0, 0)

            def turn(g, first, last):
                for u in range(UNITS):
                    for t in range(TT):
                        act.wait_ge(gu_ready, g * UNITS * TT + TT * u + t + 1)
                        act.activation(silu[t % 2][:, :], gu[t % 2][:, 0:I], ACT.Silu).then_inc(silu_ready, 1)
                        if t == 2:
                            if not (first and u == 0):
                                dlow_high(g, u - 1)
                            if not (last and u == UNITS - 1):
                                low_high(g, u + 1)
                    if u == CHUNKS + 1 and not last:
                        weights_high(0, g * 2 + 2)
                    if u == 1 and not first:
                        weights_high(1, g * 2 + 1)
                    if not (last and u >= UNITS - 2):
                        xe_high(g, u + 2)
                    for k, rows in ((0, P), (1, I2)):
                        act.wait_ge(turned_ready, 2 * count(g, u) + k + 1)
                        act.activation(innerT.hi[0:rows, k * CT:(k + 1) * CT], turned[k][0:rows, :], ACT.Copy
                                       ).then_inc(turned_hi, 1)

            turn(0, True, False)
            with act.Fori(1, TURNS_E - 1) as g:
                turn(g, False, False)
            turn(TURNS_E - 1, False, True)
            dlow_high(TURNS_E - 1, UNITS - 1)

        @block.vector
        def _(dve):
            for part in (innerT.hi, innerT.lo):
                dve.memset(part[32:64, CT:2 * CT].bitcast(F32), 0.0).then_inc(padded, 1)
            dve.wait_ge(padded, 2)

            def xe_sum(g, u):
                c = u % CHUNKS
                for k in range(DK):
                    dve.wait_ge(xe_ready, 2 * count(g, u) + k + 1)
                    dve.tensor_tensor(xe32[:, k * CT:(k + 1) * CT], feat[k][:, :],
                                      xT32[:, k * B * S + c * CT:k * B * S + (c + 1) * CT], ALU.add).then_inc(xe32_ready, 1)

            def low_product(g, u):
                c = u % CHUNKS
                dve.wait_ge(low_ready, count(g, u + 1))
                dve.wait_ge(spread_in[c], (g * 2 + u // CHUNKS) * 32 + 32)
                dve.tensor_tensor(low32[:, :], feat[1][:, :], spread[c][:, :], ALU.mult).then_inc(low32_ready, 1)

            def low_low(g, u):
                dve.wait_ge(low_hi, count(g, u + 1))
                dve.tensor_tensor(low[u % 2].lo[:, :], low32[:, :], low[u % 2].hi[:, :].bitcast(F32), ALU.subtract
                                  ).then_inc(low_lo, 1)

            def dlow_product(g, u):
                c = u % CHUNKS
                dve.wait_ge(dlow_ready, count(g, u + 1))
                dve.tensor_tensor(dlow32[64:P, :], feat[0][64:P, :], spread[c][64:P, :], ALU.mult).then_inc(dlow32_ready, 1)

            def dlow_low(g, u):
                dve.wait_ge(dlow_hi, count(g, u + 1))
                c = slice(CT, 2 * CT)
                dve.tensor_tensor(innerT.lo[64:P, c], dlow32[64:P, :], innerT.hi[64:P, c].bitcast(F32), ALU.subtract
                                  ).then_inc(dlow_lo, 1)

            def add_output(g, u):
                c = u % CHUNKS
                for i in range(2):
                    t = c * TT + 2 * i
                    dve.wait_ge(y_ready, 2 * count(g, u) + i + 1)
                    two = r[:, t * D:(t + 2) * D]
                    dve.tensor_tensor(two, y_bank[i][:, :], two, ALU.add).then_inc(r_ready, 1)

            xe_sum(0, 0)
            dve.wait_ge(xe_lo, 1)
            xe_sum(0, 1)
            low_product(0, 0)
            low_low(0, 0)

            def turn(g, first, last):
                if not first:
                    dve.wait_ge(inner_ready, g * UNITS * TT)
                dve.tensor_copy(shares[:, :].rearrange("p (e t) -> p e t", e=2),
                                share_of[:, :].rearrange("p (t e) -> p e t", e=F)[:, bass.ds(g * 2, 2), :]
                                ).then_inc(shares_ready, 1)
                dve.wait_ge(shares_ready, g + 1)
                for u in range(UNITS):
                    e, c = u // CHUNKS, u % CHUNKS
                    before = not (first and u == 0)
                    for t in range(TT):
                        if t == 2:
                            if before:
                                dlow_product(g, u - 1)
                            if not (last and u == UNITS - 1):
                                low_product(g, u + 1)
                        n = g * UNITS * TT + TT * u + t + 1
                        dve.wait_ge(silu_ready, n)
                        if t == 0 and before:
                            dve.wait_ge(turned_ready, 2 * count(g, u))
                        at = e * B + c * TT + t
                        dve.scalar_tensor_tensor(inner[:, t * I:(t + 1) * I], silu[t % 2][:, :], shares[:, at:at + 1],
                                                 gu[t % 2][:, I:2 * I], ALU.mult, ALU.mult).then_inc(inner_ready, 1)
                        if t == 2:
                            if before:
                                dlow_low(g, u - 1)
                            if not (last and u == UNITS - 1):
                                low_low(g, u + 1)
                    if before:
                        add_output(g, u - 1)
                    if not (last and u >= UNITS - 2):
                        dve.wait_ge(xe_lo, count(g, u + 2))
                        xe_sum(g, u + 2)
                    for k, rows in ((0, P), (1, I2)):
                        dve.wait_ge(turned_hi, 2 * count(g, u) + k + 1)
                        c_ = slice(k * CT, (k + 1) * CT)
                        dve.tensor_tensor(innerT.lo[0:rows, c_], turned[k][0:rows, :], innerT.hi[0:rows, c_].bitcast(F32),
                                          ALU.subtract).then_inc(turned_lo, 1)

            turn(0, True, False)
            with dve.Fori(1, TURNS_E - 1) as g:
                turn(g, False, False)
            turn(TURNS_E - 1, False, True)
            g = TURNS_E - 1
            dlow_product(g, UNITS - 1)
            dlow_low(g, UNITS - 1)
            add_output(g, UNITS - 1)


def last_norm(nc, a, r):
    m = Memory(nc, "norm")
    with m.ctx:
        stats, mv = m.sb("stats", 6 * B), m.sb("mv", 2 * B)
        var, std, rstd = m.sb("var", B), m.sb("std", B), m.sb("rstd", B)
        stats_ready, mv_ready, var_ready, std_ready, rstd_ready = (
            m.sem("stats_ready"), m.sem("mv_ready"), m.sem("var_ready"), m.sem("std_ready"), m.sem("rstd_ready"))
        by_dve, by_pool, stored = m.sem("by_dve"), m.sem("by_pool"), m.sem("stored")
        out = a["out"].rearrange("b s d -> s b d")
        block = m.ctx.enter_context(nc.Block())

        def normalise(eng, t):
            here = r[:, t * D:(t + 1) * D]
            return eng.tensor_scalar(here, here, mv[:, 2 * t:2 * t + 1], rstd[:, t:t + 1], ALU.subtract, ALU.mult)

        @block.vector
        def _(dve):
            for t in range(B):
                ins = dve.bn_stats(stats[:, 6 * t:6 * t + 6], r[:, t * D:(t + 1) * D])
            ins.then_inc(stats_ready, 1)
            dve.wait_ge(stats_ready, 1)
            for t in range(B):
                ins = dve.bn_aggr(mv[:, 2 * t:2 * t + 2], stats[:, 6 * t:6 * t + 6])
            ins.then_inc(mv_ready, 1)
            dve.wait_ge(mv_ready, 1)
            dve.tensor_scalar(var[:, :], mv[:, :].rearrange("p (t s) -> p t s", s=2)[:, :, 1], LN_EPS, None, ALU.add
                              ).then_inc(var_ready, 1)
            dve.wait_ge(std_ready, 1)
            dve.reciprocal(rstd[:, :], std[:, :]).then_inc(rstd_ready, 1)
            dve.wait_ge(rstd_ready, 1)
            for t in range(0, B, 2):
                normalise(dve, t).then_inc(by_dve, 1)

        @block.gpsimd
        def _(pool):
            pool.wait_ge(rstd_ready, 1)
            for t in range(1, B, 2):
                normalise(pool, t).then_inc(by_pool, 1)

        @block.scalar
        def _(act):
            act.wait_ge(var_ready, 1)
            act.activation(std[:, :], var[:, :], ACT.Sqrt).then_inc(std_ready, 1)

        @block.sync
        def _(sp):
            for c in range(4):
                sp.wait_ge(by_dve, 2 * c + 2)
                sp.wait_ge(by_pool, 2 * c + 2)
                sp.dma_start(out[:, 4 * c:4 * c + 4, :], r[:, 4 * c * D:4 * (c + 1) * D].rearrange("p (b d) -> p b d", b=4)
                             ).then_inc(stored, 16)
            sp.wait_ge(stored, 64)


def program(nc, a):
    m = Memory(nc, "all")
    with m.ctx:
        r = m.sb("r", B * D)
        stats = m.sb("stats", B * 6)
        ident = m.sb("ident", P)
        self_attention(nc, a, r, stats, ident)
        share_of = m.sb("share_of", B * F)
        softT = m.split("softT", B * S, FK)
        xT32 = m.sb("xT32", DK * B * S)
        soft_dram = nc.dram_tensor("soft_dram", [FK, B * S], F32, kind="Internal").ap()
        turned = Memory(nc, "features")
        with turned.ctx:
            xT = turned.split("xT", DK * B * S)
            cross_attention(nc, a, r, stats, ident, xT)
            route_and_share(nc, a, r, ident, xT, xT32, softT, share_of, soft_dram)
        experts(nc, a, r, ident, xT32, softT, share_of, soft_dram)
        last_norm(nc, a, r)


def decay_mask(np):
    gam = (1.0 - 2.0 ** (-5.0 - np.arange(XH, dtype=np.float32))).astype(np.float32)
    at = np.arange(S, dtype=np.float32)
    expo = at[None, :] - at[:, None]
    D_ = np.where(expo[None] <= 0, gam[:, None, None] ** expo[None], np.float32(0)).astype(np.float32)
    D_ = D_ / np.sqrt(D_.sum(-1))[:, None, :]
    return D_.transpose(2, 0, 1).reshape(S, XH * S).astype(np.float32)


def layout(np, v):
    T = B * S

    def rows(w, n=P):
        return w.reshape(-1, n, w.shape[1]).transpose(1, 0, 2).reshape(n, -1)

    def padded(w, shape):
        out = np.zeros(shape, w.dtype)
        out[tuple(slice(0, n) for n in w.shape)] = w
        return out

    ffn = lambda name: v["L0_ffn_" + name]
    Wh = v["L0_xattn_Wh"]
    out = {
        "x_tok": v["x"].transpose(1, 0, 2).reshape(S, B * D),
        "xT": v["x"].reshape(T, DK, P).transpose(2, 1, 0),
        "Wq": v["L0_attn_Wq"].reshape(DK, P, KV, G * DH).transpose(1, 2, 0, 3).reshape(P, -1),
        "Wk": rows(v["L0_attn_Wk"]), "Wv": rows(v["L0_attn_Wv"]), "Wo": rows(v["L0_attn_Wo"]),
        "bq": v["L0_attn_bq"].reshape(H, DH).T, "bk": v["L0_attn_bk"].reshape(KV, DH).T,
        "bv": v["L0_attn_bv"].reshape(KV, DH).T, "bo": v["L0_attn_bo"],
        "ident": np.eye(P, dtype=np.float32),
        "cross_w": np.concatenate([Wh.transpose(1, 0, 2).reshape(HD, -1), Wh.transpose(2, 0, 1).reshape(HD, -1),
                                   rows(v["L0_xattn_wg_w"]), rows(v["L0_xattn_wo_w"])], 1),
        "ctxT": v["ctx_2048"].reshape(T, XH, HD).transpose(2, 1, 0),
        "gamma": v["L0_xattn_gn_gamma"], "beta": v["L0_xattn_gn_beta"], "decay": decay_mask(np),
        "route_w": np.concatenate([rows(ffn("gate_weight").T), rows(padded(ffn("sh_gate_W").T, (D, SI * P))),
                                   rows(padded(ffn("sh_up_W").T, (D, SI * P))),
                                   rows(padded(ffn("sh_down_W").T, (SI * P, D)))], 1),
        "inv": ffn("inv_mapping").reshape(-1),
        "rows": np.arange(E, dtype=np.float32).reshape(E, 1),
        "expert_scale": np.concatenate([ffn("gate_scale"), ffn("up_scale"), ffn("down_scale")], 1),
    }
    KR = F * R
    W = np.zeros((F, P, WCOLS), np.float32)
    for f in range(F):
        w = W[f]
        w[:, GU_AT:QA_AT] = rows(np.concatenate([ffn("gate_W")[f].T, ffn("up_W")[f].T], 1))
        w[:, QA_AT:QB_AT] = rows(np.concatenate([ffn("gate_qa")[f].reshape(KR, D).T, ffn("up_qa")[f].reshape(KR, D).T], 1))
        w[:KR, QB_AT:QB_AT + I] = ffn("gate_qb")[f].transpose(0, 2, 1).reshape(KR, I)
        w[KR:, QB_AT + I:D1_AT] = ffn("up_qb")[f].transpose(0, 2, 1).reshape(KR, I)
        w[:, D1_AT:D2_AT] = ffn("down_W")[f].T[:P]
        w[:I2, D2_AT:DQ_AT] = ffn("down_W")[f].T[P:]
        w[KR:, D2_AT:DQ_AT] = ffn("down_qb")[f].transpose(0, 2, 1).reshape(KR, D)
        qa = ffn("down_qa")[f].reshape(KR, I).T
        w[:, DQ_AT + KR:DQ_AT + P] = qa[:P]
        w[:I2, DQ_AT + P + KR:MU_AT] = qa[P:]
        w[f * F:(f + 1) * F, MU_AT:] = ffn("mask_up_W")[f].T
    out["expert_w"] = W
    return out


def kernel(**inputs):
    import numpy as np
    import concourse.bacc as bacc
    from concourse.bass_utils import run_bass_kernel_spmd

    laid = layout(np, {name: np.asarray(x) for name, x in inputs.items()})
    nc = bacc.Bacc("TRN2", target_bir_lowering=False, num_devices=1)
    arrays, args = {}, {}
    for name, x in laid.items():
        x = np.ascontiguousarray(x)
        arrays[f"in_{name}"] = x
        args[name] = nc.dram_tensor(f"in_{name}", x.shape, mybir.dt.from_np(x.dtype), kind="ExternalInput").ap()
    args["out"] = nc.dram_tensor("out_0", (B, S, D), F32, kind="ExternalOutput").ap()
    program(nc, args)
    done = run_bass_kernel_spmd(nc, [arrays], core_ids=[0])
    return done.results[0]["out_0"]
```

```python
from contextlib import ExitStack

import concourse.bass as bass
from concourse import mybir
from concourse.alu_op_type import AluOpType as ALU

F32 = mybir.dt.float32
F32R = mybir.dt.float32r
ACT = mybir.ActivationFunctionType
AX = mybir.AxisListType

P = 128
B, S, D = 16, 128, 256
DK = D // P
H, KV, DH = 16, 4, 128
G = H // KV
PAIR = 2
TURNS = B // PAIR
TOK = PAIR * S
XH, HD = 2, 128
E, F, TOPK, I, R = 64, 8, 6, 176, 8
IH = I // 2
LN_EPS, GN_EPS = 1e-5, 1e-3


class Split:

    def __init__(self, hi, lo):
        self.hi, self.lo = hi, lo

    def __getitem__(self, at):
        return Split(self.hi[at], self.lo[at])

    def rearrange(self, *a, **k):
        return Split(self.hi.rearrange(*a, **k), self.lo.rearrange(*a, **k))


def product(pe, out, left, right, first=True, last=True, **more):
    pe.matmul(out, left.hi, right.hi, start=first, stop=False, **more)
    pe.matmul(out, left.hi, right.lo, start=False, stop=False, **more)
    return pe.matmul(out, left.lo, right.hi, start=False, stop=last, **more)


class Memory:

    def __init__(self, nc, stage):
        self.nc, self.stage, self.ctx, self.sems = nc, stage, ExitStack(), []
        self.ctx.callback(self.reset_sems)

    def sb(self, name, cols, dt=F32, parts=P):
        return self.ctx.enter_context(self.nc.sbuf_tensor(f"{self.stage}_{name}", [parts, cols], dt))

    def split(self, name, cols, parts=P):
        return Split(self.sb(name + "_hi", cols, F32R, parts), self.sb(name + "_lo", cols, F32R, parts))

    def bank(self, name):
        return self.ctx.enter_context(self.nc.psum_tensor(f"{self.stage}_{name}", [P, 512], F32))

    def sem(self, name):
        self.sems.append(self.nc.alloc_semaphore(name=f"{self.stage}_{name}"))
        return self.sems[-1]

    def reset_sems(self):
        if not self.sems:
            return
        self.nc.clear_and_free_semaphores(self.sems)
        self.nc.all_engine_barrier()


def self_attention(nc, a, r1, stats1, ident):
    m = Memory(nc, "att")
    with m.ctx:
        CH = 1024
        stage = [m.sb(f"stage{n}", CH) for n in range(4)]
        Wq = m.split("Wq", KV * CH)
        Wk, Wv = m.split("Wk", CH), m.split("Wv", CH)
        Wo = m.split("Wo", KV * CH)
        bq, bk, bv = m.sb("bq", H), m.sb("bk", KV), m.sb("bv", KV)
        bo = m.sb("bo", PAIR * D)
        xT32 = m.sb("xT32", DK * TOK)
        xT = m.split("xT", DK * TOK)
        x_tok = m.sb("x_tok", PAIR * D)
        QT = [m.split(f"QT{n}", G * TOK) for n in range(2)]
        KT = m.split("KT", KV * TOK)
        V = m.split("V", PAIR * KV * DH)
        by_job = lambda name, cols: [[m.sb(f"{name}{j}{b}", cols) for b in range(PAIR)] for j in range(2)]
        probs, mass, share = by_job("probs", G * S), by_job("mass", G), by_job("share", G)
        PT = [m.split(f"PT{b}", G * S) for b in range(PAIR)]
        OT = m.split("OT", G * TOK)
        top = [m.sb(f"top{b}", G) for b in range(PAIR)]
        bias = [m.sb(f"bias{b}", G) for b in range(PAIR)]
        stats, r_now = m.sb("stats", PAIR * 6), m.sb("r_now", PAIR * D)

        proj_banks = [m.bank(f"proj{n}") for n in range(3)]
        score = [m.bank(f"score{b}") for b in range(PAIR)]
        mix = [m.bank(f"mix{b}") for b in range(PAIR)]
        acc = m.bank("acc")

        small_in = m.sem("small_in")
        w_in = [m.sem(f"w_in{n}") for n in range(4)]
        w_hi, w_lo = m.sem("w_hi"), m.sem("w_lo")
        pool_hi, pool_lo = m.sem("pool_hi"), m.sem("pool_lo")
        xT_in, xT_hi, xT_lo = m.sem("xT_in"), m.sem("xT_hi"), m.sem("xT_lo")
        x_in, xb_ready = m.sem("x_in"), m.sem("xb_ready")
        proj_ready, proj_hi, proj_lo = m.sem("proj_ready"), m.sem("proj_hi"), m.sem("proj_lo")
        score_ready, max_ready, bias_ready = m.sem("score_ready"), m.sem("max_ready"), m.sem("bias_ready")
        exp_ready, share_ready, prob_ready = m.sem("exp_ready"), m.sem("share_ready"), m.sem("prob_ready")
        pt_ready, pt_hi, pt_lo = m.sem("pt_ready"), m.sem("pt_hi"), m.sem("pt_lo")
        o_ready, o_hi, o_lo = m.sem("o_ready"), m.sem("o_hi"), m.sem("o_lo")
        acc_ready, r_ready, stats_ready, kept_ready = (
            m.sem("acc_ready"), m.sem("r_ready"), m.sem("stats_ready"), m.sem("kept_ready"))

        SCALE = float(DH) ** -0.5
        cut = lambda j: slice(j * CH, (j + 1) * CH)
        q_chunk = lambda j, who: (a["Wq"][:, cut(j)], Wq[:, cut(j)], who)
        o_chunk = lambda j: (a["Wo"][:, cut(j)], Wo[:, cut(j)], "pool")
        chunks = [(a["Wk"], Wk[:, :], "act"), q_chunk(0, "act"), q_chunk(1, "act"), (a["Wv"], Wv[:, :], "act"),
                  q_chunk(2, "pool"), o_chunk(0), q_chunk(3, "pool"), o_chunk(1), o_chunk(2), o_chunk(3)]
        act_chunks = [n for n, c in enumerate(chunks) if c[2] == "act"]
        pool_chunks = [n for n, c in enumerate(chunks) if c[2] == "pool"]
        wq_at = {2: 1, 3: 3}
        wo_at = {0: 2, 1: 4, 2: 5, 3: 6}
        FIRST, PER = 8, 12

        def unit(g, n):
            return FIRST + PER * g + n

        def proj(n):
            return proj_banks[(FIRST + n - 1) % 3]

        def units_of(kind):
            if kind in ("K", "V"):
                return [(kind, 0), (kind, 1)]
            return [("Q", kind, 0), ("Q", kind, 1)]

        BEFORE = units_of("K") + units_of(0) + units_of(1) + units_of("V")

        def step_units(j, last):
            if j < 2:
                return units_of(j + 2)
            if last:
                return []
            return units_of("K") + units_of(0) if j == 2 else units_of(1)

        def job(g, j, b):
            return g * KV * PAIR + PAIR * j + b + 1

        block = m.ctx.enter_context(nc.Block())

        @block.sync
        def _(sp):
            sp.dma_start(xT32[:, :].rearrange("p (k t) -> p k t", k=DK), a["xT"][:, :, 0:TOK]).then_inc(xT_in, 16)
            for n, (src, _dst, _who) in enumerate(chunks):
                if n == 1:
                    for dst, src_s in ((bq[:, :], a["bq"]), (bk[:, :], a["bk"]), (bv[:, :], a["bv"])):
                        sp.dma_start(dst, src_s).then_inc(small_in, 16)
                    sp.dma_start(bo[:, :].rearrange("p (b d) -> p b d", b=PAIR),
                                 a["bo"].rearrange("(o b d) -> o b d", o=1, b=1).to_broadcast([P, PAIR, D])
                                 ).then_inc(small_in, 16)
                    sp.dma_start(ident[:, :], a["ident"]).then_inc(small_in, 16)
                if n >= 4:
                    if chunks[n - 4][2] == "act":
                        sp.wait_ge(w_lo, n - 3)
                    else:
                        sp.wait_ge(pool_lo, pool_chunks.index(n - 4) + 1)
                sp.dma_start(stage[n % 4][:, :], src).then_inc(w_in[n % 4], 16)
            with sp.Fori(0, TURNS - 1) as g:
                sp.wait_ge(xT_lo, g + 1)
                sp.dma_start(xT32[:, :].rearrange("p (k t) -> p k t", k=DK),
                             a["xT"][:, :, bass.ds(g * TOK + TOK, TOK)]).then_inc(xT_in, 16)

        @block.gpsimd
        def _(pool):
            def load_x(g):
                pool.dma_start(x_tok[:, :], a["x_tok"][:, bass.ds(g * PAIR * D, PAIR * D)]).then_inc(x_in, 16)

            def split_x(g):
                pool.wait_ge(xT_hi, g + 1)
                pool.tensor_tensor(xT.lo[:, :], xT32[:, :], xT.hi[:, :].bitcast(F32), ALU.subtract).then_inc(xT_lo, 1)

            split_x(0)
            waiting = list(enumerate(pool_chunks))

            def split_chunk():
                n, at = waiting.pop(0)
                dst = chunks[at][1]
                pool.wait_ge(w_in[at % 4], 16 * (at // 4 + 1))
                pool.tensor_copy(dst.hi, stage[at % 4][:, :]).then_inc(pool_hi, 1)
                pool.wait_ge(pool_hi, n + 1)
                pool.tensor_tensor(dst.lo, stage[at % 4][:, :], dst.hi.bitcast(F32), ALU.subtract).then_inc(pool_lo, 1)

            def normalise(g, j):
                for b in range(PAIR):
                    pool.wait_ge(share_ready, job(g, j, b))
                    p3 = probs[j % 2][b][:, :].rearrange("p (h k) -> p h k", h=G)
                    pool.tensor_tensor(p3, p3, share[j % 2][b][:, :].rearrange("p (h o) -> p h o", o=1).to_broadcast([P, G, S]),
                                       ALU.mult).then_inc(prob_ready, 1)

            def turn(g, first, last):
                load_x(g)
                for j in range(KV):
                    if j < KV - 1:
                        normalise(g, j + 1)
                    elif not last:
                        normalise(g + 1, 0)
                    if first and waiting:
                        split_chunk()
                        split_chunk()
                    if j == 1 and not last:
                        split_x(g + 1)
                    if j == 2:
                        pool.wait_ge(small_in, 80)
                        pool.wait_ge(x_in, g * 16 + 16)
                        pool.tensor_tensor(x_tok[:, :], x_tok[:, :], bo[:, :], ALU.add).then_inc(xb_ready, 1)
                pool.wait_ge(r_ready, g + 1)

            split_chunk()
            normalise(0, 0)
            split_chunk()
            turn(0, True, False)
            with pool.Fori(1, TURNS - 1) as g:
                turn(g, False, False)
            turn(TURNS - 1, False, True)

        @block.tensor
        def _(pe):
            def project(what, n):
                out = proj(n)
                if what[0] == "V":
                    b = what[1]
                    for k in range(DK):
                        mm = product(pe, out[:, :], xT[:, k * TOK + b * S:k * TOK + (b + 1) * S],
                                     Wv[:, k * 512:(k + 1) * 512], first=k == 0, last=k == DK - 1)
                else:
                    W = Wk[:, :] if what[0] == "K" else Wq[:, what[1] * CH:(what[1] + 1) * CH]
                    for h in range(2):
                        head = 2 * what[-1] + h
                        for k in range(DK):
                            mm = product(pe, out[:, h * TOK:(h + 1) * TOK],
                                         W[:, k * 512 + head * DH:k * 512 + (head + 1) * DH],
                                         xT[:, k * TOK:(k + 1) * TOK], first=k == 0, last=k == DK - 1)
                mm.then_inc(proj_ready, 1)

            pe.wait_ge(xT_lo, 1)
            for n, what in enumerate(BEFORE, 1):
                if n % 2:
                    pe.wait_ge(w_lo, (n + 1) // 2)
                if n > 3:
                    pe.wait_ge(proj_lo, n - 3)
                project(what, n - FIRST)
            pe.wait_ge(small_in, 80)

            def scores(j, g=None):
                for b in range(PAIR):
                    if g is not None:
                        pe.wait_ge(exp_ready, job(g, j - 1, b))
                    for h in range(G):
                        mm = product(pe, score[b][:, h * S:(h + 1) * S],
                                     QT[j % 2][:, h * TOK + b * S:h * TOK + (b + 1) * S],
                                     KT[:, j % KV * TOK + b * S:j % KV * TOK + (b + 1) * S])
                    mm.then_inc(score_ready, 1)

            scores(0)

            def turn(g, last, weights):
                n = 0

                def projects(what):
                    nonlocal n
                    n += 1
                    pe.wait_ge(proj_lo, unit(g, n) - 3)
                    project(what, n)

                def out_project(j):
                    if weights:
                        pe.wait_ge(pool_lo, wo_at[j])
                    pe.wait_ge(o_lo, g * KV * PAIR + PAIR * (j + 1))
                    if j == 0:
                        if not weights:
                            pe.wait_ge(r_ready, g)
                    for b in range(PAIR):
                        for h in range(G):
                            mm = product(pe, acc[:, b * D:(b + 1) * D],
                                         OT[:, (h * PAIR + b) * S:(h * PAIR + b + 1) * S],
                                         Wo[:, j * CH + h * D:j * CH + (h + 1) * D],
                                         first=j == 0 and b == 0 and h == 0, last=j == KV - 1 and h == G - 1,
                                         skip_group_check=True)
                    if j == KV - 1:
                        mm.then_inc(acc_ready, 1)

                for j in range(KV):
                    if not (last and j == KV - 1):
                        pe.wait_ge(proj_lo, (unit(g, 0) - 2, unit(g, 2), unit(g, 4), unit(g, 8))[j])
                        scores(j + 1, g)
                    for b in range(PAIR):
                        pe.wait_ge(prob_ready, job(g, j, b))
                        if j or not weights:
                            pe.wait_ge(o_lo, job(g, j - 1, b))
                        for h in range(G):
                            mm = pe.transpose(mix[b][:, h * S:(h + 1) * S], probs[j % 2][b][:, h * S:(h + 1) * S],
                                              ident[:, :])
                        mm.then_inc(pt_ready, 1)
                    if j < 2 and weights:
                        pe.wait_ge(pool_lo, wq_at[j + 2])
                    if j == 2 and not last:
                        pe.wait_ge(xT_lo, g + 2)
                    for what in step_units(j, last):
                        projects(what)
                    if j:
                        out_project(j - 1)
                    if j == 0:
                        pe.wait_ge(proj_lo, unit(g, 0))
                    for b in range(PAIR):
                        pe.wait_ge(pt_lo, job(g, j, b))
                        product(pe, mix[b][:, :], V[:, (b * KV + j) * DH:(b * KV + j + 1) * DH],
                                PT[b][:, :]).then_inc(o_ready, 1)
                    if j == KV - 1:
                        if not last:
                            for what in units_of("V"):
                                projects(what)
                        out_project(j)

            turn(0, False, True)
            with pe.Fori(1, TURNS - 1) as g:
                turn(g, False, False)
            turn(TURNS - 1, True, False)

        def copy_out(what):
            if what[0] == "V":
                b = what[1]
                return [(slice(0, 512), V[:, b * 512:(b + 1) * 512], None)]
            out = []
            for h in range(2):
                head = 2 * what[-1] + h
                where = slice(h * TOK, (h + 1) * TOK)
                if what[0] == "K":
                    out.append((where, KT[:, head * TOK:(head + 1) * TOK], bk[:, head:head + 1]))
                else:
                    q = what[1] * G + head
                    out.append((where, QT[what[1] % 2][:, head * TOK:(head + 1) * TOK], bq[:, q:q + 1]))
            return out

        @block.scalar
        def _(act):
            def high_x(g):
                act.wait_ge(xT_in, g * 16 + 16)
                act.activation(xT.hi[:, :], xT32[:, :], ACT.Copy).then_inc(xT_hi, 1)

            high_x(0)
            for n in act_chunks:
                act.wait_ge(w_in[n % 4], 16)
                act.activation(chunks[n][1].hi, stage[n % 4][:, :], ACT.Copy).then_inc(w_hi, 1)
            act.wait_ge(small_in, 80)

            def high(what, g, n):
                act.wait_ge(proj_ready, unit(g, n))
                for where, dst, b in copy_out(what):
                    src = proj(n)[:, where]
                    if b is None:
                        ins = act.activation(dst.hi, src, ACT.Copy)
                    else:
                        ins = act.activation(dst.hi, src, ACT.Identity, bias=b)
                ins.then_inc(proj_hi, 1)

            def exps(g, j, b):
                act.wait_ge(bias_ready, job(g, j, b))
                p_, m_ = probs[j % 2][b], mass[j % 2][b]
                for h in range(G):
                    c = slice(h * S, (h + 1) * S)
                    ins = act.activation(p_[:, c], score[b][:, c], ACT.Exp, bias=bias[b][:, h:h + 1],
                                         scale=SCALE, accum_out=m_[:, h:h + 1])
                ins.then_inc(exp_ready, 1)

            for n, what in enumerate(BEFORE, 1):
                high(what, -1, n + PER - FIRST)
            for b in range(PAIR):
                exps(0, 0, b)

            def turn(g, last):
                n = 0
                for j in range(KV):
                    for b in range(PAIR):
                        if not (last and j == KV - 1):
                            exps(g, j + 1, b)
                        act.wait_ge(pt_ready, job(g, j, b))
                        act.activation(PT[b].hi[:, :], mix[b][:, :], ACT.Copy).then_inc(pt_hi, 1)
                    for what in step_units(j, last):
                        n += 1
                        high(what, g, n)
                    if j == 1 and not last:
                        high_x(g + 1)
                    for b in range(PAIR):
                        act.wait_ge(o_ready, job(g, j, b))
                        act.activation(OT.hi[:, :].rearrange("p (h b q) -> p h b q", h=G, b=PAIR)[:, :, b, :],
                                       mix[b][:, :].rearrange("p (h q) -> p h q", h=G), ACT.Identity,
                                       bias=bv[:, j:j + 1]).then_inc(o_hi, 1)
                if not last:
                    for what in units_of("V"):
                        n += 1
                        high(what, g, n)

            with act.Fori(0, TURNS - 1) as g:
                turn(g, False)
            turn(TURNS - 1, True)

        @block.vector
        def _(dve):
            for n in act_chunks:
                dst = chunks[n][1]
                dve.wait_ge(w_hi, n + 1)
                dve.tensor_tensor(dst.lo, stage[n % 4][:, :], dst.hi.bitcast(F32), ALU.subtract).then_inc(w_lo, 1)
            dve.wait_ge(small_in, 80)

            def low(what, g, n):
                dve.wait_ge(proj_hi, unit(g, n))
                for where, dst, b in copy_out(what):
                    src = proj(n)[:, where]
                    if b is None:
                        ins = dve.tensor_tensor(dst.lo, src, dst.hi.bitcast(F32), ALU.subtract)
                    else:
                        ins = dve.scalar_tensor_tensor(dst.lo, src, b, dst.hi.bitcast(F32), ALU.add, ALU.subtract)
                ins.then_inc(proj_lo, 1)

            def maxima(g, j, b):
                dve.wait_ge(score_ready, job(g, j, b))
                dve.tensor_reduce(top[b][:, :], score[b][:, :].rearrange("p (h k) -> p h k", h=G), AX.X,
                                  ALU.max).then_inc(max_ready, 1)
                dve.wait_ge(max_ready, job(g, j, b))
                dve.tensor_scalar(bias[b][:, :], top[b][:, :], -SCALE, None, ALU.mult).then_inc(bias_ready, 1)

            def shares(g, j, b):
                dve.wait_ge(exp_ready, job(g, j, b))
                dve.reciprocal(share[j % 2][b][:, :], mass[j % 2][b][:, :]).then_inc(share_ready, 1)

            for n, what in enumerate(BEFORE, 1):
                low(what, -1, n + PER - FIRST)
            for b in range(PAIR):
                maxima(0, 0, b)
            for b in range(PAIR):
                shares(0, 0, b)

            def turn(g, last):
                n = 0
                for j in range(KV):
                    ahead = not (last and j == KV - 1)
                    for b in range(PAIR):
                        if ahead:
                            maxima(g, j + 1, b)
                    for b in range(PAIR):
                        if ahead:
                            shares(g, j + 1, b)
                        dve.wait_ge(pt_hi, job(g, j, b))
                        dve.tensor_tensor(PT[b].lo[:, :], mix[b][:, :], PT[b].hi[:, :].bitcast(F32), ALU.subtract
                                          ).then_inc(pt_lo, 1)
                    for what in step_units(j, last):
                        n += 1
                        low(what, g, n)
                    for b in range(PAIR):
                        dve.wait_ge(o_hi, job(g, j, b))
                        o4 = lambda t: t[:, :].rearrange("p (h b q) -> p h b q", h=G, b=PAIR)[:, :, b, :]
                        dve.scalar_tensor_tensor(o4(OT.lo), mix[b][:, :].rearrange("p (h q) -> p h q", h=G), bv[:, j:j + 1],
                                                 o4(OT.hi).bitcast(F32), ALU.add, ALU.subtract).then_inc(o_lo, 1)
                if not last:
                    for what in units_of("V"):
                        n += 1
                        low(what, g, n)
                dve.wait_ge(acc_ready, g + 1)
                dve.wait_ge(xb_ready, g + 1)
                dve.tensor_tensor(r_now[:, :], acc[:, :], x_tok[:, :], ALU.add).then_inc(r_ready, 1)
                dve.wait_ge(r_ready, g + 1)
                for b in range(PAIR):
                    ins = dve.bn_stats(stats[:, 6 * b:6 * b + 6], r_now[:, b * D:(b + 1) * D])
                ins.then_inc(stats_ready, 1)
                dve.tensor_scalar(r1[:, bass.ds(g * PAIR * D, PAIR * D)], r_now[:, :], 1.0, None, ALU.mult
                                  ).then_inc(kept_ready, 1)
                dve.wait_ge(stats_ready, g + 1)
                dve.tensor_scalar(stats1[:, bass.ds(g * PAIR * 6, PAIR * 6)], stats[:, :], 1.0, None, ALU.mult
                                  ).then_inc(kept_ready, 1)
                dve.wait_ge(kept_ready, 2 * g + 2)

            with dve.Fori(0, TURNS - 1) as g:
                turn(g, False)
            turn(TURNS - 1, True)


def cross_attention(nc, a, r, stats, ident, xT):
    m = Memory(nc, "cross")
    CB = 4
    CT = CB * S
    CHUNKS = B // CB
    HH = XH * HD
    with m.ctx:
        small = m.sb("small", 2 * HH + 2 * DK * D)
        Ws = m.split("W", 2 * HH + 2 * DK * D)
        Wh, WhT = Ws[:, 0:HH], Ws[:, HH:2 * HH]
        wg, wo = Ws[:, 2 * HH:2 * HH + DK * D], Ws[:, 2 * HH + DK * D:]
        gram = m.split("gram", HH)
        gamma, beta = m.sb("gamma", D), m.sb("beta", D)
        decay = m.sb("decay", XH * S)
        ctx32 = [m.sb(f"ctx32_{n}", XH * CT) for n in range(2)]
        ctxT = [m.split(f"ctxT{n}", XH * CT) for n in range(2)]
        KG = m.split("KG", XH * B * S)
        V = m.split("V", XH * B * HD)
        masked, positive = m.sb("masked", XH * S), m.sb("positive", XH * S)
        AT = m.split("AT", XH * S)
        Y = ctx32
        shift = m.sb("shift", B)
        WYT = [m.split(f"WYT{n}", 2 * D) for n in range(2)]
        WY = [small[:, n * 2 * D:(n + 1) * 2 * D] for n in range(2)]
        rstd = m.sb("rstd", B)
        std = m.sb("std", B)
        var = m.sb("var", B)
        ostats, omv = m.sb("ostats", CB * 12), m.sb("omv", CB * 2)
        ovar, ostd, orstd = m.sb("ovar", CB), m.sb("ostd", CB), m.sb("orstd", CB)
        oshift = m.sb("oshift", CB)
        mv = m.sb("mv", B * 2)
        bank = [m.bank(f"bank{n}") for n in range(8)]

        small_in, w_hi, w_lo = m.sem("small_in"), m.sem("w_hi"), m.sem("w_lo")
        const_in = m.sem("const_in")
        gram_ready, gram_hi, gram_lo = m.sem("gram_ready"), m.sem("gram_hi"), m.sem("gram_lo")
        ctx_in = [m.sem(f"ctx_in{n}") for n in range(2)]
        shift_ready, oshift_ready = m.sem("shift_ready"), m.sem("oshift_ready")
        ctx_hi, ctx_lo = m.sem("ctx_hi"), m.sem("ctx_lo")
        kv_ready, kv_hi, kv_lo = m.sem("kv_ready"), m.sem("kv_hi"), m.sem("kv_lo")
        var_ready, std_ready, rstd_ready = m.sem("var_ready"), m.sem("std_ready"), m.sem("rstd_ready")
        x_odd_ready = m.sem("x_odd_ready")
        x_ready, turned, turned_hi, turned_lo = m.sem("x_ready"), m.sem("turned"), m.sem("turned_hi"), m.sem("turned_lo")
        sum_ready, masked_ready, at32_ready, at_hi, at_lo = (
            m.sem("sum_ready"), m.sem("masked_ready"), m.sem("at32_ready"), m.sem("at_hi"), m.sem("at_lo"))
        o_ready, ostats_ready, omv_ready, ovar_ready, ostd_ready, orstd_ready, y_ready = (
            m.sem("o_ready"), m.sem("ostats_ready"), m.sem("omv_ready"), m.sem("ovar_ready"), m.sem("ostd_ready"),
            m.sem("orstd_ready"), m.sem("y_ready"))
        positive_ready = m.sem("positive_ready")
        scaled_ready, shifted_ready = m.sem("scaled_ready"), m.sem("shifted_ready")
        gate_ready, wy_ready, wyt_ready, wyt_hi, wyt_lo = (
            m.sem("gate_ready"), m.sem("wy_ready"), m.sem("wyt_ready"), m.sem("wyt_hi"), m.sem("wyt_lo"))
        out_ready, r_ready, stats_ready, mv_ready = (
            m.sem("out_ready"), m.sem("r_ready"), m.sem("stats_ready"), m.sem("mv_ready"))

        mean = lambda t: mv[:, 2 * t:2 * t + 1]
        tile = lambda t: r[:, t * D:(t + 1) * D]
        xT3 = lambda part: part[:, :].rearrange("p (k t) -> p k t", k=DK)

        block = m.ctx.enter_context(nc.Block())

        @block.sync
        def _(sp):
            sp.dma_start(small[:, :], a["cross_w"]).then_inc(small_in, 16)
            for c in range(CHUNKS):
                if c >= 2:
                    sp.wait_ge(ctx_lo, c - 1)
                sp.dma_start(ctx32[c % 2][:, :].rearrange("p (h t) -> p h t", h=XH),
                             a["ctxT"][:, :, c * CT:(c + 1) * CT]).then_inc(ctx_in[c % 2], 16)
                if c == 1:
                    sp.dma_start(decay[:, :], a["decay"]).then_inc(const_in, 16)
                    for dst, src in ((gamma, a["gamma"]), (beta, a["beta"])):
                        sp.dma_start(dst[:, :], src.rearrange("(o d) -> o d", o=1).to_broadcast([P, D])
                                     ).then_inc(const_in, 16)

        @block.gpsimd
        def _(pool):
            for c in range(CHUNKS):
                pool.wait_ge(ctx_hi, c + 1)
                pool.tensor_tensor(ctxT[c % 2].lo[:, :], ctx32[c % 2][:, :], ctxT[c % 2].hi[:, :].bitcast(F32),
                                   ALU.subtract).then_inc(ctx_lo, 1)
            pool.wait_ge(const_in, 48)
            for c in range(CHUNKS):
                Y3 = Y[c % 2][:, :].rearrange("p (b d) -> p b d", b=CB)
                pool.wait_ge(y_ready, c + 1)
                pool.tensor_tensor(Y3, Y3, gamma[:, :].rearrange("p (o d) -> p o d", o=1).to_broadcast([P, CB, D]),
                                   ALU.mult).then_inc(scaled_ready, 1)
                pool.wait_ge(scaled_ready, c + 1)
                pool.tensor_tensor(Y3, Y3, beta[:, :].rearrange("p (o d) -> p o d", o=1).to_broadcast([P, CB, D]),
                                   ALU.add).then_inc(shifted_ready, 1)

        @block.tensor
        def _(pe):
            def turn_tiles(u, at, banks, first_free):
                if at == 0:
                    pe.wait_ge(x_ready, 2 * u + 2)
                else:
                    pe.wait_ge(x_ready, B + u + 1)
                    pe.wait_ge(x_odd_ready, u + 1)
                if u >= 2:
                    pe.wait_ge(turned_lo, at * (B // 2) + u - 1)
                for k in range(DK):
                    for i in range(2):
                        t = 2 * u + i
                        mm = pe.transpose(bank[banks[u % 2]][:, (k * 2 + i) * P:(k * 2 + i + 1) * P],
                                          r[:, t * D + k * P:t * D + (k + 1) * P], ident[:, :])
                mm.then_inc(turned, 1)

            pe.wait_ge(w_lo, 1)
            for h in range(XH):
                mm = product(pe, bank[4][:, h * HD:(h + 1) * HD], WhT[:, h * HD:(h + 1) * HD], WhT[:, h * HD:(h + 1) * HD])
            mm.then_inc(gram_ready, 1)
            pe.wait_ge(gram_lo, 1)
            for c in range(CHUNKS):
                pe.wait_ge(ctx_lo, c + 1)
                for h in range(XH):
                    n = 4 * c + 2 * h
                    if n >= 4:
                        pe.wait_ge(kv_lo, n - 3)
                    product(pe, bank[n % 4][:, :], gram[:, h * HD:(h + 1) * HD], ctxT[c % 2][:, h * CT:(h + 1) * CT]
                            ).then_inc(kv_ready, 1)
                    if n >= 4:
                        pe.wait_ge(kv_lo, n - 2)
                    for b in range(CB):
                        mm = product(pe, bank[(n + 1) % 4][:, b * HD:(b + 1) * HD],
                                     ctxT[c % 2][:, h * CT + b * S:h * CT + (b + 1) * S], Wh[:, h * HD:(h + 1) * HD])
                    mm.then_inc(kv_ready, 1)

            def sum_scores(u):
                pe.wait_ge(turned_lo, u + 1)
                if u == 0:
                    pe.wait_ge(kv_lo, 4 * CHUNKS)
                for b in (2 * u, 2 * u + 1):
                    for h in range(XH):
                        at = slice(h * B * S + b * S, h * B * S + (b + 1) * S)
                        mm = product(pe, bank[6 + h][:, 0:S], KG[:, at], xT[:, at], first=b == 0, last=b == B - 1)
                if u == B // 2 - 1:
                    mm.then_inc(sum_ready, 1)

            pe.wait_ge(w_lo, 2)
            for u in range(B // 2):
                turn_tiles(u, 0, (4, 5), None)
                if u:
                    sum_scores(u - 1)
            sum_scores(B // 2 - 1)

            def mix_values(c):
                if c:
                    pe.wait_ge(y_ready, c)
                for h in range(XH):
                    mm = product(pe, bank[h][:, :], AT[:, h * S:(h + 1) * S],
                                 V[:, (h * B + c * CB) * HD:(h * B + (c + 1) * CB) * HD])
                mm.then_inc(o_ready, 1)

            def gates(c):
                for i in range(2):
                    if c:
                        pe.wait_ge(wy_ready, 2 * (c - 1) + i + 1)
                    for j in range(2):
                        b = c * CB + 2 * i + j
                        for k in range(DK):
                            mm = product(pe, bank[2 + i][:, j * D:(j + 1) * D], xT[:, (k * B + b) * S:(k * B + b + 1) * S],
                                         wg[:, k * D:(k + 1) * D], first=k == 0, last=k == DK - 1)
                    mm.then_inc(gate_ready, 1)

            gates(0)
            pe.wait_ge(at_lo, 1)
            mix_values(0)
            mix_values(1)
            for c in range(CHUNKS):
                for i in range(2):
                    pe.wait_ge(wy_ready, 2 * c + i + 1)
                    if c:
                        pe.wait_ge(wyt_lo, 2 * (c - 1) + i + 1)
                    for j in range(4):
                        mm = pe.transpose(bank[4 + i][:, j * P:(j + 1) * P], WY[i][:, j * P:(j + 1) * P], ident[:, :])
                    mm.then_inc(wyt_ready, 1)
                if c < CHUNKS - 1:
                    gates(c + 1)
                for i in range(2):
                    pe.wait_ge(wyt_lo, 2 * c + i + 1)
                    if c:
                        pe.wait_ge(r_ready, 2 * (c - 1) + i + 1)
                    for j in range(2):
                        for k in range(DK):
                            mm = product(pe, bank[6 + i][:, j * D:(j + 1) * D], WYT[i][:, (2 * j + k) * P:(2 * j + k + 1) * P],
                                         wo[:, k * D:(k + 1) * D], first=k == 0, last=k == DK - 1)
                    mm.then_inc(out_ready, 1)
                if c < CHUNKS - 2:
                    mix_values(c + 2)
            for u in range(B // 2):
                turn_tiles(u, 1, (0, 1), None)

        def split_turned(eng, u, at, banks):
            n = at * (B // 2) + u + 1
            src = bank[banks[u % 2]][:, :].rearrange("p (k t) -> p k t", k=DK)
            to = lambda part: xT3(part)[:, :, 2 * u * P:(2 * u + 2) * P]
            if eng == "act":
                nc.scalar.wait_ge(turned, n)
                nc.scalar.activation(to(xT.hi), src, ACT.Copy).then_inc(turned_hi, 1)
            else:
                nc.vector.wait_ge(turned_hi, n)
                nc.vector.tensor_tensor(to(xT.lo), src, to(xT.hi).bitcast(F32), ALU.subtract).then_inc(turned_lo, 1)

        def normalise_tiles(eng, at):
            if eng is nc.vector or at == 0:
                for t in range(0, B, 1 if at == 0 else 2):
                    nc.vector.tensor_scalar(tile(t), tile(t), mean(t), rstd[:, t:t + 1], ALU.subtract, ALU.mult
                                            ).then_inc(x_ready, 1)
            else:
                nc.scalar.wait_ge(shift_ready, 1)
                for t in range(1, B, 2):
                    nc.scalar.activation(tile(t), tile(t), ACT.Identity, bias=shift[:, t:t + 1], scale=rstd[:, t:t + 1]
                                         ).then_inc(x_odd_ready, 1)

        def kv_to(n):
            c, h = n // 4, n // 2 % 2
            if n % 2 == 0:
                return KG[:, h * B * S + c * CT:h * B * S + (c + 1) * CT]
            return V[:, (h * B + c * CB) * HD:(h * B + (c + 1) * CB) * HD]

        @block.scalar
        def _(act):
            def ctx_high(c):
                act.wait_ge(ctx_in[c % 2], 16 * (c // 2 + 1))
                if c >= 2:
                    act.wait_ge(kv_ready, 4 * (c - 1))
                act.activation(ctxT[c % 2].hi[:, :], ctx32[c % 2][:, :], ACT.Copy).then_inc(ctx_hi, 1)

            act.wait_ge(small_in, 16)
            act.activation(Ws.hi[:, 0:2 * HH], small[:, 0:2 * HH], ACT.Copy).then_inc(w_hi, 1)
            ctx_high(0)
            act.activation(Ws.hi[:, 2 * HH:], small[:, 2 * HH:], ACT.Copy).then_inc(w_hi, 1)
            act.wait_ge(gram_ready, 1)
            act.activation(gram.hi[:, :], bank[4][:, 0:HH], ACT.Copy).then_inc(gram_hi, 1)
            act.wait_ge(var_ready, 1)
            act.activation(std[:, :], var[:, :], ACT.Sqrt).then_inc(std_ready, 1)
            ctx_high(1)
            for n in range(4 * CHUNKS):
                if n in (4, 8):
                    ctx_high(n // 4 + 1)
                act.wait_ge(kv_ready, n + 1)
                act.activation(kv_to(n).hi, bank[n % 4][:, :], ACT.Copy).then_inc(kv_hi, 1)
            for u in range(B // 2):
                split_turned("act", u, 0, (4, 5))
            act.wait_ge(at32_ready, 1)
            act.activation(AT.hi[:, :], masked[:, :], ACT.Copy).then_inc(at_hi, 1)

            def normalise_mix(c):
                act.wait_ge(ovar_ready, c + 1)
                act.activation(ostd[:, :], ovar[:, :], ACT.Sqrt).then_inc(ostd_ready, 1)
                act.wait_ge(oshift_ready, c + 1)
                if c >= 2:
                    act.wait_ge(wy_ready, 2 * (c - 1))
                for b in range(CB):
                    for h in range(XH):
                        ins = act.activation(Y[c % 2][:, b * D + h * HD:b * D + (h + 1) * HD], bank[h][:, b * HD:(b + 1) * HD],
                                             ACT.Identity, bias=oshift[:, b:b + 1], scale=orstd[:, b:b + 1])
                ins.then_inc(y_ready, 1)

            normalise_mix(0)
            for c in range(CHUNKS):
                if c < CHUNKS - 1:
                    normalise_mix(c + 1)
                for i in range(2):
                    act.wait_ge(wyt_ready, 2 * c + i + 1)
                    act.activation(WYT[i].hi[:, :], bank[4 + i][:, :], ACT.Copy).then_inc(wyt_hi, 1)
            act.wait_ge(var_ready, 2)
            act.activation(std[:, :], var[:, :], ACT.Sqrt).then_inc(std_ready, 1)
            normalise_tiles(act, 1)
            for u in range(B // 2):
                split_turned("act", u, 1, (0, 1))

        @block.vector
        def _(dve):
            def norm_factors(at):
                for t in range(B):
                    ins = dve.bn_aggr(mv[:, 2 * t:2 * t + 2], stats[:, 6 * t:6 * t + 6])
                ins.then_inc(mv_ready, 1)
                dve.wait_ge(mv_ready, at + 1)
                dve.tensor_scalar(var[:, :], mv[:, :].rearrange("p (t s) -> p t s", s=2)[:, :, 1], LN_EPS, None,
                                  ALU.add).then_inc(var_ready, 1)
                dve.wait_ge(std_ready, at + 1)
                dve.reciprocal(rstd[:, :], std[:, :]).then_inc(rstd_ready, 1)

            dve.wait_ge(w_hi, 1)
            dve.tensor_tensor(Ws.lo[:, 0:2 * HH], small[:, 0:2 * HH], Ws.hi[:, 0:2 * HH].bitcast(F32), ALU.subtract
                              ).then_inc(w_lo, 1)
            norm_factors(0)
            dve.wait_ge(gram_hi, 1)
            dve.tensor_tensor(gram.lo[:, :], bank[4][:, 0:HH], gram.hi[:, :].bitcast(F32), ALU.subtract).then_inc(gram_lo, 1)
            dve.wait_ge(w_hi, 2)
            dve.tensor_tensor(Ws.lo[:, 2 * HH:], small[:, 2 * HH:], Ws.hi[:, 2 * HH:].bitcast(F32), ALU.subtract
                              ).then_inc(w_lo, 1)
            dve.wait_ge(rstd_ready, 1)
            normalise_tiles(dve, 0)
            for n in range(4 * CHUNKS):
                dve.wait_ge(kv_hi, n + 1)
                dve.tensor_tensor(kv_to(n).lo, bank[n % 4][:, :], kv_to(n).hi.bitcast(F32), ALU.subtract).then_inc(kv_lo, 1)
            for u in range(B // 2):
                split_turned("dve", u, 0, (4, 5))
            dve.wait_ge(sum_ready, 1)
            dve.wait_ge(const_in, 48)
            for h in range(XH):
                c = slice(h * S, (h + 1) * S)
                ins = dve.scalar_tensor_tensor(masked[:, c], bank[6 + h][:, 0:S], float(HD) ** -0.5, decay[:, c],
                                               ALU.mult, ALU.mult)
            ins.then_inc(masked_ready, 1)
            dve.wait_ge(masked_ready, 1)
            dve.scalar_tensor_tensor(positive[:, :], masked[:, :], -1.0, masked[:, :], ALU.mult, ALU.max
                                     ).then_inc(positive_ready, 1)
            dve.wait_ge(positive_ready, 1)
            dve.tensor_scalar(masked[:, :], positive[:, :], 1.0, None, ALU.max).then_inc(at32_ready, 1)
            dve.wait_ge(at_hi, 1)
            dve.tensor_tensor(AT.lo[:, :], masked[:, :], AT.hi[:, :].bitcast(F32), ALU.subtract).then_inc(at_lo, 1)

            def mix_factors(c):
                dve.wait_ge(o_ready, c + 1)
                if c:
                    dve.wait_ge(y_ready, c)
                for b in range(CB):
                    for h in range(XH):
                        ins = dve.bn_stats(ostats[:, b * 12 + h * 6:b * 12 + h * 6 + 6], bank[h][:, b * HD:(b + 1) * HD])
                ins.then_inc(ostats_ready, 1)
                dve.wait_ge(ostats_ready, c + 1)
                for b in range(CB):
                    ins = dve.bn_aggr(omv[:, 2 * b:2 * b + 2], ostats[:, 12 * b:12 * b + 12])
                ins.then_inc(omv_ready, 1)
                dve.wait_ge(omv_ready, c + 1)
                omv2 = omv[:, :].rearrange("p (t s) -> p t s", s=2)
                dve.tensor_scalar(ovar[:, :], omv2[:, :, 1], GN_EPS, None, ALU.add).then_inc(ovar_ready, 1)
                dve.wait_ge(ostd_ready, c + 1)
                dve.reciprocal(orstd[:, :], ostd[:, :]).then_inc(orstd_ready, 1)
                dve.wait_ge(orstd_ready, c + 1)
                dve.scalar_tensor_tensor(oshift[:, :], omv2[:, :, 0], -1.0, orstd[:, :], ALU.mult, ALU.mult
                                         ).then_inc(oshift_ready, 1)

            def gate_mix(c):
                dve.wait_ge(shifted_ready, c + 1)
                for i in range(2):
                    dve.wait_ge(gate_ready, 2 * c + i + 1)
                    if c:
                        dve.wait_ge(wyt_ready, 2 * (c - 1) + i + 1)
                    dve.scalar_tensor_tensor(WY[i][:, :], bank[2 + i][:, :], 0.0, Y[c % 2][:, i * 2 * D:(i + 1) * 2 * D],
                                             ALU.max, ALU.mult).then_inc(wy_ready, 1)

            mix_factors(0)
            for c in range(CHUNKS):
                if c < CHUNKS - 1:
                    mix_factors(c + 1)
                gate_mix(c)
                for i in range(2):
                    dve.wait_ge(wyt_hi, 2 * c + i + 1)
                    dve.tensor_tensor(WYT[i].lo[:, :], bank[4 + i][:, :], WYT[i].hi[:, :].bitcast(F32), ALU.subtract
                                      ).then_inc(wyt_lo, 1)
                for i in range(2):
                    t = c * CB + 2 * i
                    two = r[:, t * D:(t + 2) * D]
                    dve.wait_ge(out_ready, 2 * c + i + 1)
                    dve.tensor_tensor(two, bank[6 + i][:, :], two, ALU.add).then_inc(r_ready, 1)
                    dve.wait_ge(r_ready, 2 * c + i + 1)
                    for j in range(2):
                        ins = dve.bn_stats(stats[:, 6 * (t + j):6 * (t + j) + 6], tile(t + j))
                    ins.then_inc(stats_ready, 1)
            dve.wait_ge(stats_ready, 2 * CHUNKS)
            norm_factors(1)
            dve.wait_ge(rstd_ready, 2)
            dve.scalar_tensor_tensor(shift[:, :], mv[:, :].rearrange("p (t s) -> p t s", s=2)[:, :, 0], -1.0, rstd[:, :],
                                     ALU.mult, ALU.mult).then_inc(shift_ready, 1)
            normalise_tiles(dve, 1)
            for u in range(B // 2):
                split_turned("dve", u, 1, (0, 1))


FK = E
CT = 512
CHUNKS = B * S // CT
TT = CT // P
SI = 3


GUB = 3 * P
GU_AT = 0
QB_AT = GU_AT + DK * GUB
D1_AT = QB_AT + GUB
D2_AT = D1_AT + D
QA_AT = D2_AT + D
DQ_AT = QA_AT + DK * P
KR = F * R
MU_AT = DQ_AT + DK * KR
WCOLS = MU_AT + D
SCOLS = GUB + D
I2 = I - P
B2 = KR + I2
GROUPS = 2
GR = F // GROUPS * F
MR = 3 * GR


def load_weights(sp, a, e, stage, scale, done):
    sp.dma_start(stage[:, :], a["expert_w"][bass.ds(e, 1), :, :].rearrange("o p n -> p (o n)")).then_inc(done, 16)
    sp.dma_start(scale[:, :], a["expert_scale"][bass.ds(e, 1), :].to_broadcast([P, SCOLS])).then_inc(done, 16)


def scale_weights(pool, stage, scale, done, before):
    qb = slice(QB_AT, QB_AT + GUB)
    pool.tensor_tensor(stage[:, qb], stage[:, qb], scale[:, 0:GUB], ALU.mult).then_inc(done, 1)
    dn = slice(D2_AT, D2_AT + D)
    pool.wait_ge(done, before + 1)
    pool.tensor_tensor(stage[0:KR, dn], stage[0:KR, dn], scale[0:KR, GUB:], ALU.mult).then_inc(done, 1)


def split_low(pool, stage, w, low_done, all_done, count):
    pool.tensor_tensor(w.lo[:, :], stage[:, :], w.hi[:, :].bitcast(F32), ALU.subtract).then_inc(low_done, 1)
    pool.wait_ge(low_done, count)
    mu = (slice(2 * GR, MR), slice(MU_AT, WCOLS))
    pool.tensor_tensor(w.hi[mu], stage[mu], w.hi[mu].bitcast(F32), ALU.subtract).then_inc(all_done, 1)
    pool.wait_ge(all_done, count)


def route_and_share(nc, a, r, ident, xT, xT32, softT, share_of, soft_dram, stage, scale, W0):
    m = Memory(nc, "route")
    with m.ctx:
        NW = DK * E + 2 * DK * SI * P + SI * D
        w32 = m.sb("w32", NW)
        W = m.split("W", NW)
        Wr = W[:, 0:DK * E]
        at = DK * E
        Wg, Wu = W[:, at:at + DK * SI * P], W[:, at + DK * SI * P:at + 2 * DK * SI * P]
        Wd = W[:, at + 2 * DK * SI * P:]
        inv_raw = m.sb("inv_raw", FK, mybir.dt.int32, E)
        inv = m.sb("inv", FK, F32, E)
        rows = m.sb("rows", 1, F32, E)
        onehot = m.sb("onehot", FK, F32, E)
        EX = E + 2
        top1, mass, part = m.sb("top1", TT), m.sb("mass", TT), m.sb("part", TT)
        e1, soft1 = m.sb("e1", TT * E), m.sb("soft1", TT * EX)
        top8, rest = m.sb("top8", TT * 8), m.sb("rest", TT * EX)
        kept = m.sb("kept", TT * E)
        keptT = m.sb("keptT", CT, F32, E)
        unused, e2 = m.sb("unused", TT * FK), m.sb("e2", TT * FK)
        top2, mass2, part2 = m.sb("top2", TT * F), m.sb("mass2", TT * F), m.sb("part2", TT * F)
        soft2 = m.sb("soft2", TT * GROUPS * MR)
        softT32 = m.sb("softT32", GROUPS * CT, F32, GR)
        silu = [m.sb(f"silu{n}", CT) for n in range(2)]
        inner = [m.sb(f"inner{n}", CT) for n in range(2)]
        innerT = [[m.split(f"inner{n}_{k}", CT) for k in range(SI)] for n in range(2)]

        gate_bank = [m.bank(f"gate{n}") for n in range(2)]
        up_bank = [m.bank(f"up{n}") for n in range(2)]
        y_bank = [m.bank(f"y{n}") for n in range(2)]
        token_bank, turned_bank = m.bank("token"), m.bank("turned")
        soft_bank = [turned_bank, y_bank[1]]

        w_in, small_in, w_hi, w_lo = m.sem("w_in"), m.sem("small_in"), m.sem("w_hi"), m.sem("w_lo")
        inv_ready, onehot_ready, sentinels = m.sem("inv_ready"), m.sem("onehot_ready"), m.sem("sentinels")
        logit_ready, top1_ready, less1_ready, exp1_ready = (
            m.sem("logit_ready"), m.sem("top1_ready"), m.sem("less1_ready"), m.sem("exp1_ready"))
        mass1_ready, part1_ready, soft1_ready, top8_ready, rest_ready, kept_ready = (
            m.sem("mass1_ready"), m.sem("part1_ready"), m.sem("soft1_ready"), m.sem("top8_ready"),
            m.sem("rest_ready"), m.sem("kept_ready"))
        kept_turned, keptT_ready, flat_ready = m.sem("kept_turned"), m.sem("keptT_ready"), m.sem("flat_ready")
        unused_ready, masked_ready, top2_ready, less2_ready, exp2_ready, mass2_ready, part2_ready, soft2_ready = (
            m.sem("unused_ready"), m.sem("masked_ready"), m.sem("top2_ready"), m.sem("less2_ready"),
            m.sem("exp2_ready"), m.sem("mass2_ready"), m.sem("part2_ready"), m.sem("soft2_ready"))
        soft_turned, softT_hi, softT32_ready, softT_lo, stored = (
            m.sem("soft_turned"), m.sem("softT_hi"), m.sem("softT32_ready"), m.sem("softT_lo"), m.sem("stored"))
        up_ready, silu_ready, inner_ready, inner_hi, inner_lo = (
            m.sem("up_ready"), m.sem("silu_ready"), m.sem("inner_ready"), m.sem("inner_hi"), m.sem("inner_lo"))
        y_ready, r_ready, x32_ready = m.sem("y_ready"), m.sem("r_ready"), m.sem("x32_ready")
        expert_in, expert_scaled, expert_hi, expert_lo, expert_ready = (
            m.sem("expert_in"), m.sem("expert_scaled"), m.sem("expert_hi"), m.sem("expert_lo"), m.sem("expert_ready"))

        t3 = lambda t, w=E: t[:, :].rearrange("p (t e) -> p t e", t=TT, e=w) if t.shape[1] == TT * w else None
        wide = lambda t, n, w: t[:, :].rearrange("p (t o) -> p t o", o=1).to_broadcast([P, n, w])
        tok3 = token_bank[:, 0:TT * E].rearrange("p (t e) -> p t e", t=TT)
        tok8 = token_bank[:, 0:TT * FK].rearrange("p (t k) -> p t k", k=F)
        e2_8 = e2[:, :].rearrange("p (t k) -> p t k", k=F)
        s3 = soft1[:, :].rearrange("p (t e) -> p t e", t=TT)
        rest3 = rest[:, :].rearrange("p (t e) -> p t e", t=TT)

        block = m.ctx.enter_context(nc.Block())

        @block.sync
        def _(sp):
            sp.dma_start(w32[:, :], a["route_w"]).then_inc(w_in, 16)
            sp.dma_start(inv_raw[:, :], a["inv"].rearrange("(o e) -> o e", o=1).to_broadcast([E, FK])).then_inc(small_in, 16)
            sp.dma_start(rows[:, :], a["rows"]).then_inc(small_in, 16)
            load_weights(sp, a, 0, stage, scale, expert_in)
            by_parity = soft_dram.rearrange("(f two k) t -> two f k t", two=GROUPS, k=F)
            for c in range(CHUNKS):
                for n in range(GROUPS):
                    sp.wait_ge(softT32_ready, GROUPS * c + n + 1)
                    sp.dma_start(by_parity[n, :, :, c * CT:(c + 1) * CT], softT32[:, n * CT:(n + 1) * CT]).then_inc(stored, 16)
                if c == 2:
                    sp.wait_ge(expert_ready, 1)
                    load_weights(sp, a, 1, stage, scale, expert_in)
            sp.wait_ge(stored, 16 * GROUPS * CHUNKS)
            sp.wait_ge(expert_in, 64)

        @block.gpsimd
        def _(pool):
            for n in range(2 * CHUNKS):
                c = slice(n * CT, (n + 1) * CT)
                pool.tensor_tensor(xT32[:, c], xT.hi[:, c].bitcast(F32), xT.lo[:, c].bitcast(F32), ALU.add
                                   ).then_inc(x32_ready, 1)
                if n == 4:
                    pool.wait_ge(expert_in, 32)
                    scale_weights(pool, stage, scale, expert_scaled, 0)
                    pool.wait_ge(expert_scaled, 2)
                    pool.tensor_copy(W0.hi[:, :], stage[:, :]).then_inc(expert_hi, 1)
                    pool.wait_ge(expert_hi, 1)
                    split_low(pool, stage, W0, expert_lo, expert_ready, 1)
                if n % 2 == 1:
                    for k in range(SI):
                        u = n // 2 * SI + k
                        pool.wait_ge(inner_hi, u + 1)
                        pool.tensor_tensor(innerT[n // 2 % 2][k].lo[:, :], inner[u % 2][:, :],
                                           innerT[n // 2 % 2][k].hi[:, :].bitcast(F32), ALU.subtract).then_inc(inner_lo, 1)

        @block.tensor
        def _(pe):
            def shared_in(c, k):
                u = c * SI + k
                if u >= 2:
                    pe.wait_ge(inner_ready, u - 1)
                for W_, bank in ((Wg, gate_bank), (Wu, up_bank)):
                    for d in range(DK):
                        mm = product(pe, bank[u % 2][:, :], W_[:, (d * SI + k) * P:(d * SI + k + 1) * P],
                                     xT[:, d * B * S + c * CT:d * B * S + (c + 1) * CT], first=d == 0, last=d == DK - 1)
                mm.then_inc(up_ready, 1)

            def shared_out(c):
                pe.wait_ge(inner_lo, SI * (c + 1))
                for i in range(2):
                    if i:
                        pe.wait_ge(softT_lo, GROUPS * (c + 1))
                    if c:
                        pe.wait_ge(r_ready, 2 * (c - 1) + i + 1)
                    for j in range(2):
                        t = 2 * i + j
                        for k in range(SI):
                            mm = product(pe, y_bank[i][:, j * D:(j + 1) * D], innerT[c % 2][k][:, t * P:(t + 1) * P],
                                         Wd[:, k * D:(k + 1) * D], first=k == 0, last=k == SI - 1)
                    mm.then_inc(y_ready, 1)

            def soft_out(c, n):
                if n and c:
                    pe.wait_ge(r_ready, 2 * c)
                bank = soft_bank[n]
                if n == 0:
                    pe.wait_ge(soft2_ready, c + 1)
                for t in range(TT):
                    at = (t * GROUPS + n) * MR
                    mm = pe.transpose(bank[0:MR, t * P:(t + 1) * P], soft2[:, at:at + MR], ident[:, :])
                mm.then_inc(soft_turned, 1)

            pe.wait_ge(w_lo, 1)
            for c in range(CHUNKS):
                if c:
                    pe.wait_ge(masked_ready, c)
                for t in range(TT):
                    for d in range(DK):
                        at = d * B * S + c * CT + t * P
                        mm = product(pe, token_bank[:, t * E:(t + 1) * E], xT[:, at:at + P], Wr[:, d * E:(d + 1) * E],
                                     first=d == 0, last=d == DK - 1)
                mm.then_inc(logit_ready, 1)
                shared_in(c, 0)
                if c:
                    for n in range(GROUPS):
                        soft_out(c - 1, n)
                shared_in(c, 1)
                pe.wait_ge(kept_ready, c + 1)
                if c:
                    pe.wait_ge(softT_lo, GROUPS * c - 1)
                for t in range(TT):
                    mm = pe.transpose(turned_bank[0:E, t * P:(t + 1) * P], kept[:, t * E:(t + 1) * E], ident[:, :])
                mm.then_inc(kept_turned, 1)
                shared_in(c, 2)
                pe.wait_ge(keptT_ready, c + 1)
                pe.wait_ge(onehot_ready, 1)
                for t in range(TT):
                    mm = pe.matmul(token_bank[:, t * FK:(t + 1) * FK], keptT[:, t * P:(t + 1) * P], onehot[:, :],
                                   start=True, stop=True)
                mm.then_inc(flat_ready, 1)
                if c:
                    shared_out(c - 1)
            for n in range(GROUPS):
                soft_out(CHUNKS - 1, n)
            shared_out(CHUNKS - 1)

        @block.scalar
        def _(act):
            act.wait_ge(w_in, 16)
            act.activation(W.hi[:, :], w32[:, :], ACT.Copy).then_inc(w_hi, 1)

            def shared(c, k):
                u = c * SI + k
                act.wait_ge(up_ready, u + 1)
                if u >= 2:
                    act.wait_ge(inner_ready, u - 1)
                act.activation(silu[u % 2][:, :], gate_bank[u % 2][:, :], ACT.Silu).then_inc(silu_ready, 1)
                act.wait_ge(inner_ready, u + 1)
                if c >= 2:
                    act.wait_ge(y_ready, 2 * (c - 1))
                act.activation(innerT[c % 2][k].hi[:, :], inner[u % 2][:, :], ACT.Copy).then_inc(inner_hi, 1)

            def soft_high(c):
                for n in range(GROUPS):
                    act.wait_ge(soft_turned, GROUPS * c + n + 1)
                    act.activation(softT[n][0:MR, c * CT:(c + 1) * CT], soft_bank[n][0:MR, :], ACT.Copy).then_inc(softT_hi, 1)

            for c in range(CHUNKS):
                act.wait_ge(less1_ready, c + 1)
                act.activation(e1[:, :], e1[:, :], ACT.Exp).then_inc(exp1_ready, 1)
                for k in range(SI):
                    shared(c, k)
                    if k == 0 and c:
                        soft_high(c - 1)
                act.wait_ge(less2_ready, c + 1)
                act.activation(e2[:, :], e2[:, :], ACT.Exp).then_inc(exp2_ready, 1)
            soft_high(CHUNKS - 1)

        @block.vector
        def _(dve):
            dve.wait_ge(w_hi, 1)
            dve.tensor_tensor(W.lo[:, :], w32[:, :], W.hi[:, :].bitcast(F32), ALU.subtract).then_inc(w_lo, 1)
            dve.wait_ge(small_in, 32)
            dve.tensor_copy(inv[:, :], inv_raw[:, :]).then_inc(inv_ready, 1)
            dve.wait_ge(inv_ready, 1)
            dve.tensor_scalar(onehot[:, :], inv[:, :], rows[:, 0:1], None, ALU.is_equal).then_inc(onehot_ready, 1)
            dve.memset(s3[:, :, E:E + 1], 3.0).then_inc(sentinels, 1)
            dve.memset(s3[:, :, E + 1:E + 2], 2.0).then_inc(sentinels, 1)
            dve.wait_ge(sentinels, 2)

            def shared(c, k):
                u = c * SI + k
                dve.wait_ge(silu_ready, u + 1)
                if u >= 2:
                    dve.wait_ge(inner_lo, u - 1)
                dve.tensor_tensor(inner[u % 2][:, :], up_bank[u % 2][:, :], silu[u % 2][:, :], ALU.mult).then_inc(inner_ready, 1)

            def shared_out(c):
                for i in range(2):
                    t = c * TT + 2 * i
                    dve.wait_ge(y_ready, 2 * c + i + 1)
                    two = r[:, t * D:(t + 2) * D]
                    dve.tensor_tensor(two, y_bank[i][:, :], two, ALU.add).then_inc(r_ready, 1)

            def split_soft(c):
                for n in range(GROUPS):
                    dve.wait_ge(softT_hi, GROUPS * c + n + 1)
                    if c:
                        dve.wait_ge(stored, 16 * GROUPS * c)
                    dve.tensor_copy(softT32[:, n * CT:(n + 1) * CT], soft_bank[n][0:GR, :]).then_inc(softT32_ready, 1)
                    at = (slice(GR, 2 * GR), slice(c * CT, (c + 1) * CT))
                    dve.tensor_tensor(softT[n][at], soft_bank[n][GR:2 * GR, :], softT[n][at].bitcast(F32), ALU.subtract
                                      ).then_inc(softT_lo, 1)

            for c in range(CHUNKS):
                n = c + 1
                dve.wait_ge(logit_ready, n)
                dve.tensor_reduce(top1[:, :], tok3, AX.X, ALU.max).then_inc(top1_ready, 1)
                dve.wait_ge(top1_ready, n)
                dve.tensor_tensor(e1[:, :].rearrange("p (t e) -> p t e", t=TT), tok3, wide(top1, TT, E), ALU.subtract
                                  ).then_inc(less1_ready, 1)
                dve.wait_ge(exp1_ready, n)
                e13 = e1[:, :].rearrange("p (t e) -> p t e", t=TT)
                dve.tensor_reduce(mass[:, :], e13, AX.X, ALU.add).then_inc(mass1_ready, 1)
                dve.wait_ge(mass1_ready, n)
                dve.reciprocal(part[:, :], mass[:, :]).then_inc(part1_ready, 1)
                dve.wait_ge(part1_ready, n)
                dve.tensor_tensor(s3[:, :, 0:E], e13, wide(part, TT, E), ALU.mult).then_inc(soft1_ready, 1)
                dve.wait_ge(soft1_ready, n)
                for t in range(TT):
                    ins = dve.max(top8[:, t * 8:(t + 1) * 8], soft1[:, t * EX:(t + 1) * EX])
                ins.then_inc(top8_ready, 1)
                dve.wait_ge(top8_ready, n)
                for t in range(TT):
                    ins = dve.match_replace(rest[:, t * EX:(t + 1) * EX], top8[:, t * 8:(t + 1) * 8],
                                            soft1[:, t * EX:(t + 1) * EX], 0.0)
                ins.then_inc(rest_ready, 1)
                dve.wait_ge(rest_ready, n)
                dve.tensor_tensor(kept[:, :].rearrange("p (t e) -> p t e", t=TT), s3[:, :, 0:E], rest3[:, :, 0:E],
                                  ALU.subtract).then_inc(kept_ready, 1)
                shared(c, 0)
                if c:
                    split_soft(c - 1)
                shared(c, 1)
                dve.wait_ge(kept_turned, n)
                dve.tensor_copy(keptT[:, :], turned_bank[0:E, :]).then_inc(keptT_ready, 1)
                shared(c, 2)
                dve.wait_ge(flat_ready, n)
                dve.tensor_reduce(share_of[:, c * TT * F:(c + 1) * TT * F], tok8, AX.X, ALU.add)
                dve.tensor_scalar(unused[:, :], token_bank[:, 0:TT * FK], 0.0, -1e9, ALU.is_equal, ALU.mult
                                  ).then_inc(unused_ready, 1)
                dve.wait_ge(unused_ready, n)
                dve.tensor_tensor(e2[:, :], token_bank[:, 0:TT * FK], unused[:, :], ALU.add).then_inc(masked_ready, 1)
                dve.wait_ge(masked_ready, n)
                dve.tensor_reduce(top2[:, :], e2_8, AX.X, ALU.max).then_inc(top2_ready, 1)
                dve.wait_ge(top2_ready, n)
                dve.tensor_tensor(e2_8, e2_8, wide(top2, TT * F, F), ALU.subtract).then_inc(less2_ready, 1)
                dve.wait_ge(exp2_ready, n)
                dve.tensor_reduce(mass2[:, :], e2_8, AX.X, ALU.add).then_inc(mass2_ready, 1)
                dve.wait_ge(mass2_ready, n)
                dve.reciprocal(part2[:, :], mass2[:, :]).then_inc(part2_ready, 1)
                dve.wait_ge(part2_ready, n)
                four = lambda t: t.rearrange("p (t f k) -> p t f k", t=TT * GROUPS, f=F // GROUPS)
                if c:
                    dve.wait_ge(soft_turned, GROUPS * c)
                for copy in range(3):
                    to = soft2[:, :].rearrange("p (t n c) -> p n t c", t=TT * GROUPS, n=3)[:, copy]
                    ins = dve.tensor_tensor(to.rearrange("p t (f k) -> p t f k", k=F), four(e2[:, :]),
                                            four(part2[:, :]).to_broadcast([P, TT * GROUPS, F // GROUPS, F]), ALU.mult)
                ins.then_inc(soft2_ready, 1)
                if c:
                    shared_out(c - 1)
            split_soft(CHUNKS - 1)
            shared_out(CHUNKS - 1)


def experts(nc, a, r, xT, xT32, softT, share_of, soft_dram, stage, scale, W0):
    m = Memory(nc, "moe")
    UNITS = 2 * CHUNKS
    with m.ctx:
        W = [W0, m.split("W1", WCOLS)]
        xe32 = m.sb("xe32", DK * CT)
        place = lambda part, n: part[:, n * 2 * CT:(n + 1) * 2 * CT]
        xe = [Split(place(xT.hi, 2 * n), place(xT.hi, 2 * n + 1)) for n in range(2)]
        spread = [m.sb(f"spread{c}", CT) for c in range(CHUNKS)]
        low32 = m.sb("low32", CT)
        low = m.split("low", CT)
        silu, inner = m.sb("silu", 2 * CT), m.sb("inner", 2 * CT)
        innerT = [Split(place(xT.lo, 2 * n), place(xT.lo, 2 * n + 1)) for n in range(2)]
        dlow32 = m.sb("dlow32", CT, parts=KR)
        shares = m.sb("shares", 2 * B)

        gu = [m.bank(f"gu{n}") for n in range(3)]
        dlow_bank, low_bank, xe_bank = m.bank("dlow"), m.bank("low"), m.bank("xe")
        y_bank = [m.bank(f"y{n}") for n in range(2)]
        feat = [xe_bank, dlow_bank]

        w_in, w_scaled, w_hi, w_lo, w_ready = (
            m.sem("w_in"), m.sem("w_scaled"), m.sem("w_hi"), m.sem("w_lo"), m.sem("w_ready"))
        spread_in = [m.sem(f"spread_in{c}") for c in range(CHUNKS)]
        xe_ready, xe32_ready, xe_hi, xe_lo = m.sem("xe_ready"), m.sem("xe32_ready"), m.sem("xe_hi"), m.sem("xe_lo")
        low_ready, low32_ready, low_hi, low_lo = m.sem("low_ready"), m.sem("low32_ready"), m.sem("low_hi"), m.sem("low_lo")
        gu_ready, silu_ready, inner_ready = m.sem("gu_ready"), m.sem("silu_ready"), m.sem("inner_ready")
        inner_hi, inner_lo = m.sem("inner_hi"), m.sem("inner_lo")
        dlow_ready, dlow32_ready, dlow_hi, dlow_lo = (
            m.sem("dlow_ready"), m.sem("dlow32_ready"), m.sem("dlow_hi"), m.sem("dlow_lo"))
        y_ready, r_ready, shares_ready = m.sem("y_ready"), m.sem("r_ready"), m.sem("shares_ready")

        TURNS_E = F // 2
        LAST = TURNS_E - 1
        FEATURES = ((slice(0, P), slice(0, CT)), (slice(KR, B2), slice(CT, 2 * CT)))
        block = m.ctx.enter_context(nc.Block())

        def count(g, u):
            return g * UNITS + u

        @block.sync
        def _(sp):
            def load_spread(e, c):
                for half in range(2):
                    sp.dma_start(spread[c][half * KR:(half + 1) * KR, :],
                                 soft_dram[bass.ds(e * F, F), c * CT:(c + 1) * CT].rearrange("(k o) t -> k o t", o=1)
                                 .to_broadcast([F, R, CT])).then_inc(spread_in[c], 16)

            for c in range(CHUNKS):
                load_spread(0, c)

            def turn(g, last):
                for u in range(CHUNKS if last else UNITS):
                    sp.wait_ge(dlow32_ready, count(g, u + 1))
                    load_spread(g * 2 + u // CHUNKS + 1, u % CHUNKS)
                    if u in (0, CHUNKS) and not last:
                        e = g * 2 + 2 + u // CHUNKS
                        sp.wait_ge(w_ready, e - 1)
                        load_weights(sp, a, e, stage, scale, w_in)

            with sp.Fori(0, LAST) as g:
                turn(g, False)
            turn(LAST, True)

        @block.gpsimd
        def _(pool):
            def scale_next(e, first=False):
                if not first:
                    pool.wait_ge(w_in, e * 32 - 32)
                scale_weights(pool, stage, scale, w_scaled, e * 2 - 2)

            def split_weights(n, e):
                pool.wait_ge(w_hi, e)
                split_low(pool, stage, W[n], w_lo, w_ready, e)

            def xe_low(g, u):
                pool.wait_ge(xe_hi, count(g, u + 1))
                pool.tensor_tensor(xe[u % 2].lo[:, :], xe32[:, :], xe[u % 2].hi[:, :].bitcast(F32), ALU.subtract
                                   ).then_inc(xe_lo, 1)

            def inner_low(g, u, k):
                pool.wait_ge(inner_hi, 2 * count(g, u) + k + 1)
                at = FEATURES[k]
                if k:
                    pool.wait_ge(inner_lo, 2 * count(g, u) + 1)
                pool.tensor_tensor(innerT[u % 2].lo[at], inner[at], innerT[u % 2].hi[at].bitcast(F32), ALU.subtract
                                   ).then_inc(inner_lo, 1)

            scale_next(1, True)
            pool.wait_ge(w_scaled, 2)
            xe_low(0, 1)

            def turn(g, first, last):
                for u in range(UNITS):
                    for k in range(2):
                        inner_low(g, u, k)
                    pool.wait_ge(inner_lo, 2 * count(g, u + 1))
                    if not (last and u >= UNITS - 2):
                        xe_low(g, u + 2)
                    if u == 0:
                        split_weights(1, g * 2 + 1)
                    if u == CHUNKS and not last:
                        split_weights(0, g * 2 + 2)
                    if u in (CHUNKS - 1, UNITS - 1) and not last:
                        e = g * 2 + 2 + u // CHUNKS
                        scale_next(e)
                        pool.wait_ge(w_scaled, e * 2)

            turn(0, True, False)
            with pool.Fori(1, LAST) as g:
                turn(g, False, False)
            turn(LAST, False, True)

        @block.tensor
        def _(pe):
            def inputs(g, u, slot):
                c = u % CHUNKS
                for k in range(DK):
                    pe.matmul(feat[k][:, :], W[slot].hi[0:MR, MU_AT + k * P:MU_AT + (k + 1) * P],
                              softT[slot][0:MR, c * CT:(c + 1) * CT], start=True, stop=True
                              ).then_inc(xe_ready, 1)

            def low_rank(g, u, slot):
                for k in range(DK):
                    mm = product(pe, low_bank[:, :], W[slot][:, QA_AT + k * P:QA_AT + (k + 1) * P],
                                 xe[u % 2][:, k * CT:(k + 1) * CT], first=k == 0, last=k == DK - 1)
                mm.then_inc(low_ready, 1)

            def gate_up(g, u, slot, first):
                w, x = W[slot], xe[u % 2]
                for n, rows in ((0, P), (1, P), (2, B2)):
                    if not first:
                        pe.wait_ge(inner_ready, 2 * count(g, u) - (n < 2))
                    for k in range(DK):
                        at = GU_AT + k * GUB + n * P
                        product(pe, gu[n][0:rows, :], w[:, at:at + rows], x[:, k * CT:(k + 1) * CT], first=k == 0, last=False)
                    if n == 0:
                        pe.wait_ge(low_lo, count(g, u + 1))
                    at = QB_AT + n * P
                    product(pe, gu[n][0:rows, :], w[:, at:at + rows], low[:, :], first=False).then_inc(gu_ready, 1)

            def down_low(g, u, slot):
                pe.wait_ge(inner_lo, 2 * count(g, u + 1))
                w, x = W[slot], innerT[u % 2]
                product(pe, dlow_bank[0:KR, :], w[:, DQ_AT:DQ_AT + KR], x[:, 0:CT], last=False)
                product(pe, dlow_bank[0:KR, :], w[KR:B2, DQ_AT + KR:DQ_AT + 2 * KR], x[KR:B2, CT:2 * CT],
                        first=False).then_inc(dlow_ready, 1)

            def down(g, u, slot, first):
                for k, at, rows in ((0, D1_AT, P), (1, D2_AT, B2)):
                    if k:
                        pe.wait_ge(dlow_lo, count(g, u + 1))
                    for i in range(2):
                        if not first and k == 0:
                            pe.wait_ge(r_ready, 4 * count(g, u) - 2 + 2 * i)
                        for j in range(2):
                            t = 2 * i + j
                            mm = product(pe, y_bank[i][:, j * D:(j + 1) * D],
                                         innerT[u % 2][0:rows, k * CT + t * P:k * CT + (t + 1) * P],
                                         W[slot][0:rows, at:at + D], first=k == 0 and j == 0, last=k == 1,
                                         skip_group_check=True)
                        if k:
                            mm.then_inc(y_ready, 1)

            def turn(g, first, last):
                for u in range(UNITS):
                    before = not (first and u == 0)
                    gate_up(g, u, u // CHUNKS, not before)
                    if before:
                        pe.wait_ge(xe32_ready, 2 * count(g, u + (1 if last and u == UNITS - 1 else 2)))
                        down_low(g, u - 1, (u - 1) // CHUNKS % 2)
                    if not (last and u == UNITS - 1):
                        pe.wait_ge(xe_lo, count(g, u + 2))
                        low_rank(g, u + 1, (u + 1) // CHUNKS % 2)
                    if not (last and u >= UNITS - 2):
                        if u in (2, CHUNKS + 2):
                            pe.wait_ge(w_ready, g * 2 + (1 if u == 2 else 2))
                        if before:
                            pe.wait_ge(dlow32_ready, count(g, u))
                        inputs(g, u + 2, (u + 2) // CHUNKS % 2)
                    if before:
                        down(g, u - 1, (u - 1) // CHUNKS % 2, first and u == 1)

            inputs(0, 0, 0)
            pe.wait_ge(xe32_ready, 2)
            inputs(0, 1, 0)
            pe.wait_ge(xe_lo, 1)
            low_rank(0, 0, 0)
            pe.wait_ge(low32_ready, 1)
            turn(0, True, False)
            with pe.Fori(1, LAST) as g:
                turn(g, False, False)
            turn(LAST, False, True)
            down_low(LAST, UNITS - 1, 1)
            down(LAST, UNITS - 1, 1, False)

        @block.scalar
        def _(act):
            def xe_high(g, u):
                act.wait_ge(xe32_ready, 2 * count(g, u + 1))
                act.activation(xe[u % 2].hi[:, :], xe32[:, :], ACT.Copy).then_inc(xe_hi, 1)

            def low_high(g, u):
                act.wait_ge(low32_ready, count(g, u + 1))
                act.activation(low.hi[:, :], low32[:, :], ACT.Copy).then_inc(low_hi, 1)

            def dlow_high(g, u):
                act.wait_ge(dlow32_ready, count(g, u + 1))
                act.activation(innerT[u % 2].hi[0:KR, CT:2 * CT], dlow32[:, :], ACT.Copy).then_inc(dlow_hi, 1)

            def weights_high(n, e, first=False):
                act.wait_ge(w_scaled, e * 2)
                if not first:
                    act.wait_ge(y_ready, 2 * CHUNKS * (e - 1))
                act.activation(W[n].hi[:, :], stage[:, :], ACT.Copy).then_inc(w_hi, 1)

            xe_high(0, 0)
            xe_high(0, 1)
            low_high(0, 0)

            def turn(g, first, last):
                for u in range(UNITS):
                    for k, n in ((0, 0), (1, 2)):
                        rows, cols = FEATURES[k]
                        act.wait_ge(gu_ready, 3 * count(g, u) + n + 1)
                        act.activation(silu[rows, cols], gu[n][rows, :], ACT.Silu).then_inc(silu_ready, 1)
                        act.wait_ge(inner_ready, 2 * count(g, u) + k + 1)
                        if k == 0 and not (first and u < 2):
                            act.wait_ge(y_ready, 2 * count(g, u - 1))
                        act.activation(innerT[u % 2].hi[rows, cols], inner[rows, cols], ACT.Copy).then_inc(inner_hi, 1)
                    if not (first and u == 0):
                        dlow_high(g, u - 1)
                    if not (last and u == UNITS - 1):
                        low_high(g, u + 1)
                    if not (last and u >= UNITS - 2):
                        xe_high(g, u + 2)
                    if u == CHUNKS and not last:
                        weights_high(0, g * 2 + 2)
                    if u == 0:
                        weights_high(1, g * 2 + 1, first)

            turn(0, True, False)
            with act.Fori(1, LAST) as g:
                turn(g, False, False)
            turn(LAST, False, True)
            dlow_high(LAST, UNITS - 1)

        @block.vector
        def _(dve):
            def xe_sum(g, u):
                c = u % CHUNKS
                for k in range(DK):
                    dve.wait_ge(xe_ready, 2 * count(g, u) + k + 1)
                    dve.tensor_tensor(xe32[:, k * CT:(k + 1) * CT], feat[k][:, :],
                                      xT32[:, k * B * S + c * CT:k * B * S + (c + 1) * CT], ALU.add).then_inc(xe32_ready, 1)

            def low_product(g, u):
                c = u % CHUNKS
                dve.wait_ge(low_ready, count(g, u + 1))
                dve.wait_ge(spread_in[c], (g * 2 + u // CHUNKS) * 32 + 32)
                dve.tensor_tensor(low32[:, :], low_bank[:, :], spread[c][:, :], ALU.mult).then_inc(low32_ready, 1)

            def low_low(g, u):
                dve.wait_ge(low_hi, count(g, u + 1))
                dve.tensor_tensor(low.lo[:, :], low32[:, :], low.hi[:, :].bitcast(F32), ALU.subtract).then_inc(low_lo, 1)

            def dlow_product(g, u):
                c = u % CHUNKS
                dve.wait_ge(dlow_ready, count(g, u + 1))
                dve.tensor_tensor(dlow32[:, :], dlow_bank[0:KR, :], spread[c][0:KR, :], ALU.mult).then_inc(dlow32_ready, 1)

            def dlow_low(g, u):
                dve.wait_ge(dlow_hi, count(g, u + 1))
                at = (slice(0, KR), slice(CT, 2 * CT))
                dve.tensor_tensor(innerT[u % 2].lo[at], dlow32[:, :], innerT[u % 2].hi[at].bitcast(F32), ALU.subtract
                                  ).then_inc(dlow_lo, 1)

            def inner_product(g, u, k, first):
                rows, cols = FEATURES[k]
                dve.wait_ge(silu_ready, 2 * count(g, u) + k + 1)
                if k == 0:
                    dve.wait_ge(gu_ready, 3 * count(g, u) + 2)
                if not first:
                    dve.wait_ge(inner_lo, 2 * count(g, u) - 1 + k)
                up = gu[1][:, :] if k == 0 else gu[2][0:I2, :]
                dve.tensor_tensor(inner[rows, cols], up, silu[rows, cols], ALU.mult).then_inc(inner_ready, 1)

            def add_output(g, u):
                e, c = u // CHUNKS % 2, u % CHUNKS
                for t in range(TT):
                    if t % 2 == 0:
                        dve.wait_ge(y_ready, 2 * count(g, u) + t // 2 + 1)
                    at = c * TT + t
                    here = r[:, at * D:(at + 1) * D]
                    dve.scalar_tensor_tensor(here, y_bank[t // 2][:, t % 2 * D:(t % 2 + 1) * D],
                                             shares[:, e * B + at:e * B + at + 1], here, ALU.mult, ALU.add
                                             ).then_inc(r_ready, 1)

            xe_sum(0, 0)
            dve.wait_ge(xe_hi, 1)
            dve.tensor_tensor(xe[0].lo[:, :], xe32[:, :], xe[0].hi[:, :].bitcast(F32), ALU.subtract).then_inc(xe_lo, 1)
            dve.wait_ge(xe_lo, 1)
            xe_sum(0, 1)
            low_product(0, 0)
            low_low(0, 0)

            def turn(g, first, last):
                for u in range(UNITS):
                    if not (first and u < 2):
                        add_output(g, u - 2)
                    if u == 1:
                        if not first:
                            dve.wait_ge(r_ready, 4 * count(g, 0))
                        dve.tensor_copy(shares[:, :].rearrange("p (e t) -> p e t", e=2),
                                        share_of[:, :].rearrange("p (t n e) -> p e n t", t=B, n=GROUPS)[:, bass.ds(g, 1)].rearrange("p o n t -> p (o n) t")
                                        ).then_inc(shares_ready, 1)
                        dve.wait_ge(shares_ready, g + 1)
                    inner_product(g, u, 0, first and u == 0)
                    inner_product(g, u, 1, first and u == 0)
                    if not (first and u == 0):
                        dlow_product(g, u - 1)
                        dlow_low(g, u - 1)
                    if not (last and u == UNITS - 1):
                        low_product(g, u + 1)
                    if not (last and u >= UNITS - 2):
                        dve.wait_ge(xe_lo, count(g, u + 2))
                        xe_sum(g, u + 2)
                    if not (last and u == UNITS - 1):
                        low_low(g, u + 1)

            turn(0, True, False)
            with dve.Fori(1, LAST) as g:
                turn(g, False, False)
            turn(LAST, False, True)
            add_output(LAST, UNITS - 2)
            dlow_product(LAST, UNITS - 1)
            dlow_low(LAST, UNITS - 1)
            add_output(LAST, UNITS - 1)


def last_norm(nc, a, r):
    m = Memory(nc, "norm")
    with m.ctx:
        stats, mv = m.sb("stats", 6 * B), m.sb("mv", 2 * B)
        var, std, rstd = m.sb("var", B), m.sb("std", B), m.sb("rstd", B)
        stats_ready, mv_ready, var_ready, std_ready, rstd_ready = (
            m.sem("stats_ready"), m.sem("mv_ready"), m.sem("var_ready"), m.sem("std_ready"), m.sem("rstd_ready"))
        by_dve, by_pool, stored = m.sem("by_dve"), m.sem("by_pool"), m.sem("stored")
        out = a["out"].rearrange("b s d -> s b d")
        block = m.ctx.enter_context(nc.Block())

        def normalise(eng, t):
            here = r[:, t * D:(t + 1) * D]
            return eng.tensor_scalar(here, here, mv[:, 2 * t:2 * t + 1], rstd[:, t:t + 1], ALU.subtract, ALU.mult)

        @block.vector
        def _(dve):
            for t in range(B):
                ins = dve.bn_stats(stats[:, 6 * t:6 * t + 6], r[:, t * D:(t + 1) * D])
            ins.then_inc(stats_ready, 1)
            dve.wait_ge(stats_ready, 1)
            for t in range(B):
                ins = dve.bn_aggr(mv[:, 2 * t:2 * t + 2], stats[:, 6 * t:6 * t + 6])
            ins.then_inc(mv_ready, 1)
            dve.wait_ge(mv_ready, 1)
            dve.tensor_scalar(var[:, :], mv[:, :].rearrange("p (t s) -> p t s", s=2)[:, :, 1], LN_EPS, None, ALU.add
                              ).then_inc(var_ready, 1)
            dve.wait_ge(std_ready, 1)
            dve.reciprocal(rstd[:, :], std[:, :]).then_inc(rstd_ready, 1)
            dve.wait_ge(rstd_ready, 1)
            for t in range(0, B, 2):
                normalise(dve, t).then_inc(by_dve, 1)

        @block.gpsimd
        def _(pool):
            pool.wait_ge(rstd_ready, 1)
            for t in range(1, B, 2):
                normalise(pool, t).then_inc(by_pool, 1)

        @block.scalar
        def _(act):
            act.wait_ge(var_ready, 1)
            act.activation(std[:, :], var[:, :], ACT.Sqrt).then_inc(std_ready, 1)

        @block.sync
        def _(sp):
            for c in range(4):
                sp.wait_ge(by_dve, 2 * c + 2)
                sp.wait_ge(by_pool, 2 * c + 2)
                sp.dma_start(out[:, 4 * c:4 * c + 4, :], r[:, 4 * c * D:4 * (c + 1) * D].rearrange("p (b d) -> p b d", b=4)
                             ).then_inc(stored, 16)
            sp.wait_ge(stored, 64)


def program(nc, a):
    m = Memory(nc, "all")
    with m.ctx:
        r = m.sb("r", B * D)
        stats = m.sb("stats", B * 6)
        ident = m.sb("ident", P)
        self_attention(nc, a, r, stats, ident)
        soft_dram = nc.dram_tensor("soft_dram", [FK, B * S], F32, kind="Internal").ap()
        xT = m.split("xT", DK * B * S)
        cross_attention(nc, a, r, stats, ident, xT)
        share_of = m.sb("share_of", B * F)
        softT = [m.sb(f"softT{n}", B * S, F32R, MR) for n in range(GROUPS)]
        xT32 = m.sb("xT32", DK * B * S)
        stage, scale = m.sb("stage", WCOLS), m.sb("scale", SCOLS)
        W0 = m.split("W0", WCOLS)
        route_and_share(nc, a, r, ident, xT, xT32, softT, share_of, soft_dram, stage, scale, W0)
        experts(nc, a, r, xT, xT32, softT, share_of, soft_dram, stage, scale, W0)
        last_norm(nc, a, r)


def decay_mask(np):
    gam = (1.0 - 2.0 ** (-5.0 - np.arange(XH, dtype=np.float32))).astype(np.float32)
    at = np.arange(S, dtype=np.float32)
    expo = at[None, :] - at[:, None]
    D_ = np.where(expo[None] <= 0, gam[:, None, None] ** expo[None], np.float32(0)).astype(np.float32)
    D_ = D_ / np.sqrt(D_.sum(-1))[:, None, :]
    return D_.transpose(2, 0, 1).reshape(S, XH * S).astype(np.float32)


def layout(np, v):
    T = B * S

    def rows(w, n=P):
        return w.reshape(-1, n, w.shape[1]).transpose(1, 0, 2).reshape(n, -1)

    def padded(w, shape):
        out = np.zeros(shape, w.dtype)
        out[tuple(slice(0, n) for n in w.shape)] = w
        return out

    ffn = lambda name: v["L0_ffn_" + name]
    Wh = v["L0_xattn_Wh"]
    out = {
        "x_tok": v["x"].transpose(1, 0, 2).reshape(S, B * D),
        "xT": v["x"].reshape(T, DK, P).transpose(2, 1, 0),
        "Wq": v["L0_attn_Wq"].reshape(DK, P, KV, G * DH).transpose(1, 2, 0, 3).reshape(P, -1),
        "Wk": rows(v["L0_attn_Wk"]), "Wv": rows(v["L0_attn_Wv"]), "Wo": rows(v["L0_attn_Wo"]),
        "bq": v["L0_attn_bq"].reshape(H, DH).T, "bk": v["L0_attn_bk"].reshape(KV, DH).T,
        "bv": v["L0_attn_bv"].reshape(KV, DH).T, "bo": v["L0_attn_bo"],
        "ident": np.eye(P, dtype=np.float32),
        "cross_w": np.concatenate([Wh.transpose(1, 0, 2).reshape(HD, -1), Wh.transpose(2, 0, 1).reshape(HD, -1),
                                   rows(v["L0_xattn_wg_w"]), rows(v["L0_xattn_wo_w"])], 1),
        "ctxT": v["ctx_2048"].reshape(T, XH, HD).transpose(2, 1, 0),
        "gamma": v["L0_xattn_gn_gamma"], "beta": v["L0_xattn_gn_beta"], "decay": decay_mask(np),
        "route_w": np.concatenate([rows(ffn("gate_weight").T), rows(padded(ffn("sh_gate_W").T, (D, SI * P))),
                                   rows(padded(ffn("sh_up_W").T, (D, SI * P))),
                                   rows(padded(ffn("sh_down_W").T, (SI * P, D)))], 1),
        "inv": ffn("inv_mapping").reshape(F // GROUPS, GROUPS, F).transpose(1, 0, 2).reshape(-1),
        "rows": np.arange(E, dtype=np.float32).reshape(E, 1),
    }

    def blocks(gate, up):
        w = np.zeros(gate.shape[:-1] + (GUB,), gate.dtype)
        w[..., :P], w[..., P:2 * P] = gate[..., :P], up[..., :P]
        w[..., 2 * P:2 * P + I2], w[..., 2 * P + KR:2 * P + B2] = up[..., P:], gate[..., P:]
        return w

    out["expert_scale"] = np.concatenate([blocks(ffn("gate_scale"), ffn("up_scale")), ffn("down_scale")], 1)
    W = np.zeros((F, P, WCOLS), np.float32)
    for f in range(F):
        w = W[f]
        w[:, GU_AT:QB_AT] = rows(blocks(ffn("gate_W")[f].T, ffn("up_W")[f].T))
        gate_qb, up_qb = (ffn(n)[f].transpose(0, 2, 1).reshape(KR, I) for n in ("gate_qb", "up_qb"))
        none = np.zeros_like(gate_qb)
        w[:KR, QB_AT:D1_AT], w[KR:, QB_AT:D1_AT] = blocks(gate_qb, none), blocks(none, up_qb)
        w[:, D1_AT:D2_AT] = ffn("down_W")[f].T[:P]
        w[:KR, D2_AT:QA_AT] = ffn("down_qb")[f].transpose(0, 2, 1).reshape(KR, D)
        w[KR:B2, D2_AT:QA_AT] = ffn("down_W")[f].T[P:]
        w[:, QA_AT:DQ_AT] = rows(np.concatenate([ffn("gate_qa")[f].reshape(KR, D).T, ffn("up_qa")[f].reshape(KR, D).T], 1))
        qa = ffn("down_qa")[f].reshape(KR, I).T
        w[:, DQ_AT:DQ_AT + KR] = qa[:P]
        w[KR:B2, DQ_AT + KR:MU_AT] = qa[P:]
        for n in range(3):
            w[n * GR + f // GROUPS * F:n * GR + (f // GROUPS + 1) * F, MU_AT:] = ffn("mask_up_W")[f].T
    out["expert_w"] = W
    return out


def kernel(**inputs):
    import numpy as np
    import concourse.bacc as bacc
    from concourse.bass_utils import run_bass_kernel_spmd

    laid = layout(np, {name: np.asarray(x) for name, x in inputs.items()})
    nc = bacc.Bacc("TRN2", target_bir_lowering=False, num_devices=1)
    arrays, args = {}, {}
    for name, x in laid.items():
        x = np.ascontiguousarray(x)
        arrays[f"in_{name}"] = x
        args[name] = nc.dram_tensor(f"in_{name}", x.shape, mybir.dt.from_np(x.dtype), kind="ExternalInput").ap()
    args["out"] = nc.dram_tensor("out_0", (B, S, D), F32, kind="ExternalOutput").ap()
    program(nc, args)
    done = run_bass_kernel_spmd(nc, [arrays], core_ids=[0])
    return done.results[0]["out_0"]
```

```python
from contextlib import ExitStack

import concourse.bass as bass
from concourse import mybir
from concourse.alu_op_type import AluOpType as ALU

F32 = mybir.dt.float32
F32R = mybir.dt.float32r
ACT = mybir.ActivationFunctionType
AX = mybir.AxisListType

P = 128
B, S, D = 16, 128, 256
DK = D // P
H, KV, DH = 16, 4, 128
G = H // KV
PAIR = 2
TURNS = B // PAIR
TOK = PAIR * S
XH, HD = 2, 128
E, F, TOPK, I, R = 64, 8, 6, 176, 8
LN_EPS, GN_EPS = 1e-5, 1e-3
FK = E
CT = 512
CHUNKS = B * S // CT
TT = CT // P
SI = 3
NROUTE = DK * E + 2 * DK * SI * P + SI * D


class Split:

    def __init__(self, hi, lo):
        self.hi, self.lo = hi, lo

    def __getitem__(self, at):
        return Split(self.hi[at], self.lo[at])

    def rearrange(self, *a, **k):
        return Split(self.hi.rearrange(*a, **k), self.lo.rearrange(*a, **k))


def product(pe, out, left, right, first=True, last=True, **more):
    pe.matmul(out, left.hi, right.hi, start=first, stop=False, **more)
    pe.matmul(out, left.hi, right.lo, start=False, stop=False, **more)
    return pe.matmul(out, left.lo, right.hi, start=False, stop=last, **more)


class Memory:

    def __init__(self, nc, stage):
        self.nc, self.stage, self.ctx, self.sems = nc, stage, ExitStack(), []
        self.ctx.callback(self.reset_sems)

    def sb(self, name, cols, dt=F32, parts=P):
        return self.ctx.enter_context(self.nc.sbuf_tensor(f"{self.stage}_{name}", [parts, cols], dt))

    def split(self, name, cols, parts=P):
        return Split(self.sb(name + "_hi", cols, F32R, parts), self.sb(name + "_lo", cols, F32R, parts))

    def bank(self, name):
        return self.ctx.enter_context(self.nc.psum_tensor(f"{self.stage}_{name}", [P, 512], F32))

    def sem(self, name):
        self.sems.append(self.nc.alloc_semaphore(name=f"{self.stage}_{name}"))
        return self.sems[-1]

    def reset_sems(self):
        if not self.sems:
            return
        self.nc.clear_and_free_semaphores(self.sems)
        self.nc.all_engine_barrier()


def self_attention(nc, a, r1, stats1, ident, cross_w, ctxT0):
    m = Memory(nc, "att")
    with m.ctx:
        CH = 1024
        stage = [m.sb(f"stage{n}", CH) for n in range(4)]
        Wq = m.split("Wq", KV * CH)
        Wk, Wv = m.split("Wk", CH), m.split("Wv", CH)
        Wo = m.split("Wo", KV * CH)
        bq, bk, bv = m.sb("bq", H), m.sb("bk", KV), m.sb("bv", KV)
        bo = m.sb("bo", PAIR * D)
        xT32 = m.sb("xT32", DK * TOK)
        xT = m.split("xT", DK * TOK)
        x_tok = m.sb("x_tok", PAIR * D)
        QT = [m.sb(f"QT{n}", G * TOK) for n in range(2)]
        KT = m.sb("KT", KV * TOK)
        V = m.split("V", PAIR * KV * DH)
        by_job = lambda name, cols: [[m.sb(f"{name}{j}{b}", cols) for b in range(PAIR)] for j in range(2)]
        probs, mass, share = by_job("probs", G * S), by_job("mass", G), by_job("share", G)
        PT = [m.split(f"PT{b}", G * S) for b in range(PAIR)]
        OT = m.split("OT", G * TOK)
        top = [m.sb(f"top{b}", G) for b in range(PAIR)]
        bias = [m.sb(f"bias{b}", G) for b in range(PAIR)]
        stats, r_now = m.sb("stats", PAIR * 6), m.sb("r_now", PAIR * D)

        proj_banks = [m.bank(f"proj{n}") for n in range(3)]
        score = [m.bank(f"score{b}") for b in range(PAIR)]
        mix = [m.bank(f"mix{b}") for b in range(PAIR)]
        acc = m.bank("acc")

        small_in, next_in = m.sem("small_in"), m.sem("next_in")
        w_in = [m.sem(f"w_in{n}") for n in range(4)]
        w_hi, w_lo = m.sem("w_hi"), m.sem("w_lo")
        pool_hi, pool_lo = m.sem("pool_hi"), m.sem("pool_lo")
        xT_in, xT_hi, xT_lo = m.sem("xT_in"), m.sem("xT_hi"), m.sem("xT_lo")
        x_in, xb_ready = m.sem("x_in"), m.sem("xb_ready")
        proj_ready, proj_act, proj_dve = m.sem("proj_ready"), m.sem("proj_act"), m.sem("proj_dve")
        score_ready, max_ready, bias_ready = m.sem("score_ready"), m.sem("max_ready"), m.sem("bias_ready")
        exp_ready, share_ready, prob_ready = m.sem("exp_ready"), m.sem("share_ready"), m.sem("prob_ready")
        pt_ready, pt_hi, pt_lo = m.sem("pt_ready"), m.sem("pt_hi"), m.sem("pt_lo")
        o_ready, o_hi, o_lo = m.sem("o_ready"), m.sem("o_hi"), m.sem("o_lo")
        acc_ready, r_ready, stats_ready, kept_ready = (
            m.sem("acc_ready"), m.sem("r_ready"), m.sem("stats_ready"), m.sem("kept_ready"))

        SCALE = float(DH) ** -0.5
        cut = lambda j: slice(j * CH, (j + 1) * CH)
        q_chunk = lambda j, who: (a["Wq"][:, cut(j)], Wq[:, cut(j)], who)
        o_chunk = lambda j: (a["Wo"][:, cut(j)], Wo[:, cut(j)], "pool")
        chunks = [(a["Wk"], Wk[:, :], "act"), q_chunk(0, "act"), q_chunk(1, "act"), (a["Wv"], Wv[:, :], "act"),
                  q_chunk(2, "act"), q_chunk(3, "act"), o_chunk(0), o_chunk(1), o_chunk(2), o_chunk(3)]
        pool_chunks = [n for n, c in enumerate(chunks) if c[2] == "pool"]
        TURNED_FIRST = (0,)
        AFTER = {4: 4, 6: 5}
        FIRST, PER = 8, 12

        def unit(g, n):
            return FIRST + PER * g + n

        def taken(g, n, parity):
            qk = PER - PAIR
            before = (FIRST - PAIR) // 2 + PAIR + (PER // 2 + PAIR // 2) * g
            return before + (min(n, qk) + parity) // 2 + max(0, n - qk)

        def wait_out(pe, g, n):
            if n < 1:
                g, n = g - 1, n + PER
            odd = n % 2 and n <= PER - PAIR
            pe.wait_ge(proj_act if odd else proj_dve, taken(g, n, 1 if odd else 0))

        def proj(n):
            return proj_banks[(FIRST + n - 1) % 3]

        def units_of(kind):
            if kind in ("K", "V"):
                return [(kind, 0), (kind, 1)]
            return [("Q", kind, 0), ("Q", kind, 1)]

        BEFORE = units_of("K") + units_of(0) + units_of(1) + units_of("V")

        def step_units(j, last):
            if j < 2:
                return units_of(j + 2)
            if last:
                return []
            return units_of("K") + units_of(0) if j == 2 else units_of(1)

        def job(g, j, b):
            return g * KV * PAIR + PAIR * j + b + 1

        block = m.ctx.enter_context(nc.Block())

        @block.sync
        def _(sp):
            sp.dma_start(xT32[:, :].rearrange("p (k t) -> p k t", k=DK), a["xT"][:, :, 0:TOK]).then_inc(xT_in, 16)
            for n, (src, _dst, _who) in enumerate(chunks):
                if n == 1:
                    for dst, src_s in ((bq[:, :], a["bq"]), (bk[:, :], a["bk"]), (bv[:, :], a["bv"])):
                        sp.dma_start(dst, src_s).then_inc(small_in, 16)
                    sp.dma_start(bo[:, :].rearrange("p (b d) -> p b d", b=PAIR),
                                 a["bo"].rearrange("(o b d) -> o b d", o=1, b=1).to_broadcast([P, PAIR, D])
                                 ).then_inc(small_in, 16)
                    sp.dma_start(ident[:, :], a["ident"]).then_inc(small_in, 16)
                if n >= 4:
                    if chunks[n - 4][2] == "act":
                        sp.wait_ge(w_lo, n - 3)
                    else:
                        sp.wait_ge(pool_lo, pool_chunks.index(n - 4) + 1)
                sp.dma_start(stage[n % 4][:, :], src).then_inc(w_in[n % 4], 16)
            sp.dma_start(cross_w[:, :], a["cross_w"]).then_inc(next_in, 16)
            sp.dma_start(ctxT0[:, :].rearrange("p (h t) -> p h t", h=XH), a["ctxT"][:, :, 0:CT]).then_inc(next_in, 16)
            with sp.Fori(0, TURNS - 1) as g:
                sp.wait_ge(xT_lo, g + 1)
                sp.dma_start(xT32[:, :].rearrange("p (k t) -> p k t", k=DK),
                             a["xT"][:, :, bass.ds(g * TOK + TOK, TOK)]).then_inc(xT_in, 16)
            sp.wait_ge(next_in, 32)

        @block.gpsimd
        def _(pool):
            def load_x(g):
                pool.dma_start(x_tok[:, :], a["x_tok"][:, bass.ds(g * PAIR * D, PAIR * D)]).then_inc(x_in, 16)

            waiting = list(enumerate(pool_chunks))

            def split_chunk():
                n, at = waiting.pop(0)
                dst = chunks[at][1]
                pool.wait_ge(w_in[at % 4], 16 * (at // 4 + 1))
                pool.tensor_copy(dst.hi, stage[at % 4][:, :]).then_inc(pool_hi, 1)
                pool.wait_ge(pool_hi, n + 1)
                pool.tensor_tensor(dst.lo, stage[at % 4][:, :], dst.hi.bitcast(F32), ALU.subtract).then_inc(pool_lo, 1)

            def normalise(g, j):
                for b in range(PAIR):
                    pool.wait_ge(share_ready, job(g, j, b))
                    p3 = probs[j % 2][b][:, :].rearrange("p (h k) -> p h k", h=G)
                    each = share[j % 2][b][:, :].rearrange("p (h o) -> p h o", o=1).to_broadcast([P, G, S])
                    pool.tensor_tensor(p3, p3, each, ALU.mult).then_inc(prob_ready, 1)

            def turn(g, first, last):
                load_x(g)
                for j in range(KV):
                    if j < KV - 1:
                        normalise(g, j + 1)
                    elif not last:
                        normalise(g + 1, 0)
                    if first and waiting:
                        split_chunk()
                    if j == 2:
                        pool.wait_ge(small_in, 80)
                        pool.wait_ge(x_in, g * 16 + 16)
                        pool.tensor_tensor(x_tok[:, :], x_tok[:, :], bo[:, :], ALU.add).then_inc(xb_ready, 1)
                pool.wait_ge(r_ready, g + 1)

            split_chunk()
            normalise(0, 0)
            split_chunk()
            turn(0, True, False)
            with pool.Fori(1, TURNS - 1) as g:
                turn(g, False, False)
            turn(TURNS - 1, False, True)

        @block.tensor
        def _(pe):
            def project(what, n):
                out = proj(n)
                if what[0] == "V":
                    b = what[1]
                    for k in range(DK):
                        mm = product(pe, out[:, :], xT[:, k * TOK + b * S:k * TOK + (b + 1) * S],
                                     Wv[:, k * 512:(k + 1) * 512], first=k == 0, last=k == DK - 1)
                else:
                    W = Wk[:, :] if what[0] == "K" else Wq[:, what[1] * CH:(what[1] + 1) * CH]
                    for h in range(2):
                        head = 2 * what[-1] + h
                        for k in range(DK):
                            mm = product(pe, out[:, h * TOK:(h + 1) * TOK],
                                         W[:, k * 512 + head * DH:k * 512 + (head + 1) * DH],
                                         xT[:, k * TOK:(k + 1) * TOK], first=k == 0, last=k == DK - 1)
                mm.then_inc(proj_ready, 1)

            pe.wait_ge(xT_lo, 1)
            for n, what in enumerate(BEFORE, 1):
                if n % 2:
                    pe.wait_ge(w_lo, (n + 1) // 2)
                if n > 3:
                    wait_out(pe, -1, n - 3 + PER - FIRST)
                project(what, n - FIRST)
            pe.wait_ge(small_in, 80)

            def scores(j, g=None):
                for b in range(PAIR):
                    if g is not None:
                        pe.wait_ge(exp_ready, job(g, j - 1, b))
                    for h in range(G):
                        mm = pe.matmul(score[b][:, h * S:(h + 1) * S],
                                       QT[j % 2][:, h * TOK + b * S:h * TOK + (b + 1) * S],
                                       KT[:, j % KV * TOK + b * S:j % KV * TOK + (b + 1) * S], start=True, stop=True)
                    mm.then_inc(score_ready, 1)

            for n in (3, 4):
                wait_out(pe, -1, n + PER - FIRST)
            scores(0)

            def turn(g, last, weights):
                n = 0

                def projects(what):
                    nonlocal n
                    n += 1
                    wait_out(pe, g, n - 3)
                    project(what, n)

                def out_project(j):
                    if weights:
                        pe.wait_ge(pool_lo, j + 1)
                    pe.wait_ge(o_lo, g * KV * PAIR + PAIR * (j + 1))
                    if j == 0:
                        if not weights:
                            pe.wait_ge(r_ready, g)
                    for b in range(PAIR):
                        for h in range(G):
                            mm = product(pe, acc[:, b * D:(b + 1) * D],
                                         OT[:, (h * PAIR + b) * S:(h * PAIR + b + 1) * S],
                                         Wo[:, j * CH + h * D:j * CH + (h + 1) * D],
                                         first=j == 0 and b == 0 and h == 0, last=j == KV - 1 and h == G - 1,
                                         skip_group_check=True)
                    if j == KV - 1:
                        mm.then_inc(acc_ready, 1)

                for j in range(KV):
                    if not (last and j == KV - 1):
                        for q_unit in ((-3, -2), (1, 2), (3, 4), (7, 8))[j]:
                            wait_out(pe, g, q_unit)
                        scores(j + 1, g)
                    if j == 1:
                        for what in step_units(j, last):
                            if weights:
                                pe.wait_ge(w_lo, j + 5)
                            projects(what)
                    for b in range(PAIR):
                        pe.wait_ge(prob_ready, job(g, j, b))
                        if j or not weights:
                            pe.wait_ge(o_lo, job(g, j - 1, b))
                        for h in range(G):
                            mm = pe.transpose(mix[b][:, h * S:(h + 1) * S], probs[j % 2][b][:, h * S:(h + 1) * S],
                                              ident[:, :])
                        mm.then_inc(pt_ready, 1)
                    if j == 0 and weights:
                        pe.wait_ge(w_lo, j + 5)
                    if j == 2 and not last:
                        pe.wait_ge(xT_lo, g + 2)
                    if j != 1:
                        for what in step_units(j, last):
                            projects(what)
                    if j:
                        out_project(j - 1)
                    if j == 0:
                        wait_out(pe, g, 0)
                    for b in range(PAIR):
                        pe.wait_ge(pt_lo, job(g, j, b))
                        product(pe, mix[b][:, :], V[:, (b * KV + j) * DH:(b * KV + j + 1) * DH],
                                PT[b][:, :]).then_inc(o_ready, 1)
                    if j == KV - 1:
                        if not last:
                            for what in units_of("V"):
                                projects(what)
                        out_project(j)

            turn(0, False, True)
            with pe.Fori(1, TURNS - 1) as g:
                turn(g, False, False)
            turn(TURNS - 1, True, False)

        def half_out(what, h):
            head = 2 * what[-1] + h
            if what[0] == "K":
                return KT[:, head * TOK:(head + 1) * TOK], bk[:, head:head + 1]
            q = what[1] * G + head
            return QT[what[1] % 2][:, head * TOK:(head + 1) * TOK], bq[:, q:q + 1]

        @block.scalar
        def _(act):
            def high_x(g):
                act.wait_ge(xT_in, g * 16 + 16)
                act.activation(xT.hi[:, :], xT32[:, :], ACT.Copy).then_inc(xT_hi, 1)

            high_x(0)

            def high_weights(n):
                act.wait_ge(w_in[n % 4], 16 * (n // 4 + 1))
                act.activation(chunks[n][1].hi, stage[n % 4][:, :], ACT.Copy).then_inc(w_hi, 1)

            for n in range(4):
                high_weights(n)
            act.wait_ge(small_in, 80)

            def unit_part(what, g, n):
                if what[0] == "V" or n % 2:
                    act.wait_ge(proj_ready, unit(g, n))
                if what[0] == "V":
                    ins = act.activation(V.hi[:, what[1] * 512:(what[1] + 1) * 512], proj(n)[:, :], ACT.Copy)
                elif n % 2:
                    for h in range(2):
                        dst, b = half_out(what, h)
                        ins = act.activation(dst, proj(n)[:, h * TOK:(h + 1) * TOK], ACT.Identity, bias=b)
                else:
                    return
                ins.then_inc(proj_act, 1)

            def exps(g, j, b):
                act.wait_ge(bias_ready, job(g, j, b))
                p_, m_ = probs[j % 2][b], mass[j % 2][b]
                for h in range(G):
                    c = slice(h * S, (h + 1) * S)
                    ins = act.activation(p_[:, c], score[b][:, c], ACT.Exp, bias=bias[b][:, h:h + 1],
                                         scale=SCALE, accum_out=m_[:, h:h + 1])
                ins.then_inc(exp_ready, 1)

            for n, what in enumerate(BEFORE, 1):
                unit_part(what, -1, n + PER - FIRST)
                if n in AFTER:
                    high_weights(AFTER[n])
            for b in range(PAIR):
                exps(0, 0, b)

            def turn(g, last):
                n = 0
                for j in range(KV):
                    def high_p(b):
                        act.wait_ge(pt_ready, job(g, j, b))
                        act.activation(PT[b].hi[:, :], mix[b][:, :], ACT.Copy).then_inc(pt_hi, 1)

                    if j in TURNED_FIRST:
                        for b in range(PAIR):
                            high_p(b)
                    for b in range(PAIR):
                        if not (last and j == KV - 1):
                            exps(g, j + 1, b)
                        if j != 1 and j not in TURNED_FIRST:
                            high_p(b)
                    for what in step_units(j, last):
                        n += 1
                        unit_part(what, g, n)
                    if j == 1:
                        if not last:
                            act.wait_ge(proj_ready, unit(g, n))
                            high_x(g + 1)
                        for b in range(PAIR):
                            high_p(b)
                    for b in range(PAIR):
                        act.wait_ge(o_ready, job(g, j, b))
                        act.activation(OT.hi[:, :].rearrange("p (h b q) -> p h b q", h=G, b=PAIR)[:, :, b, :],
                                       mix[b][:, :].rearrange("p (h q) -> p h q", h=G), ACT.Identity,
                                       bias=bv[:, j:j + 1]).then_inc(o_hi, 1)
                if not last:
                    for what in units_of("V"):
                        n += 1
                        unit_part(what, g, n)

            with act.Fori(0, TURNS - 1) as g:
                turn(g, False)
            turn(TURNS - 1, True)

        @block.vector
        def _(dve):
            def low_x(g):
                dve.wait_ge(xT_hi, g + 1)
                dve.tensor_tensor(xT.lo[:, :], xT32[:, :], xT.hi[:, :].bitcast(F32), ALU.subtract).then_inc(xT_lo, 1)

            low_x(0)

            def low_weights(n):
                dst = chunks[n][1]
                dve.wait_ge(w_hi, n + 1)
                dve.tensor_tensor(dst.lo, stage[n % 4][:, :], dst.hi.bitcast(F32), ALU.subtract).then_inc(w_lo, 1)

            for n in range(4):
                low_weights(n)
            dve.wait_ge(small_in, 80)

            def unit_part(what, g, n):
                if what[0] == "V":
                    dve.wait_ge(proj_act, taken(g, n, 1))
                    at = slice(what[1] * 512, (what[1] + 1) * 512)
                    ins = dve.tensor_tensor(V.lo[:, at], proj(n)[:, :], V.hi[:, at].bitcast(F32), ALU.subtract)
                elif n % 2 == 0:
                    dve.wait_ge(proj_ready, unit(g, n))
                    for h in range(2):
                        dst, b = half_out(what, h)
                        ins = dve.tensor_scalar(dst, proj(n)[:, h * TOK:(h + 1) * TOK], b, None, ALU.add)
                else:
                    return
                ins.then_inc(proj_dve, 1)

            def maxima(g, j, b):
                dve.wait_ge(score_ready, job(g, j, b))
                dve.tensor_reduce(top[b][:, :], score[b][:, :].rearrange("p (h k) -> p h k", h=G), AX.X,
                                  ALU.max).then_inc(max_ready, 1)
                dve.wait_ge(max_ready, job(g, j, b))
                dve.tensor_scalar(bias[b][:, :], top[b][:, :], -SCALE, None, ALU.mult).then_inc(bias_ready, 1)

            def low_p(g, j, b):
                dve.wait_ge(pt_hi, job(g, j, b))
                dve.tensor_tensor(PT[b].lo[:, :], mix[b][:, :], PT[b].hi[:, :].bitcast(F32), ALU.subtract
                                  ).then_inc(pt_lo, 1)

            def shares(g, j, b):
                dve.wait_ge(exp_ready, job(g, j, b))
                dve.reciprocal(share[j % 2][b][:, :], mass[j % 2][b][:, :]).then_inc(share_ready, 1)

            for n, what in enumerate(BEFORE, 1):
                unit_part(what, -1, n + PER - FIRST)
                if n in AFTER:
                    low_weights(AFTER[n])
            for b in range(PAIR):
                maxima(0, 0, b)
            for b in range(PAIR):
                shares(0, 0, b)

            def turn(g, last):
                n = 0
                for j in range(KV):
                    ahead = not (last and j == KV - 1)
                    for b in range(PAIR):
                        if ahead:
                            maxima(g, j + 1, b)
                    if j in TURNED_FIRST:
                        for b in range(PAIR):
                            low_p(g, j, b)
                    for b in range(PAIR):
                        if ahead:
                            shares(g, j + 1, b)
                        if j != 1 and j not in TURNED_FIRST:
                            low_p(g, j, b)
                    for what in step_units(j, last):
                        n += 1
                        unit_part(what, g, n)
                    if j == 1:
                        if not last:
                            low_x(g + 1)
                        for b in range(PAIR):
                            low_p(g, j, b)
                    for b in range(PAIR):
                        dve.wait_ge(o_hi, job(g, j, b))
                        o4 = lambda t: t[:, :].rearrange("p (h b q) -> p h b q", h=G, b=PAIR)[:, :, b, :]
                        dve.scalar_tensor_tensor(o4(OT.lo), mix[b][:, :].rearrange("p (h q) -> p h q", h=G), bv[:, j:j + 1],
                                                 o4(OT.hi).bitcast(F32), ALU.add, ALU.subtract).then_inc(o_lo, 1)
                if not last:
                    for what in units_of("V"):
                        n += 1
                        unit_part(what, g, n)
                dve.wait_ge(acc_ready, g + 1)
                dve.wait_ge(xb_ready, g + 1)
                dve.tensor_tensor(r_now[:, :], acc[:, :], x_tok[:, :], ALU.add).then_inc(r_ready, 1)
                dve.wait_ge(r_ready, g + 1)
                for b in range(PAIR):
                    ins = dve.bn_stats(stats[:, 6 * b:6 * b + 6], r_now[:, b * D:(b + 1) * D])
                ins.then_inc(stats_ready, 1)
                dve.tensor_scalar(r1[:, bass.ds(g * PAIR * D, PAIR * D)], r_now[:, :], 1.0, None, ALU.mult
                                  ).then_inc(kept_ready, 1)
                dve.wait_ge(stats_ready, g + 1)
                dve.tensor_scalar(stats1[:, bass.ds(g * PAIR * 6, PAIR * 6)], stats[:, :], 1.0, None, ALU.mult
                                  ).then_inc(kept_ready, 1)
                dve.wait_ge(kept_ready, 2 * g + 2)

            with dve.Fori(0, TURNS - 1) as g:
                turn(g, False)
            turn(TURNS - 1, True)


def whole(eng, xT, xT32, c):
    at = lambda t: t[:, :].rearrange("p (k t) -> p k t", k=DK)[:, :, c * CT:(c + 1) * CT]
    return eng.tensor_tensor(at(xT32), at(xT.hi).bitcast(F32), at(xT.lo).bitcast(F32), ALU.add)


def cross_attention(nc, a, r, stats, ident, W, ctxT0, xT, xT32, w32, Wroute):
    m = Memory(nc, "cross")
    CB = CT // S
    HH = XH * HD
    with m.ctx:
        Wh, WhT = W[:, 0:HH], W[:, HH:2 * HH]
        wg, wo = W[:, 2 * HH:2 * HH + DK * D], W[:, 2 * HH + DK * D:]
        gram = m.sb("gram", HH)
        gamma, beta = m.sb("gamma", D), m.sb("beta", D)
        decay = m.sb("decay", XH * S)
        ctxT = [ctxT0] + [m.sb(f"ctxT{n}", XH * CT) for n in range(1, CHUNKS)]
        KG = m.sb("KG", XH * B * S)
        V = m.sb("V", XH * B * HD)
        x1T = xT32[:, :]
        masked, positive = m.sb("masked", XH * S), m.sb("positive", XH * S)
        AT = m.sb("AT", XH * S)
        Y = [m.sb(f"Y{n}", CB * D) for n in range(2)]
        WY = [m.sb(f"WY{n}", 2 * D) for n in range(2)]
        WYT = [m.sb(f"WYT{n}", 2 * D) for n in range(2)]
        mv, var, std, rstd = m.sb("mv", B * 2), m.sb("var", B), m.sb("std", B), m.sb("rstd", B)
        shift = m.sb("shift", B)
        ostats, omv = m.sb("ostats", CB * 12), m.sb("omv", CB * 2)
        ovar, ostd, orstd, oshift = m.sb("ovar", CB), m.sb("ostd", CB), m.sb("orstd", CB), m.sb("oshift", CB)
        bank = [m.bank(f"bank{n}") for n in range(8)]

        const_in, gram_ready, gram_out = m.sem("const_in"), m.sem("gram_ready"), m.sem("gram_out")
        ctx_in = [m.sem(f"ctx_in{n}") for n in range(CHUNKS)]
        kv_ready, kg_out, v_out = m.sem("kv_ready"), m.sem("kg_out"), m.sem("v_out")
        mv_ready, var_ready, std_ready, rstd_ready = (
            m.sem("mv_ready"), m.sem("var_ready"), m.sem("std_ready"), m.sem("rstd_ready"))
        x_ready, turned = m.sem("x_ready"), m.sem("turned")
        x1T_out = [m.sem("x1T_by_act"), m.sem("x1T_by_dve")]
        sum_ready, masked_ready, positive_ready, at_ready = (
            m.sem("sum_ready"), m.sem("masked_ready"), m.sem("positive_ready"), m.sem("at_ready"))
        o_ready, ostats_ready, omv_ready, ovar_ready, ostd_ready, orstd_ready, oshift_ready, y_ready = (
            m.sem("o_ready"), m.sem("ostats_ready"), m.sem("omv_ready"), m.sem("ovar_ready"), m.sem("ostd_ready"),
            m.sem("orstd_ready"), m.sem("oshift_ready"), m.sem("y_ready"))
        scaled_ready, shifted_ready = m.sem("scaled_ready"), m.sem("shifted_ready")
        scaled_dve, shifted_dve = m.sem("scaled_dve"), m.sem("shifted_dve")
        gate_ready, wy_ready, wyt_ready = m.sem("gate_ready"), m.sem("wy_ready"), m.sem("wyt_ready")
        wyt_out = m.sem("wyt_out")
        out_ready, r_ready, stats_ready, shift_ready, even_ready, odd_ready = (
            m.sem("out_ready"), m.sem("r_ready"), m.sem("stats_ready"), m.sem("shift_ready"),
            m.sem("even_ready"), m.sem("odd_ready"))
        turned2, turned2_hi, turned2_lo = m.sem("turned2"), m.sem("turned2_hi"), m.sem("turned2_lo")
        route_in, route_hi, route_lo, whole_ready = (
            m.sem("route_in"), m.sem("route_hi"), m.sem("route_lo"), m.sem("whole_ready"))

        mean = lambda t: mv[:, 2 * t:2 * t + 1]
        tile = lambda t: r[:, t * D:(t + 1) * D]
        pairs = lambda src: src.rearrange("p (k t) -> p k t", k=DK)
        mv2 = mv[:, :].rearrange("p (t s) -> p t s", s=2)
        omv2 = omv[:, :].rearrange("p (t s) -> p t s", s=2)

        def kv_to(n):
            c, h = n // 4, n // 2 % 2
            if n % 2 == 0:
                return KG[:, h * B * S + c * CT:h * B * S + (c + 1) * CT]
            return V[:, (h * B + c * CB) * HD:(h * B + (c + 1) * CB) * HD]

        def affine(eng, c, half, scaled, shifted, n):
            Y3 = Y[c % 2][:, half * 2 * D:(half + 1) * 2 * D].rearrange("p (b d) -> p b d", b=2)
            both = lambda t: t[:, :].rearrange("p (o d) -> p o d", o=1).to_broadcast([P, 2, D])
            eng.tensor_tensor(Y3, Y3, both(gamma), ALU.mult).then_inc(scaled, 1)
            eng.wait_ge(scaled, n)
            eng.tensor_tensor(Y3, Y3, both(beta), ALU.add).then_inc(shifted, 1)

        def mix_bank(c):
            return bank[6:8] if c == 1 else bank[0:2]

        def x1T_of(u):
            return pairs(x1T)[:, :, 2 * u * P:(2 * u + 2) * P], pairs(bank[4 + u % 2][:, :])

        block = m.ctx.enter_context(nc.Block())

        @block.sync
        def _(sp):
            for c in range(1, CHUNKS):
                sp.dma_start(ctxT[c][:, :].rearrange("p (h t) -> p h t", h=XH),
                             a["ctxT"][:, :, c * CT:(c + 1) * CT]).then_inc(ctx_in[c], 16)
            sp.dma_start(decay[:, :], a["decay"]).then_inc(const_in, 16)
            for dst, src in ((gamma, a["gamma"]), (beta, a["beta"])):
                sp.dma_start(dst[:, :], src.rearrange("(o d) -> o d", o=1).to_broadcast([P, D])).then_inc(const_in, 16)
            sp.dma_start(w32[:, :], a["route_w"]).then_inc(route_in, 16)

        @block.gpsimd
        def _(pool):
            pool.wait_ge(route_in, 16)
            pool.tensor_copy(Wroute.hi[:, :], w32[:, :]).then_inc(route_hi, 1)
            pool.wait_ge(route_hi, 1)
            pool.tensor_tensor(Wroute.lo[:, :], w32[:, :], Wroute.hi[:, :].bitcast(F32), ALU.subtract).then_inc(route_lo, 1)
            pool.wait_ge(const_in, 48)
            for c in range(CHUNKS):
                pool.wait_ge(y_ready, c + 1)
                for half in range(2 if c else 1):
                    affine(pool, c, half, scaled_ready, shifted_ready, max(2 * c + half, 1))
            for c in range(CHUNKS - 1):
                pool.wait_ge(turned2_lo, 2 * c + 2)
                whole(pool, xT, xT32, c).then_inc(whole_ready, 1)

        @block.tensor
        def _(pe):
            def turn_tiles(u, to):
                for k in range(DK):
                    for i in range(2):
                        t = 2 * u + i
                        mm = pe.transpose(to[:, (k * 2 + i) * P:(k * 2 + i + 1) * P],
                                          r[:, t * D + k * P:t * D + (k + 1) * P], ident[:, :])
                return mm

            for h in range(XH):
                mm = pe.matmul(bank[4][:, h * HD:(h + 1) * HD], WhT[:, h * HD:(h + 1) * HD], WhT[:, h * HD:(h + 1) * HD],
                               start=True, stop=True)
            mm.then_inc(gram_ready, 1)
            for n in range(4 * CHUNKS):
                c, h = n // 4, n // 2 % 2
                if n == 0:
                    pe.wait_ge(gram_out, 1)
                if n % 4 == 0 and c:
                    pe.wait_ge(ctx_in[c], 16)
                if n >= 4:
                    pe.wait_ge((kg_out, v_out)[n % 2], (n - 4) // 2 + 1)
                if n % 2 == 0:
                    pe.matmul(bank[n % 4][:, :], gram[:, h * HD:(h + 1) * HD], ctxT[c][:, h * CT:(h + 1) * CT],
                              start=True, stop=True).then_inc(kv_ready, 1)
                else:
                    for b in range(CB):
                        mm = pe.matmul(bank[n % 4][:, b * HD:(b + 1) * HD], ctxT[c][:, h * CT + b * S:h * CT + (b + 1) * S],
                                       Wh[:, h * HD:(h + 1) * HD], start=True, stop=True)
                    mm.then_inc(kv_ready, 1)

            def sum_scores(u):
                pe.wait_ge(x1T_out[u % 2], u // 2 + 1)
                if u == 0:
                    pe.wait_ge(kg_out, 2 * CHUNKS)
                for b in (2 * u, 2 * u + 1):
                    for h in range(XH):
                        at = slice(h * B * S + b * S, h * B * S + (b + 1) * S)
                        mm = pe.matmul(bank[6 + h][:, 0:S], KG[:, at], x1T[:, at], start=b == 0, stop=b == B - 1)
                if u == B // 2 - 1:
                    mm.then_inc(sum_ready, 1)

            for u in range(B // 2):
                pe.wait_ge(x_ready, 2 * u + 2)
                if u >= 2:
                    pe.wait_ge(x1T_out[u % 2], u // 2)
                turn_tiles(u, bank[4 + u % 2]).then_inc(turned, 1)
                if u:
                    sum_scores(u - 1)
            sum_scores(B // 2 - 1)

            def mix_values(c):
                if c >= 2:
                    pe.wait_ge(y_ready, 2 * c - 3)
                elif c == 0:
                    pe.wait_ge(v_out, 2 * CHUNKS)
                for h in range(XH):
                    mm = pe.matmul(mix_bank(c)[h][:, :], AT[:, h * S:(h + 1) * S],
                                   V[:, (h * B + c * CB) * HD:(h * B + (c + 1) * CB) * HD], start=True, stop=True)
                mm.then_inc(o_ready, 1)

            def gates(c, halves=(0, 1)):
                for i in halves:
                    if c:
                        pe.wait_ge(wy_ready, 2 * (c - 1) + i + 1)
                    for j in range(2):
                        b = c * CB + 2 * i + j
                        for k in range(DK):
                            mm = pe.matmul(bank[2 + i][:, j * D:(j + 1) * D], x1T[:, (k * B + b) * S:(k * B + b + 1) * S],
                                           wg[:, k * D:(k + 1) * D], start=k == 0, stop=k == DK - 1)
                    mm.then_inc(gate_ready, 1)

            def turn_x2(c):
                for i in range(2):
                    u = 2 * c + i
                    pe.wait_ge(even_ready, u + 1)
                    pe.wait_ge(odd_ready, u + 1)
                    turn_tiles(u, bank[4 + i]).then_inc(turned2, 1)

            gates(0, (0,))
            pe.wait_ge(at_ready, 1)
            mix_values(0)
            gates(0, (1,))
            mix_values(1)
            mix_values(2)
            for c in range(CHUNKS):
                for i in range(2):
                    pe.wait_ge(wy_ready, 2 * c + i + 1)
                    if c >= 2:
                        pe.wait_ge(turned2_lo, 2 * (c - 2) + i + 1)
                    for j in range(4):
                        mm = pe.transpose(bank[4 + i][:, j * P:(j + 1) * P], WY[i][:, j * P:(j + 1) * P], ident[:, :])
                    mm.then_inc(wyt_ready, 1)
                if c and c < CHUNKS - 2:
                    mix_values(c + 2)
                if c < CHUNKS - 1:
                    gates(c + 1)
                pe.wait_ge(wyt_out, 2 * c + 2)
                if c:
                    turn_x2(c - 1)
                for i in range(2):
                    if c:
                        pe.wait_ge(r_ready, 2 * (c - 1) + i + 1)
                    else:
                        pe.wait_ge(y_ready, 2)
                    for j in range(2):
                        for k in range(DK):
                            mm = pe.matmul(bank[6 + i][:, j * D:(j + 1) * D], WYT[i][:, (2 * j + k) * P:(2 * j + k + 1) * P],
                                           wo[:, k * D:(k + 1) * D], start=k == 0, stop=k == DK - 1)
                    mm.then_inc(out_ready, 1)
            for i in range(2):
                pe.wait_ge(turned2_lo, 2 * (CHUNKS - 2) + i + 1)
            turn_x2(CHUNKS - 1)

        @block.scalar
        def _(act):
            act.wait_ge(gram_ready, 1)
            act.activation(gram[:, :], bank[4][:, 0:HH], ACT.Copy).then_inc(gram_out, 1)
            act.wait_ge(var_ready, 1)
            act.activation(std[:, :], var[:, :], ACT.Sqrt).then_inc(std_ready, 1)
            for n in range(0, 4 * CHUNKS, 2):
                act.wait_ge(kv_ready, n + 1)
                act.activation(kv_to(n), bank[n % 4][:, :], ACT.Copy).then_inc(kg_out, 1)
            for u in range(0, B // 2, 2):
                act.wait_ge(turned, u + 1)
                dst, src = x1T_of(u)
                act.activation(dst, src, ACT.Copy).then_inc(x1T_out[0], 1)

            def normalise_mix(c):
                act.wait_ge(ovar_ready, c + 1)
                act.activation(ostd[:, :], ovar[:, :], ACT.Sqrt).then_inc(ostd_ready, 1)
                act.wait_ge(oshift_ready, c + 1)
                if c >= 2:
                    act.wait_ge(wy_ready, 2 * (c - 1))
                for b in range(CB):
                    for h in range(XH):
                        ins = act.activation(Y[c % 2][:, b * D + h * HD:b * D + (h + 1) * HD],
                                             mix_bank(c)[h][:, b * HD:(b + 1) * HD],
                                             ACT.Identity, bias=oshift[:, b:b + 1], scale=orstd[:, b:b + 1])
                ins.then_inc(y_ready, 1)

            def normalise_x2(c):
                act.wait_ge(shift_ready, c + 1)
                for t in (c * CB + 1, c * CB + 3):
                    act.activation(tile(t), tile(t), ACT.Identity, bias=shift[:, t:t + 1], scale=rstd[:, t:t + 1]
                                   ).then_inc(odd_ready, 1)

            def high_x2(c):
                for i in range(2):
                    u = 2 * c + i
                    act.wait_ge(turned2, u + 1)
                    act.activation(pairs(xT.hi[:, :])[:, :, 2 * u * P:(2 * u + 2) * P], pairs(bank[4 + i][:, :]), ACT.Copy
                                   ).then_inc(turned2_hi, 1)

            def deviation(c):
                act.wait_ge(var_ready, c + 2)
                act.activation(std[:, c * CB:(c + 1) * CB], var[:, c * CB:(c + 1) * CB], ACT.Sqrt).then_inc(std_ready, 1)

            normalise_mix(0)
            normalise_mix(1)
            for c in range(CHUNKS):
                for i in range(2):
                    act.wait_ge(wyt_ready, 2 * c + i + 1)
                    act.activation(WYT[i][:, :], bank[4 + i][:, :], ACT.Copy).then_inc(wyt_out, 1)
                if c:
                    deviation(c - 1)
                    normalise_x2(c - 1)
                if c < CHUNKS - 2:
                    normalise_mix(c + 2)
                if c:
                    high_x2(c - 1)
            deviation(CHUNKS - 1)
            normalise_x2(CHUNKS - 1)
            high_x2(CHUNKS - 1)

        @block.vector
        def _(dve):
            def variance(tiles, n):
                for t in tiles:
                    ins = dve.bn_aggr(mv[:, 2 * t:2 * t + 2], stats[:, 6 * t:6 * t + 6])
                ins.then_inc(mv_ready, 1)
                dve.wait_ge(mv_ready, n)
                at = slice(tiles[0], tiles[-1] + 1)
                dve.tensor_scalar(var[:, at], mv2[:, at, 1], LN_EPS, None, ALU.add).then_inc(var_ready, 1)

            variance(range(B), 1)
            dve.wait_ge(std_ready, 1)
            dve.reciprocal(rstd[:, :], std[:, :]).then_inc(rstd_ready, 1)
            dve.wait_ge(rstd_ready, 1)

            def normalise(t):
                return dve.tensor_scalar(tile(t), tile(t), mean(t), rstd[:, t:t + 1], ALU.subtract, ALU.mult)

            for n in range(2 * CHUNKS):
                for t in (2 * n, 2 * n + 1):
                    normalise(t).then_inc(x_ready, 1)
                dve.wait_ge(kv_ready, 2 * n + 2)
                dve.tensor_copy(kv_to(2 * n + 1), bank[(2 * n + 1) % 4][:, :]).then_inc(v_out, 1)
            for u in range(1, B // 2, 2):
                dve.wait_ge(turned, u + 1)
                dst, src = x1T_of(u)
                dve.tensor_copy(dst, src).then_inc(x1T_out[1], 1)
            dve.wait_ge(sum_ready, 1)
            dve.wait_ge(const_in, 48)
            for h in range(XH):
                c = slice(h * S, (h + 1) * S)
                ins = dve.scalar_tensor_tensor(masked[:, c], bank[6 + h][:, 0:S], float(HD) ** -0.5, decay[:, c],
                                               ALU.mult, ALU.mult)
            ins.then_inc(masked_ready, 1)
            dve.wait_ge(masked_ready, 1)
            dve.scalar_tensor_tensor(positive[:, :], masked[:, :], -1.0, masked[:, :], ALU.mult, ALU.max
                                     ).then_inc(positive_ready, 1)
            dve.wait_ge(positive_ready, 1)
            dve.tensor_scalar(AT[:, :], positive[:, :], 1.0, None, ALU.max).then_inc(at_ready, 1)

            def mix_factors(c):
                dve.wait_ge(o_ready, c + 1)
                if c:
                    dve.wait_ge(y_ready, c)
                for b in range(CB):
                    for h in range(XH):
                        ins = dve.bn_stats(ostats[:, b * 12 + h * 6:b * 12 + h * 6 + 6], mix_bank(c)[h][:, b * HD:(b + 1) * HD])
                ins.then_inc(ostats_ready, 1)
                dve.wait_ge(ostats_ready, c + 1)
                for b in range(CB):
                    ins = dve.bn_aggr(omv[:, 2 * b:2 * b + 2], ostats[:, 12 * b:12 * b + 12])
                ins.then_inc(omv_ready, 1)
                dve.wait_ge(omv_ready, c + 1)
                dve.tensor_scalar(ovar[:, :], omv2[:, :, 1], GN_EPS, None, ALU.add).then_inc(ovar_ready, 1)
                dve.wait_ge(ostd_ready, c + 1)
                dve.reciprocal(orstd[:, :], ostd[:, :]).then_inc(orstd_ready, 1)
                dve.wait_ge(orstd_ready, c + 1)
                dve.scalar_tensor_tensor(oshift[:, :], omv2[:, :, 0], -1.0, orstd[:, :], ALU.mult, ALU.mult
                                         ).then_inc(oshift_ready, 1)

            def gate_mix(c):
                for i in range(2):
                    if c or i == 0:
                        dve.wait_ge(shifted_ready, max(2 * c + i, 1))
                    else:
                        dve.wait_ge(shifted_dve, 1)
                    dve.wait_ge(gate_ready, 2 * c + i + 1)
                    if c:
                        dve.wait_ge(wyt_ready, 2 * (c - 1) + i + 1)
                    dve.scalar_tensor_tensor(WY[i][:, :], bank[2 + i][:, :], 0.0, Y[c % 2][:, i * 2 * D:(i + 1) * 2 * D],
                                             ALU.max, ALU.mult).then_inc(wy_ready, 1)

            def add_output(c):
                for i in range(2):
                    t = c * CB + 2 * i
                    two = r[:, t * D:(t + 2) * D]
                    dve.wait_ge(out_ready, 2 * c + i + 1)
                    dve.tensor_tensor(two, bank[6 + i][:, :], two, ALU.add).then_inc(r_ready, 1)
                    dve.wait_ge(r_ready, 2 * c + i + 1)
                    for j in range(2):
                        ins = dve.bn_stats(stats[:, 6 * (t + j):6 * (t + j) + 6], tile(t + j))
                    ins.then_inc(stats_ready, 1)
                dve.wait_ge(stats_ready, 2 * c + 2)
                variance(range(c * CB, (c + 1) * CB), c + 2)

            def normalise_x2(c):
                at = slice(c * CB, (c + 1) * CB)
                dve.wait_ge(std_ready, c + 2)
                dve.reciprocal(rstd[:, at], std[:, at]).then_inc(rstd_ready, 1)
                dve.wait_ge(rstd_ready, c + 2)
                dve.scalar_tensor_tensor(shift[:, at], mv2[:, at, 0], -1.0, rstd[:, at], ALU.mult, ALU.mult
                                         ).then_inc(shift_ready, 1)
                for t in (c * CB, c * CB + 2):
                    normalise(t).then_inc(even_ready, 1)

            def split_x2(c):
                for i in range(2):
                    u = 2 * c + i
                    dve.wait_ge(turned2_hi, u + 1)
                    to = lambda part: pairs(part[:, :])[:, :, 2 * u * P:(2 * u + 2) * P]
                    dve.tensor_tensor(to(xT.lo), pairs(bank[4 + i][:, :]), to(xT.hi).bitcast(F32), ALU.subtract
                                      ).then_inc(turned2_lo, 1)

            mix_factors(0)
            dve.wait_ge(y_ready, 1)
            affine(dve, 0, 1, scaled_dve, shifted_dve, 1)
            mix_factors(1)
            gate_mix(0)
            for c in range(CHUNKS):
                if c:
                    normalise_x2(c - 1)
                if c < CHUNKS - 2:
                    mix_factors(c + 2)
                if c < CHUNKS - 1:
                    gate_mix(c + 1)
                if c:
                    split_x2(c - 1)
                add_output(c)
            normalise_x2(CHUNKS - 1)
            split_x2(CHUNKS - 1)


GUB = 3 * P
GU_AT = 0
QB_AT = GU_AT + DK * GUB
D1_AT = QB_AT + GUB
D2_AT = D1_AT + D
QA_AT = D2_AT + D
DQ_AT = QA_AT + DK * P
KR = F * R
MU_AT = DQ_AT + DK * KR
WCOLS = MU_AT + D
SCOLS = GUB + D
I2 = I - P
B2 = KR + I2
GROUPS = 2
GR = F // GROUPS * F
MR = 3 * GR


def load_weights(sp, a, e, stage, scale, done):
    sp.dma_start(stage[:, :], a["expert_w"][bass.ds(e, 1), :, :].rearrange("o p n -> p (o n)")).then_inc(done, 16)
    sp.dma_start(scale[:, :], a["expert_scale"][bass.ds(e, 1), :].to_broadcast([P, SCOLS])).then_inc(done, 16)


def scale_weights(pool, stage, scale, done, before):
    qb = slice(QB_AT, QB_AT + GUB)
    pool.tensor_tensor(stage[:, qb], stage[:, qb], scale[:, 0:GUB], ALU.mult).then_inc(done, 1)
    dn = slice(D2_AT, D2_AT + D)
    pool.wait_ge(done, before + 1)
    pool.tensor_tensor(stage[0:KR, dn], stage[0:KR, dn], scale[0:KR, GUB:], ALU.mult).then_inc(done, 1)


def split_low(pool, stage, w, low_done, all_done, count):
    pool.tensor_tensor(w.lo[:, :], stage[:, :], w.hi[:, :].bitcast(F32), ALU.subtract).then_inc(low_done, 1)
    pool.wait_ge(low_done, count)
    mu = (slice(2 * GR, MR), slice(MU_AT, WCOLS))
    pool.tensor_tensor(w.hi[mu], stage[mu], w.hi[mu].bitcast(F32), ALU.subtract).then_inc(all_done, 1)
    pool.wait_ge(all_done, count)


def route_and_share(nc, a, r, ident, xT, xT32, w32, W, softT, share_of, soft_dram, stage, scale, W0):
    m = Memory(nc, "route")
    with m.ctx:
        Wr = w32[:, 0:DK * E]
        at = DK * E
        Wg, Wu = W[:, at:at + DK * SI * P], W[:, at + DK * SI * P:at + 2 * DK * SI * P]
        Wd = W[:, at + 2 * DK * SI * P:]
        inv_raw = m.sb("inv_raw", FK, mybir.dt.int32, E)
        inv = m.sb("inv", FK, F32, E)
        rows = m.sb("rows", 1, F32, E)
        onehot = m.sb("onehot", FK, F32, E)
        EX = E + 8 - TOPK
        top1, mass, part = m.sb("top1", TT), m.sb("mass", TT), m.sb("part", TT)
        e1, soft1 = m.sb("e1", TT * E), m.sb("soft1", TT * EX)
        top8, rest = m.sb("top8", TT * 8), m.sb("rest", TT * EX)
        kept = m.sb("kept", TT * E)
        keptT = m.sb("keptT", CT, F32, E)
        unused, e2 = m.sb("unused", TT * FK), m.sb("e2", TT * FK)
        top2, mass2, part2 = m.sb("top2", TT * F), m.sb("mass2", TT * F), m.sb("part2", TT * F)
        soft2 = m.sb("soft2", TT * GROUPS * MR)
        softT32 = m.sb("softT32", GROUPS * CT, F32, GR)
        silu = [m.sb(f"silu{n}", CT) for n in range(2)]
        inner = [m.sb(f"inner{n}", CT) for n in range(2)]
        innerT = [[m.split(f"inner{n}_{k}", CT) for k in range(SI)] for n in range(2)]

        gate_bank = [m.bank(f"gate{n}") for n in range(2)]
        up_bank = [m.bank(f"up{n}") for n in range(2)]
        y_bank = [m.bank(f"y{n}") for n in range(2)]
        token_bank, turned_bank = m.bank("token"), m.bank("turned")
        soft_bank = [turned_bank, y_bank[1]]

        small_in = m.sem("small_in")
        inv_ready, onehot_ready, sentinels = m.sem("inv_ready"), m.sem("onehot_ready"), m.sem("sentinels")
        logit_ready, top1_ready, less1_ready, exp1_ready = (
            m.sem("logit_ready"), m.sem("top1_ready"), m.sem("less1_ready"), m.sem("exp1_ready"))
        mass1_ready, part1_ready, soft1_ready, top8_ready, rest_ready, kept_ready = (
            m.sem("mass1_ready"), m.sem("part1_ready"), m.sem("soft1_ready"), m.sem("top8_ready"),
            m.sem("rest_ready"), m.sem("kept_ready"))
        kept_turned, keptT_ready, flat_ready = m.sem("kept_turned"), m.sem("keptT_ready"), m.sem("flat_ready")
        unused_ready, masked_ready, top2_ready, less2_ready, exp2_ready, mass2_ready, part2_ready, soft2_ready = (
            m.sem("unused_ready"), m.sem("masked_ready"), m.sem("top2_ready"), m.sem("less2_ready"),
            m.sem("exp2_ready"), m.sem("mass2_ready"), m.sem("part2_ready"), m.sem("soft2_ready"))
        soft_turned, softT_hi, softT32_ready, softT_lo, stored = (
            m.sem("soft_turned"), m.sem("softT_hi"), m.sem("softT32_ready"), m.sem("softT_lo"), m.sem("stored"))
        up_ready, silu_ready, inner_ready, inner_hi, inner_lo = (
            m.sem("up_ready"), m.sem("silu_ready"), m.sem("inner_ready"), m.sem("inner_hi"), m.sem("inner_lo"))
        y_ready, r_ready, x32_ready = m.sem("y_ready"), m.sem("r_ready"), m.sem("x32_ready")
        expert_in, expert_scaled, expert_hi, expert_lo, expert_ready = (
            m.sem("expert_in"), m.sem("expert_scaled"), m.sem("expert_hi"), m.sem("expert_lo"), m.sem("expert_ready"))

        wide = lambda t, n, w: t[:, :].rearrange("p (t o) -> p t o", o=1).to_broadcast([P, n, w])
        tok3 = token_bank[:, 0:TT * E].rearrange("p (t e) -> p t e", t=TT)
        tok8 = token_bank[:, 0:TT * FK].rearrange("p (t k) -> p t k", k=F)
        e2_8 = e2[:, :].rearrange("p (t k) -> p t k", k=F)
        s3 = soft1[:, :].rearrange("p (t e) -> p t e", t=TT)
        rest3 = rest[:, :].rearrange("p (t e) -> p t e", t=TT)

        block = m.ctx.enter_context(nc.Block())

        @block.sync
        def _(sp):
            sp.dma_start(inv_raw[:, :], a["inv"].rearrange("(o e) -> o e", o=1).to_broadcast([E, FK])).then_inc(small_in, 16)
            sp.dma_start(rows[:, :], a["rows"]).then_inc(small_in, 16)
            load_weights(sp, a, 0, stage, scale, expert_in)
            by_parity = soft_dram.rearrange("(f two k) t -> two f k t", two=GROUPS, k=F)
            for c in range(CHUNKS):
                for n in range(GROUPS):
                    sp.wait_ge(softT32_ready, GROUPS * c + n + 1)
                    sp.dma_start(by_parity[n, :, :, c * CT:(c + 1) * CT], softT32[:, n * CT:(n + 1) * CT]).then_inc(stored, 16)
                if c == 2:
                    sp.wait_ge(expert_ready, 1)
                    load_weights(sp, a, 1, stage, scale, expert_in)
            sp.wait_ge(stored, 16 * GROUPS * CHUNKS)
            sp.wait_ge(expert_in, 64)

        @block.gpsimd
        def _(pool):
            whole(pool, xT, xT32, CHUNKS - 1).then_inc(x32_ready, 1)
            for c in range(CHUNKS):
                if c == 2:
                    pool.wait_ge(expert_in, 32)
                    scale_weights(pool, stage, scale, expert_scaled, 0)
                    pool.wait_ge(expert_scaled, 2)
                    pool.tensor_copy(W0.hi[:, :], stage[:, :]).then_inc(expert_hi, 1)
                    pool.wait_ge(expert_hi, 1)
                    split_low(pool, stage, W0, expert_lo, expert_ready, 1)
                for k in range(SI):
                    u = c * SI + k
                    pool.wait_ge(inner_hi, u + 1)
                    pool.tensor_tensor(innerT[c % 2][k].lo[:, :], inner[u % 2][:, :],
                                       innerT[c % 2][k].hi[:, :].bitcast(F32), ALU.subtract).then_inc(inner_lo, 1)

        @block.tensor
        def _(pe):
            def shared_in(c, k):
                u = c * SI + k
                if u >= 2:
                    pe.wait_ge(inner_ready, u - 1)
                for W_, bank in ((Wg, gate_bank), (Wu, up_bank)):
                    for d in range(DK):
                        mm = product(pe, bank[u % 2][:, :], W_[:, (d * SI + k) * P:(d * SI + k + 1) * P],
                                     xT[:, d * B * S + c * CT:d * B * S + (c + 1) * CT], first=d == 0, last=d == DK - 1)
                mm.then_inc(up_ready, 1)

            def shared_out(c):
                pe.wait_ge(inner_lo, SI * (c + 1))
                for i in range(2):
                    if i:
                        pe.wait_ge(softT_lo, GROUPS * (c + 1))
                    if c:
                        pe.wait_ge(r_ready, 2 * (c - 1) + i + 1)
                    for j in range(2):
                        t = 2 * i + j
                        for k in range(SI):
                            mm = product(pe, y_bank[i][:, j * D:(j + 1) * D], innerT[c % 2][k][:, t * P:(t + 1) * P],
                                         Wd[:, k * D:(k + 1) * D], first=k == 0, last=k == SI - 1)
                    mm.then_inc(y_ready, 1)

            def soft_out(c, n):
                if n and c:
                    pe.wait_ge(r_ready, 2 * c)
                bank = soft_bank[n]
                if n == 0:
                    pe.wait_ge(soft2_ready, c + 1)
                for t in range(TT):
                    at = (t * GROUPS + n) * MR
                    mm = pe.transpose(bank[0:MR, t * P:(t + 1) * P], soft2[:, at:at + MR], ident[:, :])
                mm.then_inc(soft_turned, 1)

            for c in range(CHUNKS):
                if c == CHUNKS - 1:
                    pe.wait_ge(x32_ready, 1)
                if c:
                    pe.wait_ge(masked_ready, c)
                for t in range(TT):
                    for d in range(DK):
                        at = d * B * S + c * CT + t * P
                        mm = pe.matmul(token_bank[:, t * E:(t + 1) * E], xT32[:, at:at + P], Wr[:, d * E:(d + 1) * E],
                                       start=d == 0, stop=d == DK - 1)
                mm.then_inc(logit_ready, 1)
                shared_in(c, 0)
                if c:
                    for n in range(GROUPS):
                        soft_out(c - 1, n)
                shared_in(c, 1)
                pe.wait_ge(kept_ready, c + 1)
                if c:
                    pe.wait_ge(softT_lo, GROUPS * c - 1)
                for t in range(TT):
                    mm = pe.transpose(turned_bank[0:E, t * P:(t + 1) * P], kept[:, t * E:(t + 1) * E], ident[:, :])
                mm.then_inc(kept_turned, 1)
                shared_in(c, 2)
                pe.wait_ge(keptT_ready, c + 1)
                pe.wait_ge(onehot_ready, 1)
                for t in range(TT):
                    mm = pe.matmul(token_bank[:, t * FK:(t + 1) * FK], keptT[:, t * P:(t + 1) * P], onehot[:, :],
                                   start=True, stop=True)
                mm.then_inc(flat_ready, 1)
                if c:
                    shared_out(c - 1)
            for n in range(GROUPS):
                soft_out(CHUNKS - 1, n)
            shared_out(CHUNKS - 1)

        @block.scalar
        def _(act):
            def shared(c, k):
                u = c * SI + k
                act.wait_ge(up_ready, u + 1)
                if u >= 2:
                    act.wait_ge(inner_ready, u - 1)
                act.activation(silu[u % 2][:, :], gate_bank[u % 2][:, :], ACT.Silu).then_inc(silu_ready, 1)
                if k == 0 and c:
                    soft_high(c - 1)
                act.wait_ge(inner_ready, u + 1)
                if c >= 2:
                    act.wait_ge(y_ready, 2 * (c - 1))
                act.activation(innerT[c % 2][k].hi[:, :], inner[u % 2][:, :], ACT.Copy).then_inc(inner_hi, 1)

            def soft_high(c):
                for n in range(GROUPS):
                    act.wait_ge(soft_turned, GROUPS * c + n + 1)
                    act.activation(softT[n][0:MR, c * CT:(c + 1) * CT], soft_bank[n][0:MR, :], ACT.Copy).then_inc(softT_hi, 1)

            for c in range(CHUNKS):
                act.wait_ge(less1_ready, c + 1)
                act.activation(e1[:, :], e1[:, :], ACT.Exp).then_inc(exp1_ready, 1)
                for k in range(SI):
                    shared(c, k)
                act.wait_ge(less2_ready, c + 1)
                act.activation(e2[:, :], e2[:, :], ACT.Exp).then_inc(exp2_ready, 1)
            soft_high(CHUNKS - 1)

        @block.vector
        def _(dve):
            dve.wait_ge(small_in, 32)
            dve.tensor_copy(inv[:, :], inv_raw[:, :]).then_inc(inv_ready, 1)
            dve.wait_ge(inv_ready, 1)
            dve.tensor_scalar(onehot[:, :], inv[:, :], rows[:, 0:1], None, ALU.is_equal).then_inc(onehot_ready, 1)
            dve.memset(s3[:, :, E:E + 1], 3.0).then_inc(sentinels, 1)
            dve.memset(s3[:, :, E + 1:E + 2], 2.0).then_inc(sentinels, 1)
            dve.wait_ge(sentinels, 2)

            def shared(c, k):
                u = c * SI + k
                dve.wait_ge(silu_ready, u + 1)
                if u >= 2:
                    dve.wait_ge(inner_lo, u - 1)
                dve.tensor_tensor(inner[u % 2][:, :], up_bank[u % 2][:, :], silu[u % 2][:, :], ALU.mult).then_inc(inner_ready, 1)

            def shared_out(c):
                for i in range(2):
                    t = c * TT + 2 * i
                    dve.wait_ge(y_ready, 2 * c + i + 1)
                    two = r[:, t * D:(t + 2) * D]
                    dve.tensor_tensor(two, y_bank[i][:, :], two, ALU.add).then_inc(r_ready, 1)

            def split_soft(c, n):
                dve.wait_ge(softT_hi, GROUPS * c + n + 1)
                at = (slice(GR, 2 * GR), slice(c * CT, (c + 1) * CT))
                if c:
                    dve.wait_ge(stored, 16 * GROUPS * c)
                dve.tensor_copy(softT32[:, n * CT:(n + 1) * CT], soft_bank[n][0:GR, :]).then_inc(softT32_ready, 1)
                dve.tensor_tensor(softT[n][at], soft_bank[n][GR:2 * GR, :], softT[n][at].bitcast(F32), ALU.subtract
                                  ).then_inc(softT_lo, 1)

            for c in range(CHUNKS):
                n = c + 1
                dve.wait_ge(logit_ready, n)
                dve.tensor_reduce(top1[:, :], tok3, AX.X, ALU.max).then_inc(top1_ready, 1)
                dve.wait_ge(top1_ready, n)
                dve.tensor_tensor(e1[:, :].rearrange("p (t e) -> p t e", t=TT), tok3, wide(top1, TT, E), ALU.subtract
                                  ).then_inc(less1_ready, 1)
                if c >= 2:
                    shared_out(c - 2)
                dve.wait_ge(exp1_ready, n)
                e13 = e1[:, :].rearrange("p (t e) -> p t e", t=TT)
                dve.tensor_reduce(mass[:, :], e13, AX.X, ALU.add).then_inc(mass1_ready, 1)
                dve.wait_ge(mass1_ready, n)
                dve.reciprocal(part[:, :], mass[:, :]).then_inc(part1_ready, 1)
                dve.wait_ge(part1_ready, n)
                dve.tensor_tensor(s3[:, :, 0:E], e13, wide(part, TT, E), ALU.mult).then_inc(soft1_ready, 1)
                dve.wait_ge(soft1_ready, n)
                for t in range(TT):
                    ins = dve.max(top8[:, t * 8:(t + 1) * 8], soft1[:, t * EX:(t + 1) * EX])
                ins.then_inc(top8_ready, 1)
                dve.wait_ge(top8_ready, n)
                for t in range(TT):
                    ins = dve.match_replace(rest[:, t * EX:(t + 1) * EX], top8[:, t * 8:(t + 1) * 8],
                                            soft1[:, t * EX:(t + 1) * EX], 0.0)
                ins.then_inc(rest_ready, 1)
                dve.wait_ge(rest_ready, n)
                dve.tensor_tensor(kept[:, :].rearrange("p (t e) -> p t e", t=TT), s3[:, :, 0:E], rest3[:, :, 0:E],
                                  ALU.subtract).then_inc(kept_ready, 1)
                if c:
                    split_soft(c - 1, 0)
                shared(c, 0)
                if c:
                    split_soft(c - 1, 1)
                shared(c, 1)
                dve.wait_ge(kept_turned, n)
                dve.tensor_copy(keptT[:, :], turned_bank[0:E, :]).then_inc(keptT_ready, 1)
                shared(c, 2)
                dve.wait_ge(flat_ready, n)
                dve.tensor_reduce(share_of[:, c * TT * F:(c + 1) * TT * F], tok8, AX.X, ALU.add)
                dve.tensor_scalar(unused[:, :], token_bank[:, 0:TT * FK], 0.0, -1e9, ALU.is_equal, ALU.mult
                                  ).then_inc(unused_ready, 1)
                dve.wait_ge(unused_ready, n)
                dve.tensor_tensor(e2[:, :], token_bank[:, 0:TT * FK], unused[:, :], ALU.add).then_inc(masked_ready, 1)
                dve.wait_ge(masked_ready, n)
                dve.tensor_reduce(top2[:, :], e2_8, AX.X, ALU.max).then_inc(top2_ready, 1)
                dve.wait_ge(top2_ready, n)
                dve.tensor_tensor(e2_8, e2_8, wide(top2, TT * F, F), ALU.subtract).then_inc(less2_ready, 1)
                dve.wait_ge(exp2_ready, n)
                dve.tensor_reduce(mass2[:, :], e2_8, AX.X, ALU.add).then_inc(mass2_ready, 1)
                dve.wait_ge(mass2_ready, n)
                dve.reciprocal(part2[:, :], mass2[:, :]).then_inc(part2_ready, 1)
                dve.wait_ge(part2_ready, n)
                four = lambda t: t.rearrange("p (t f k) -> p t f k", t=TT * GROUPS, f=F // GROUPS)
                if c:
                    dve.wait_ge(soft_turned, GROUPS * c)
                for copy in range(3):
                    to = soft2[:, :].rearrange("p (t n c) -> p n t c", t=TT * GROUPS, n=3)[:, copy]
                    ins = dve.tensor_tensor(to.rearrange("p t (f k) -> p t f k", k=F), four(e2[:, :]),
                                            four(part2[:, :]).to_broadcast([P, TT * GROUPS, F // GROUPS, F]), ALU.mult)
                ins.then_inc(soft2_ready, 1)
            shared_out(CHUNKS - 2)
            for n in range(GROUPS):
                split_soft(CHUNKS - 1, n)
            shared_out(CHUNKS - 1)


def experts(nc, a, r, stats, xT, xT32, softT, share_of, soft_dram, stage, scale, W0):
    m = Memory(nc, "moe")
    UNITS = 2 * CHUNKS
    with m.ctx:
        W = [W0, m.split("W1", WCOLS)]
        xe32 = m.sb("xe32", DK * CT)
        place = lambda part, n: part[:, n * 2 * CT:(n + 1) * 2 * CT]
        xe = [Split(place(xT.hi, 2 * n), place(xT.hi, 2 * n + 1)) for n in range(2)]
        spread = [m.sb(f"spread{c}", CT) for c in range(CHUNKS)]
        low32 = m.sb("low32", CT)
        low = m.split("low", CT)
        low_pair = m.sb("low_pair", 2 * CT, F32R)
        silu, inner = m.sb("silu", 2 * CT), m.sb("inner", 2 * CT)
        innerT = [Split(place(xT.lo, 2 * n), place(xT.lo, 2 * n + 1)) for n in range(2)]
        dlow32 = m.sb("dlow32", CT, parts=KR)
        shares = m.sb("shares", 2 * B)
        mv, var, std, rstd = m.sb("mv", B * 2), m.sb("var", B), m.sb("std", B), m.sb("rstd", B)
        shift = m.sb("shift", B)

        gu = [m.bank(f"gu{n}") for n in range(3)]
        dlow_bank, low_bank, xe_bank = m.bank("dlow"), m.bank("low"), m.bank("xe")
        y_bank = [m.bank(f"y{n}") for n in range(2)]
        feat = [xe_bank, dlow_bank]

        w_in, w_scaled, w_hi, w_lo, w_ready = (
            m.sem("w_in"), m.sem("w_scaled"), m.sem("w_hi"), m.sem("w_lo"), m.sem("w_ready"))
        spread_in = [m.sem(f"spread_in{c}") for c in range(CHUNKS)]
        xe_ready, xe32_ready, xe_hi, xe_lo = m.sem("xe_ready"), m.sem("xe32_ready"), m.sem("xe_hi"), m.sem("xe_lo")
        low_ready, low32_ready, low_hi, low_lo = m.sem("low_ready"), m.sem("low32_ready"), m.sem("low_hi"), m.sem("low_lo")
        pair_hi, pair_ready = m.sem("pair_hi"), m.sem("pair_ready")
        gu_ready, silu_ready, inner_ready = m.sem("gu_ready"), m.sem("silu_ready"), m.sem("inner_ready")
        inner_hi, inner_lo, low_moved = m.sem("inner_hi"), m.sem("inner_lo"), m.sem("low_moved")
        dlow_ready, dlow32_ready, dlow_hi, dlow_lo = (
            m.sem("dlow_ready"), m.sem("dlow32_ready"), m.sem("dlow_hi"), m.sem("dlow_lo"))
        y_ready, r_ready, shares_ready = m.sem("y_ready"), m.sem("r_ready"), m.sem("shares_ready")
        stats_ready, mv_ready, var_ready, std_ready, rstd_ready, shift_ready = (
            m.sem("stats_ready"), m.sem("mv_ready"), m.sem("var_ready"), m.sem("std_ready"), m.sem("rstd_ready"),
            m.sem("shift_ready"))
        even_ready, odd_ready, stored = m.sem("even_ready"), m.sem("odd_ready"), m.sem("stored")

        mv2 = mv[:, :].rearrange("p (t s) -> p t s", s=2)
        tile = lambda t: r[:, t * D:(t + 1) * D]
        tiles = lambda c: slice(c * TT, (c + 1) * TT)
        out = a["out"].rearrange("b s d -> s b d")
        NORM = (range(0, CHUNKS - 1), range(CHUNKS - 1, CHUNKS))
        TURNS_E = F // 2
        LAST = TURNS_E - 1
        PAIRS = ((slice(0, KR), slice(KR, P), slice(0, CT)), (slice(KR, P), slice(0, KR), slice(CT, 2 * CT)))
        FEATURES = ((slice(0, P), slice(0, CT)), (slice(KR, B2), slice(CT, 2 * CT)))
        block = m.ctx.enter_context(nc.Block())

        def count(g, u):
            return g * UNITS + u

        @block.sync
        def _(sp):
            def load_spread(e, c):
                for half in range(2):
                    sp.dma_start(spread[c][half * KR:(half + 1) * KR, :],
                                 soft_dram[bass.ds(e * F, F), c * CT:(c + 1) * CT].rearrange("(k o) t -> k o t", o=1)
                                 .to_broadcast([F, R, CT])).then_inc(spread_in[c], 16)

            for c in range(CHUNKS):
                load_spread(0, c)

            def turn(g, last):
                for u in range(CHUNKS if last else UNITS):
                    sp.wait_ge(dlow32_ready, count(g, u + 1))
                    load_spread(g * 2 + u // CHUNKS + 1, u % CHUNKS)
                    if u in (0, CHUNKS) and not last:
                        e = g * 2 + 2 + u // CHUNKS
                        sp.wait_ge(w_ready, e - 1)
                        load_weights(sp, a, e, stage, scale, w_in)

            with sp.Fori(0, LAST) as g:
                turn(g, False)
            turn(LAST, True)
            for c in range(CHUNKS):
                sp.wait_ge(even_ready, TT // 2 * (c + 1))
                sp.wait_ge(odd_ready, TT // 2 * (c + 1))
                sp.dma_start(out[:, tiles(c), :], r[:, c * TT * D:(c + 1) * TT * D].rearrange("p (b d) -> p b d", b=TT)
                             ).then_inc(stored, 16)
            sp.wait_ge(stored, 16 * CHUNKS)

        @block.gpsimd
        def _(pool):
            def scale_next(e, first=False):
                if not first:
                    pool.wait_ge(w_in, e * 32 - 32)
                scale_weights(pool, stage, scale, w_scaled, e * 2 - 2)

            def split_weights(n, e):
                pool.wait_ge(w_hi, e)
                split_low(pool, stage, W[n], w_lo, w_ready, e)

            def xe_low(g, u):
                pool.wait_ge(xe_hi, count(g, u + 1))
                pool.tensor_tensor(xe[u % 2].lo[:, :], xe32[:, :], xe[u % 2].hi[:, :].bitcast(F32), ALU.subtract
                                   ).then_inc(xe_lo, 1)

            def inner_low(g, u, k):
                pool.wait_ge(inner_hi, 2 * count(g, u) + k + 1)
                at = FEATURES[k]
                if k:
                    pool.wait_ge(inner_lo, 2 * count(g, u) + 1)
                pool.tensor_tensor(innerT[u % 2].lo[at], inner[at], innerT[u % 2].hi[at].bitcast(F32), ALU.subtract
                                   ).then_inc(inner_lo, 1)

            scale_next(1, True)
            pool.wait_ge(w_scaled, 2)
            xe_low(0, 1)

            def turn(g, first, last):
                for u in range(UNITS):
                    for k in range(2):
                        inner_low(g, u, k)
                    pool.wait_ge(inner_lo, 2 * count(g, u + 1))
                    if not (last and u >= UNITS - 2):
                        xe_low(g, u + 2)
                    if u == 0:
                        split_weights(1, g * 2 + 1)
                    if u == CHUNKS and not last:
                        split_weights(0, g * 2 + 2)
                    if u in (CHUNKS - 1, UNITS - 1) and not last:
                        e = g * 2 + 2 + u // CHUNKS
                        scale_next(e)
                        pool.wait_ge(w_scaled, e * 2)

            turn(0, True, False)
            with pool.Fori(1, LAST) as g:
                turn(g, False, False)
            turn(LAST, False, True)

        @block.tensor
        def _(pe):
            def inputs(g, u, slot):
                c = u % CHUNKS
                for k in range(DK):
                    pe.matmul(feat[k][:, :], W[slot].hi[0:MR, MU_AT + k * P:MU_AT + (k + 1) * P],
                              softT[slot][0:MR, c * CT:(c + 1) * CT], start=True, stop=True
                              ).then_inc(xe_ready, 1)

            def low_rank(g, u, slot):
                for k in range(DK):
                    mm = product(pe, low_bank[:, :], W[slot][:, QA_AT + k * P:QA_AT + (k + 1) * P],
                                 xe[u % 2][:, k * CT:(k + 1) * CT], first=k == 0, last=k == DK - 1)
                mm.then_inc(low_ready, 1)

            def gate_up(g, u, slot, first):
                w, x = W[slot], xe[u % 2]
                for n, rows in ((0, P), (1, P), (2, B2)):
                    if not first:
                        pe.wait_ge(inner_ready, 2 * count(g, u) - (n < 2))
                    for k in range(DK):
                        at = GU_AT + k * GUB + n * P
                        product(pe, gu[n][0:rows, :], w[:, at:at + rows], x[:, k * CT:(k + 1) * CT], first=k == 0, last=False)
                    at = slice(QB_AT + n * P, QB_AT + n * P + rows)
                    if n < 2:
                        hi, _, cols = PAIRS[n]
                        pe.wait_ge(pair_ready, 2 * count(g, u) + n + 1)
                        pe.matmul(gu[n][:, :], w.hi[:, at], low_pair[:, cols], start=False, stop=False)
                        mm = pe.matmul(gu[n][:, :], w.lo[hi, at], low_pair[hi, cols], start=False, stop=True)
                    else:
                        pe.wait_ge(low_lo, count(g, u + 1))
                        mm = product(pe, gu[n][0:rows, :], w[:, at], low[:, :], first=False)
                    mm.then_inc(gu_ready, 1)

            def down_low(g, u, slot):
                pe.wait_ge(low_moved, count(g, u + 1))
                w, x = W[slot], innerT[u % 2]
                product(pe, dlow_bank[0:KR, :], w[:, DQ_AT:DQ_AT + KR], x[:, 0:CT], last=False)
                qa = slice(DQ_AT + KR, DQ_AT + 2 * KR)
                pe.matmul(dlow_bank[0:KR, :], w.hi[0:B2, qa], x.hi[0:B2, CT:2 * CT], start=False, stop=False)
                pe.matmul(dlow_bank[0:KR, :], w.lo[KR:B2, qa], x.hi[KR:B2, CT:2 * CT], start=False, stop=True
                          ).then_inc(dlow_ready, 1)

            def down(g, u, slot, first):
                for k, at, rows in ((0, D1_AT, P), (1, D2_AT, B2)):
                    if k:
                        pe.wait_ge(dlow_lo, count(g, u + 1))
                    for i in range(2):
                        if not first and k == 0:
                            pe.wait_ge(r_ready, 4 * count(g, u) - 2 + 2 * i)
                        for j in range(2):
                            t = 2 * i + j
                            mm = product(pe, y_bank[i][:, j * D:(j + 1) * D],
                                         innerT[u % 2][0:rows, k * CT + t * P:k * CT + (t + 1) * P],
                                         W[slot][0:rows, at:at + D], first=k == 0 and j == 0, last=k == 1,
                                         skip_group_check=True)
                        if k:
                            mm.then_inc(y_ready, 1)

            def turn(g, first, last):
                for u in range(UNITS):
                    before = not (first and u == 0)
                    gate_up(g, u, u // CHUNKS, not before)
                    if before:
                        pe.wait_ge(xe32_ready, 2 * count(g, u + (1 if last and u == UNITS - 1 else 2)))
                        down_low(g, u - 1, (u - 1) // CHUNKS % 2)
                    if not (last and u == UNITS - 1):
                        pe.wait_ge(xe_lo, count(g, u + 2))
                        low_rank(g, u + 1, (u + 1) // CHUNKS % 2)
                    if not (last and u >= UNITS - 2):
                        if u in (2, CHUNKS + 2):
                            pe.wait_ge(w_ready, g * 2 + (1 if u == 2 else 2))
                        if before:
                            pe.wait_ge(dlow32_ready, count(g, u))
                        inputs(g, u + 2, (u + 2) // CHUNKS % 2)
                    if before:
                        down(g, u - 1, (u - 1) // CHUNKS % 2, first and u == 1)

            inputs(0, 0, 0)
            pe.wait_ge(xe32_ready, 2)
            inputs(0, 1, 0)
            pe.wait_ge(xe_lo, 1)
            low_rank(0, 0, 0)
            turn(0, True, False)
            with pe.Fori(1, LAST) as g:
                turn(g, False, False)
            turn(LAST, False, True)
            down_low(LAST, UNITS - 1, 1)
            down(LAST, UNITS - 1, 1, False)

        @block.scalar
        def _(act):
            def xe_high(g, u):
                act.wait_ge(xe32_ready, 2 * count(g, u + 1))
                act.activation(xe[u % 2].hi[:, :], xe32[:, :], ACT.Copy).then_inc(xe_hi, 1)

            def low_high(g, u):
                act.wait_ge(low32_ready, count(g, u + 1))
                for hi, _, cols in PAIRS:
                    act.activation(low_pair[hi, cols], low32[hi, :], ACT.Copy).then_inc(pair_hi, 1)
                act.activation(low.hi[:, :], low32[:, :], ACT.Copy).then_inc(low_hi, 1)

            def dlow_high(g, u):
                act.wait_ge(dlow32_ready, count(g, u + 1))
                act.activation(innerT[u % 2].hi[0:KR, CT:2 * CT], dlow32[:, :], ACT.Copy).then_inc(dlow_hi, 1)

            def move_low(g, u):
                act.wait_ge(inner_lo, 2 * count(g, u + 1))
                act.activation(innerT[u % 2].hi[0:I2, CT:2 * CT], innerT[u % 2].lo[KR:B2, CT:2 * CT].bitcast(F32), ACT.Copy
                               ).then_inc(low_moved, 1)

            def weights_high(n, e, first=False):
                act.wait_ge(w_scaled, e * 2)
                if not first:
                    act.wait_ge(y_ready, 2 * CHUNKS * (e - 1))
                act.activation(W[n].hi[:, :], stage[:, :], ACT.Copy).then_inc(w_hi, 1)

            xe_high(0, 0)
            xe_high(0, 1)
            low_high(0, 0)

            def turn(g, first, last):
                for u in range(UNITS):
                    if not (first and u == 0):
                        move_low(g, u - 1)
                    for k, n in ((0, 0), (1, 2)):
                        rows, cols = FEATURES[k]
                        act.wait_ge(gu_ready, 3 * count(g, u) + n + 1)
                        act.activation(silu[rows, cols], gu[n][rows, :], ACT.Silu).then_inc(silu_ready, 1)
                        act.wait_ge(inner_ready, 2 * count(g, u) + k + 1)
                        if k == 0 and not (first and u < 2):
                            act.wait_ge(y_ready, 2 * count(g, u - 1))
                        act.activation(innerT[u % 2].hi[rows, cols], inner[rows, cols], ACT.Copy).then_inc(inner_hi, 1)
                    if not (first and u == 0):
                        dlow_high(g, u - 1)
                    if not (last and u == UNITS - 1):
                        low_high(g, u + 1)
                    if not (last and u >= UNITS - 2):
                        xe_high(g, u + 2)
                    if u == CHUNKS and not last:
                        weights_high(0, g * 2 + 2)
                    if u == 0:
                        weights_high(1, g * 2 + 1, first)

            turn(0, True, False)
            with act.Fori(1, LAST) as g:
                turn(g, False, False)
            turn(LAST, False, True)
            move_low(LAST, UNITS - 1)
            dlow_high(LAST, UNITS - 1)
            for n, group in enumerate(NORM):
                at = slice(group[0] * TT, (group[-1] + 1) * TT)
                act.wait_ge(var_ready, group[-1] + 1)
                act.activation(std[:, at], var[:, at], ACT.Sqrt).then_inc(std_ready, 1)
                act.wait_ge(shift_ready, n + 1)
                for t in range(at.start + 1, at.stop, 2):
                    act.activation(tile(t), tile(t), ACT.Identity, bias=shift[:, t:t + 1], scale=rstd[:, t:t + 1]
                                   ).then_inc(odd_ready, 1)

        @block.vector
        def _(dve):
            def xe_sum(g, u):
                c = u % CHUNKS
                for k in range(DK):
                    dve.wait_ge(xe_ready, 2 * count(g, u) + k + 1)
                    dve.tensor_tensor(xe32[:, k * CT:(k + 1) * CT], feat[k][:, :],
                                      xT32[:, k * B * S + c * CT:k * B * S + (c + 1) * CT], ALU.add).then_inc(xe32_ready, 1)

            def low_product(g, u):
                c = u % CHUNKS
                dve.wait_ge(low_ready, count(g, u + 1))
                dve.wait_ge(spread_in[c], (g * 2 + u // CHUNKS) * 32 + 32)
                dve.tensor_tensor(low32[:, :], low_bank[:, :], spread[c][:, :], ALU.mult).then_inc(low32_ready, 1)

            def low_low(g, u):
                for n, (hi, lo, cols) in enumerate(PAIRS):
                    dve.wait_ge(pair_hi, 2 * count(g, u) + n + 1)
                    dve.tensor_tensor(low_pair[lo, cols], low32[hi, :], low_pair[hi, cols].bitcast(F32), ALU.subtract
                                      ).then_inc(pair_ready, 1)
                dve.wait_ge(low_hi, count(g, u + 1))
                dve.tensor_tensor(low.lo[:, :], low32[:, :], low.hi[:, :].bitcast(F32), ALU.subtract).then_inc(low_lo, 1)

            def dlow_product(g, u):
                c = u % CHUNKS
                dve.wait_ge(dlow_ready, count(g, u + 1))
                dve.tensor_tensor(dlow32[:, :], dlow_bank[0:KR, :], spread[c][0:KR, :], ALU.mult).then_inc(dlow32_ready, 1)

            def dlow_low(g, u):
                dve.wait_ge(dlow_hi, count(g, u + 1))
                at = (slice(0, KR), slice(CT, 2 * CT))
                dve.tensor_tensor(innerT[u % 2].lo[at], dlow32[:, :], innerT[u % 2].hi[at].bitcast(F32), ALU.subtract
                                  ).then_inc(dlow_lo, 1)

            def inner_product(g, u, k, first):
                rows, cols = FEATURES[k]
                dve.wait_ge(silu_ready, 2 * count(g, u) + k + 1)
                if k == 0:
                    dve.wait_ge(gu_ready, 3 * count(g, u) + 2)
                if not first:
                    dve.wait_ge(inner_lo, 2 * count(g, u) - 1 + k)
                up = gu[1][:, :] if k == 0 else gu[2][0:I2, :]
                dve.tensor_tensor(inner[rows, cols], up, silu[rows, cols], ALU.mult).then_inc(inner_ready, 1)

            def add_output(g, u):
                e, c = u // CHUNKS % 2, u % CHUNKS
                for t in range(TT):
                    if t % 2 == 0:
                        dve.wait_ge(y_ready, 2 * count(g, u) + t // 2 + 1)
                    at = c * TT + t
                    here = r[:, at * D:(at + 1) * D]
                    dve.scalar_tensor_tensor(here, y_bank[t // 2][:, t % 2 * D:(t % 2 + 1) * D],
                                             shares[:, e * B + at:e * B + at + 1], here, ALU.mult, ALU.add
                                             ).then_inc(r_ready, 1)

            def variance(c):
                dve.wait_ge(r_ready, TT * count(LAST, CHUNKS + c + 1))
                for t in range(c * TT, (c + 1) * TT):
                    ins = dve.bn_stats(stats[:, 6 * t:6 * t + 6], tile(t))
                ins.then_inc(stats_ready, 1)
                dve.wait_ge(stats_ready, c + 1)
                for t in range(c * TT, (c + 1) * TT):
                    ins = dve.bn_aggr(mv[:, 2 * t:2 * t + 2], stats[:, 6 * t:6 * t + 6])
                ins.then_inc(mv_ready, 1)
                dve.wait_ge(mv_ready, c + 1)
                dve.tensor_scalar(var[:, tiles(c)], mv2[:, tiles(c), 1], LN_EPS, None, ALU.add).then_inc(var_ready, 1)

            def factors(n):
                at = slice(NORM[n][0] * TT, (NORM[n][-1] + 1) * TT)
                dve.wait_ge(std_ready, n + 1)
                dve.reciprocal(rstd[:, at], std[:, at]).then_inc(rstd_ready, 1)
                dve.wait_ge(rstd_ready, n + 1)
                dve.scalar_tensor_tensor(shift[:, at], mv2[:, at, 0], -1.0, rstd[:, at], ALU.mult, ALU.mult
                                         ).then_inc(shift_ready, 1)

            def normalise(n):
                for t in range(NORM[n][0] * TT, (NORM[n][-1] + 1) * TT, 2):
                    dve.tensor_scalar(tile(t), tile(t), mv[:, 2 * t:2 * t + 1], rstd[:, t:t + 1], ALU.subtract, ALU.mult
                                      ).then_inc(even_ready, 1)

            xe_sum(0, 0)
            dve.wait_ge(xe_hi, 1)
            dve.tensor_tensor(xe[0].lo[:, :], xe32[:, :], xe[0].hi[:, :].bitcast(F32), ALU.subtract).then_inc(xe_lo, 1)
            dve.wait_ge(xe_lo, 1)
            xe_sum(0, 1)
            low_product(0, 0)
            low_low(0, 0)

            def turn(g, first, last):
                for u in range(UNITS):
                    if not (first and u < 2):
                        add_output(g, u - 2)
                    if last and u >= CHUNKS + 2:
                        variance(u - 2 - CHUNKS)
                    if u == 1:
                        if not first:
                            dve.wait_ge(r_ready, 4 * count(g, 0))
                        dve.tensor_copy(shares[:, :].rearrange("p (e t) -> p e t", e=2),
                                        share_of[:, :].rearrange("p (t n e) -> p e n t", t=B, n=GROUPS)
                                        [:, bass.ds(g, 1)].rearrange("p o n t -> p (o n) t")
                                        ).then_inc(shares_ready, 1)
                        dve.wait_ge(shares_ready, g + 1)
                    inner_product(g, u, 0, first and u == 0)
                    inner_product(g, u, 1, first and u == 0)
                    if not (first and u == 0):
                        dlow_product(g, u - 1)
                        dlow_low(g, u - 1)
                    if not (last and u == UNITS - 1):
                        low_product(g, u + 1)
                    if not (last and u >= UNITS - 2):
                        dve.wait_ge(xe_lo, count(g, u + 2))
                        xe_sum(g, u + 2)
                    if not (last and u == UNITS - 1):
                        low_low(g, u + 1)

            turn(0, True, False)
            with dve.Fori(1, LAST) as g:
                turn(g, False, False)
            turn(LAST, False, True)
            add_output(LAST, UNITS - 2)
            dlow_product(LAST, UNITS - 1)
            dlow_low(LAST, UNITS - 1)
            variance(CHUNKS - 2)
            factors(0)
            add_output(LAST, UNITS - 1)
            variance(CHUNKS - 1)
            normalise(0)
            factors(1)
            normalise(1)


def program(nc, a):
    m = Memory(nc, "all")
    with m.ctx:
        r = m.sb("r", B * D)
        stats = m.sb("stats", B * 6)
        ident = m.sb("ident", P)
        cross_w = m.sb("cross_w", XH * HD * 2 + 2 * DK * D)
        ctxT0 = m.sb("ctxT0", XH * CT)
        self_attention(nc, a, r, stats, ident, cross_w, ctxT0)
        soft_dram = nc.dram_tensor("soft_dram", [FK, B * S], F32, kind="Internal").ap()
        xT, xT32 = m.split("xT", DK * B * S), m.sb("xT32", DK * B * S)
        w32, Wroute = m.sb("w32", NROUTE), m.split("Wroute", NROUTE)
        cross_attention(nc, a, r, stats, ident, cross_w, ctxT0, xT, xT32, w32, Wroute)
        share_of = m.sb("share_of", B * F)
        softT = [m.sb(f"softT{n}", B * S, F32R, MR) for n in range(GROUPS)]
        stage, scale = m.sb("stage", WCOLS), m.sb("scale", SCOLS)
        W0 = m.split("W0", WCOLS)
        route_and_share(nc, a, r, ident, xT, xT32, w32, Wroute, softT, share_of, soft_dram, stage, scale, W0)
        experts(nc, a, r, stats, xT, xT32, softT, share_of, soft_dram, stage, scale, W0)


def decay_mask(np):
    gam = (1.0 - 2.0 ** (-5.0 - np.arange(XH, dtype=np.float32))).astype(np.float32)
    at = np.arange(S, dtype=np.float32)
    expo = at[None, :] - at[:, None]
    D_ = np.where(expo[None] <= 0, gam[:, None, None] ** expo[None], np.float32(0)).astype(np.float32)
    D_ = D_ / np.sqrt(D_.sum(-1))[:, None, :]
    return D_.transpose(2, 0, 1).reshape(S, XH * S).astype(np.float32)


def layout(np, v):
    T = B * S

    def rows(w, n=P):
        return w.reshape(-1, n, w.shape[1]).transpose(1, 0, 2).reshape(n, -1)

    def padded(w, shape):
        out = np.zeros(shape, w.dtype)
        out[tuple(slice(0, n) for n in w.shape)] = w
        return out

    ffn = lambda name: v["L0_ffn_" + name]
    Wh = v["L0_xattn_Wh"]
    out = {
        "x_tok": v["x"].transpose(1, 0, 2).reshape(S, B * D),
        "xT": v["x"].reshape(T, DK, P).transpose(2, 1, 0),
        "Wq": v["L0_attn_Wq"].reshape(DK, P, KV, G * DH).transpose(1, 2, 0, 3).reshape(P, -1),
        "Wk": rows(v["L0_attn_Wk"]), "Wv": rows(v["L0_attn_Wv"]), "Wo": rows(v["L0_attn_Wo"]),
        "bq": v["L0_attn_bq"].reshape(H, DH).T, "bk": v["L0_attn_bk"].reshape(KV, DH).T,
        "bv": v["L0_attn_bv"].reshape(KV, DH).T, "bo": v["L0_attn_bo"],
        "ident": np.eye(P, dtype=np.float32),
        "cross_w": np.concatenate([Wh.transpose(1, 0, 2).reshape(HD, -1), Wh.transpose(2, 0, 1).reshape(HD, -1),
                                   rows(v["L0_xattn_wg_w"]), rows(v["L0_xattn_wo_w"])], 1),
        "ctxT": v["ctx_2048"].reshape(T, XH, HD).transpose(2, 1, 0),
        "gamma": v["L0_xattn_gn_gamma"], "beta": v["L0_xattn_gn_beta"], "decay": decay_mask(np),
        "route_w": np.concatenate([rows(ffn("gate_weight").T), rows(padded(ffn("sh_gate_W").T, (D, SI * P))),
                                   rows(padded(ffn("sh_up_W").T, (D, SI * P))),
                                   rows(padded(ffn("sh_down_W").T, (SI * P, D)))], 1),
        "inv": ffn("inv_mapping").reshape(F // GROUPS, GROUPS, F).transpose(1, 0, 2).reshape(-1),
        "rows": np.arange(E, dtype=np.float32).reshape(E, 1),
    }

    def blocks(gate, up):
        w = np.zeros(gate.shape[:-1] + (GUB,), gate.dtype)
        w[..., :P], w[..., P:2 * P] = gate[..., :P], up[..., :P]
        w[..., 2 * P:2 * P + I2], w[..., 2 * P + KR:2 * P + B2] = up[..., P:], gate[..., P:]
        return w

    out["expert_scale"] = np.concatenate([blocks(ffn("gate_scale"), ffn("up_scale")), ffn("down_scale")], 1)
    W = np.zeros((F, P, WCOLS), np.float32)
    for f in range(F):
        w = W[f]
        w[:, GU_AT:QB_AT] = rows(blocks(ffn("gate_W")[f].T, ffn("up_W")[f].T))
        gate_qb, up_qb = (ffn(n)[f].transpose(0, 2, 1).reshape(KR, I) for n in ("gate_qb", "up_qb"))
        none = np.zeros_like(gate_qb)
        w[:KR, QB_AT:D1_AT], w[KR:, QB_AT:D1_AT] = blocks(gate_qb, none), blocks(none, up_qb)
        w[KR:, QB_AT:QB_AT + P], w[:KR, QB_AT + P:QB_AT + 2 * P] = gate_qb[:, :P], up_qb[:, :P]
        w[:, D1_AT:D2_AT] = ffn("down_W")[f].T[:P]
        w[:KR, D2_AT:QA_AT] = ffn("down_qb")[f].transpose(0, 2, 1).reshape(KR, D)
        w[KR:B2, D2_AT:QA_AT] = ffn("down_W")[f].T[P:]
        w[:, QA_AT:DQ_AT] = rows(np.concatenate([ffn("gate_qa")[f].reshape(KR, D).T, ffn("up_qa")[f].reshape(KR, D).T], 1))
        qa = ffn("down_qa")[f].reshape(KR, I).T
        w[:, DQ_AT:DQ_AT + KR] = qa[:P]
        w[KR:B2, DQ_AT + KR:MU_AT] = w[:I2, DQ_AT + KR:MU_AT] = qa[P:]
        for n in range(3):
            w[n * GR + f // GROUPS * F:n * GR + (f // GROUPS + 1) * F, MU_AT:] = ffn("mask_up_W")[f].T
    out["expert_w"] = W
    return out


def kernel(**inputs):
    import numpy as np
    import concourse.bacc as bacc
    from concourse.bass_utils import run_bass_kernel_spmd

    laid = layout(np, {name: np.asarray(x) for name, x in inputs.items()})
    nc = bacc.Bacc("TRN2", target_bir_lowering=False, num_devices=1)
    arrays, args = {}, {}
    for name, x in laid.items():
        x = np.ascontiguousarray(x)
        arrays[f"in_{name}"] = x
        args[name] = nc.dram_tensor(f"in_{name}", x.shape, mybir.dt.from_np(x.dtype), kind="ExternalInput").ap()
    args["out"] = nc.dram_tensor("out_0", (B, S, D), F32, kind="ExternalOutput").ap()
    program(nc, args)
    done = run_bass_kernel_spmd(nc, [arrays], core_ids=[0])
    return done.results[0]["out_0"]
```
